# Optimizing a Trainium2 kernel written in Bass

```python
import numpy as np
import jax
import jax.numpy as jnp

def _softmax(x, axis=-1):
    return jax.nn.softmax(x, axis=axis)

def _gelu(x):
    return jax.nn.gelu(x, approximate=True)

def _silu(x):
    return jax.nn.silu(x)

def _sigmoid(x):
    return jax.nn.sigmoid(x)

def _layernorm(x, axis=-1, eps=1e-05):
    m = jnp.mean(x, axis=axis, keepdims=True)
    v = jnp.var(x, axis=axis, keepdims=True)
    return (x - m) / jnp.sqrt(v + eps)

def _scatter_add(tgt, idx, src, axis=0):
    return tgt.at[idx].add(src)

def _segment_sum(src, seg, n):
    return jax.ops.segment_sum(src, seg, n)
kernel_name = 'mk_flamingo_gated_d1_seqx_r4_e72141'

def setup_inputs(seed: int=0):
    np.random.seed(seed)
    _w = jnp.asarray

    def _rec_inputs():
        import jax
        import jax.numpy as jnp
        _rk = jax.random.key(seed)
        x = -0.0002928 + 1 * jax.random.normal(jax.random.fold_in(_rk, 1), (8, 512, 256), jnp.float32)
        _lenS = 512 - jax.random.randint(jax.random.fold_in(_rk, 7), (8,), 0, max(1, 512 // 4) + 1, jnp.int32)
        _lenS2 = 1601 - jax.random.randint(jax.random.fold_in(_rk, 8), (8,), 0, max(1, 1601 // 4) + 1, jnp.int32)
        _ctx_512P = jax.random.normal(jax.random.fold_in(_rk, 11), (8, 16, 128), jnp.float32)
        _ctx_512c = jax.random.dirichlet(jax.random.fold_in(_rk, 511), 0.3 * jnp.ones((16,), jnp.float32), (8, 1601))
        _ctx_512t = jnp.einsum('bsk,bkd->bsd', _ctx_512c, _ctx_512P)
        _ctx_512t = _ctx_512t * jax.lax.rsqrt(jnp.mean(jnp.square(_ctx_512t)) + 1e-12) * 0.953939
        ctx_512 = 0.00222621 + 0.99962 * (_ctx_512t + 0.3 * jax.random.normal(jax.random.fold_in(_rk, 611), (8, 1601, 128), jnp.float32))
        _g = jax.random.normal(jax.random.fold_in(_rk, 9001), (2, 1), jnp.float32)
        _g = jnp.sign(_g) * jnp.maximum(jnp.abs(_g), 1.0) + (_g == 0) * 1.0
        g_xattn = _g[0]
        g_ffn = _g[1]
        return (x, ctx_512, g_xattn, g_ffn)
    x, ctx_512, g_xattn, g_ffn = _rec_inputs()

    def _L0_xattn_setup():
        import jax, jax.numpy as jnp
        import numpy as np
        B, T, TC, C, CC, H = (2, 512, 128, 256, 128, 16)
        D = C // H

        def _heads(t):
            b, l, _ = t.shape
            return t.reshape(b, l, H, D).transpose(0, 2, 1, 3)
        key = jax.random.key(seed)
        ks = jax.random.split(key, 18)
        w = lambda k, i, o: jax.random.normal(k, (i, o), jnp.float32) / np.sqrt(i).astype(np.float32)
        return {'x': jax.random.normal(ks[0], (B, T, C), jnp.float32), 'cross_input': jax.random.normal(ks[1], (B, TC, CC), jnp.float32), 'Wk': w(ks[2], C, C), 'bk': jnp.zeros((C,), jnp.float32), 'Wq': w(ks[3], C, C), 'bq': jnp.zeros((C,), jnp.float32), 'Wv': w(ks[4], C, C), 'bv': jnp.zeros((C,), jnp.float32), 'Wck': w(ks[5], CC, C), 'bck': jnp.zeros((C,), jnp.float32), 'Wcq': w(ks[6], C, C), 'bcq': jnp.zeros((C,), jnp.float32), 'Wcv': w(ks[7], CC, C), 'bcv': jnp.zeros((C,), jnp.float32), 'Wp': w(ks[8], C, C), 'bp': jnp.zeros((C,), jnp.float32)}
    _L0_xattn_all = _L0_xattn_setup()
    _L0_xattn_in = {k: v for k, v in _L0_xattn_all.items() if k in ('Wk', 'bk', 'Wq', 'bq', 'Wv', 'bv', 'Wck', 'bck', 'Wcq', 'bcq', 'Wcv', 'bcv', 'Wp', 'bp')}
    del _L0_xattn_all

    def _L0_ffn_setup():
        import jax, jax.numpy as jnp
        import numpy as np
        H, I, E, NS, C = (256, 256, 6, 2, 2)
        TOPK = 2
        TEMP = 1.0
        EPS = 1e-06
        key = jax.random.key(seed)
        ks = jax.random.split(key, 20)
        sd = 0.02
        inp = {'x': jax.random.normal(ks[0], (4, 512, H), jnp.float32), 'router_W': jax.random.normal(ks[1], (C, H, E), jnp.float32) * sd, 'router_b': jax.random.normal(ks[2], (C, E), jnp.float32) * sd, 'gate_bias': jax.random.normal(ks[3], (C, E), jnp.float32) * sd, 'exp_Wup': jax.random.normal(ks[4], (E, H, I), jnp.float32) * sd, 'exp_bup': jnp.zeros((E, I), jnp.float32), 'exp_Wg': jax.random.normal(ks[5], (E, I, I), jnp.float32) * sd, 'exp_bg': jnp.zeros((E, I), jnp.float32), 'exp_Wdown': jax.random.normal(ks[6], (E, I, H), jnp.float32) * sd, 'exp_bdown': jnp.zeros((E, H), jnp.float32), 'share_Wup': jax.random.normal(ks[7], (H, NS * I), jnp.float32) * sd, 'share_bup': jnp.zeros((NS * I,), jnp.float32), 'share_Wg': jax.random.normal(ks[8], (I, I), jnp.float32) * sd, 'share_bg': jnp.zeros((I,), jnp.float32), 'share_Wdown': jax.random.normal(ks[9], (I, H), jnp.float32) * sd, 'share_bdown': jnp.zeros((H,), jnp.float32), 'norm_w': jnp.ones((C, H), jnp.float32)}
        return inp
    _L0_ffn_all = _L0_ffn_setup()
    _L0_ffn_in = {k: v for k, v in _L0_ffn_all.items() if k in ('router_W', 'router_b', 'gate_bias', 'exp_Wup', 'exp_bup', 'exp_Wg', 'exp_bg', 'exp_Wdown', 'exp_bdown', 'share_Wup', 'share_bup', 'share_Wg', 'share_bg', 'share_Wdown', 'share_bdown', 'norm_w')}
    del _L0_ffn_all
    return {'x': x, 'ctx_512': ctx_512, 'g_xattn': g_xattn, 'g_ffn': g_ffn, 'L0_xattn_Wk': _L0_xattn_in['Wk'], 'L0_xattn_bk': _L0_xattn_in['bk'], 'L0_xattn_Wq': _L0_xattn_in['Wq'], 'L0_xattn_bq': _L0_xattn_in['bq'], 'L0_xattn_Wv': _L0_xattn_in['Wv'], 'L0_xattn_bv': _L0_xattn_in['bv'], 'L0_xattn_Wck': _L0_xattn_in['Wck'], 'L0_xattn_bck': _L0_xattn_in['bck'], 'L0_xattn_Wcq': _L0_xattn_in['Wcq'], 'L0_xattn_bcq': _L0_xattn_in['bcq'], 'L0_xattn_Wcv': _L0_xattn_in['Wcv'], 'L0_xattn_bcv': _L0_xattn_in['bcv'], 'L0_xattn_Wp': _L0_xattn_in['Wp'], 'L0_xattn_bp': _L0_xattn_in['bp'], 'L0_ffn_router_W': _L0_ffn_in['router_W'], 'L0_ffn_router_b': _L0_ffn_in['router_b'], 'L0_ffn_gate_bias': _L0_ffn_in['gate_bias'], 'L0_ffn_exp_Wup': _L0_ffn_in['exp_Wup'], 'L0_ffn_exp_bup': _L0_ffn_in['exp_bup'], 'L0_ffn_exp_Wg': _L0_ffn_in['exp_Wg'], 'L0_ffn_exp_bg': _L0_ffn_in['exp_bg'], 'L0_ffn_exp_Wdown': _L0_ffn_in['exp_Wdown'], 'L0_ffn_exp_bdown': _L0_ffn_in['exp_bdown'], 'L0_ffn_share_Wup': _L0_ffn_in['share_Wup'], 'L0_ffn_share_bup': _L0_ffn_in['share_bup'], 'L0_ffn_share_Wg': _L0_ffn_in['share_Wg'], 'L0_ffn_share_bg': _L0_ffn_in['share_bg'], 'L0_ffn_share_Wdown': _L0_ffn_in['share_Wdown'], 'L0_ffn_share_bdown': _L0_ffn_in['share_bdown'], 'L0_ffn_norm_w': _L0_ffn_in['norm_w']}

def reference(x, ctx_512, g_xattn, g_ffn, L0_xattn_Wk, L0_xattn_bk, L0_xattn_Wq, L0_xattn_bq, L0_xattn_Wv, L0_xattn_bv, L0_xattn_Wck, L0_xattn_bck, L0_xattn_Wcq, L0_xattn_bcq, L0_xattn_Wcv, L0_xattn_bcv, L0_xattn_Wp, L0_xattn_bp, L0_ffn_router_W, L0_ffn_router_b, L0_ffn_gate_bias, L0_ffn_exp_Wup, L0_ffn_exp_bup, L0_ffn_exp_Wg, L0_ffn_exp_bg, L0_ffn_exp_Wdown, L0_ffn_exp_bdown, L0_ffn_share_Wup, L0_ffn_share_bup, L0_ffn_share_Wg, L0_ffn_share_bg, L0_ffn_share_Wdown, L0_ffn_share_bdown, L0_ffn_norm_w):
    import jax
    import jax.numpy as jnp

    def _L0_xattn_ref(x, cross_input, Wk, bk, Wq, bq, Wv, bv, Wck, bck, Wcq, bcq, Wcv, bcv, Wp, bp):
        import jax, jax.numpy as jnp
        import numpy as np
        B, T, TC, C, CC, H = (2, 512, 128, 256, 128, 16)
        D = C // H

        def _heads(t):
            b, l, _ = t.shape
            return t.reshape(b, l, H, D).transpose(0, 2, 1, 3)
        scale = np.float32(1.0 / np.sqrt(D))
        q = _heads(x @ Wq + bq)
        k = _heads(x @ Wk + bk)
        v = _heads(x @ Wv + bv)
        att = jnp.einsum('bhqd,bhkd->bhqk', q, k) * scale
        causal = jnp.tril(jnp.ones((T, T), bool))
        att = jnp.where(causal[None, None], att, -jnp.inf)
        y = jnp.einsum('bhqk,bhkd->bhqd', jax.nn.softmax(att, axis=-1), v)
        qc = _heads(x @ Wcq + bcq)
        kc = _heads(cross_input @ Wck + bck)
        vc = _heads(cross_input @ Wcv + bcv)
        attc = jnp.einsum('bhqd,bhkd->bhqk', qc, kc) * scale
        y = y + jnp.einsum('bhqk,bhkd->bhqd', jax.nn.softmax(attc, axis=-1), vc)
        y = y.transpose(0, 2, 1, 3).reshape(x.shape[0], T, C)
        return y @ Wp + bp

    def _L0_ffn_ref(x, router_W, router_b, gate_bias, exp_Wup, exp_bup, exp_Wg, exp_bg, exp_Wdown, exp_bdown, share_Wup, share_bup, share_Wg, share_bg, share_Wdown, share_bdown, norm_w):
        import jax, jax.numpy as jnp
        import numpy as np
        H, I, E, NS, C = (256, 256, 6, 2, 2)
        TOPK = 2
        TEMP = 1.0
        EPS = 1e-06
        B, S, Hd = x.shape
        xf = x.reshape(-1, Hd)
        for j in range(C):
            residual = xf
            gate = (xf @ router_W[j] + router_b[j]) / TEMP
            biased = gate + gate_bias[j]
            _, ids = jax.lax.top_k(biased, TOPK)
            sel = (ids[:, :, None] == jnp.arange(E)[None, None, :]).any(axis=1)
            weights = jax.nn.softmax(jnp.where(sel, gate, -jnp.inf), axis=-1)
            h = jnp.einsum('nh,ehi->eni', xf, exp_Wup) + exp_bup[:, None, :]
            h = jax.nn.silu(jnp.einsum('eni,eij->enj', h, exp_Wg) + exp_bg[:, None, :]) * h
            eo = jnp.einsum('eni,eih->enh', h, exp_Wdown) + exp_bdown[:, None, :]
            combined = jnp.einsum('ne,enh->nh', weights, eo)
            s = (xf @ share_Wup + share_bup).reshape(-1, NS, I)
            s = jax.nn.silu(s @ share_Wg + share_bg) * s
            share_out = (s @ share_Wdown + share_bdown).sum(axis=1)
            z = combined + share_out
            y = residual + z
            y = y * jax.lax.rsqrt(jnp.mean(y * y, axis=-1, keepdims=True) + EPS) * norm_w[j]
            xf = y
        return xf.reshape(B, S, Hd)
    x = x + jnp.tanh(g_xattn[0]) * _L0_xattn_ref(_layernorm(x, axis=-1), ctx_512, L0_xattn_Wk, L0_xattn_bk, L0_xattn_Wq, L0_xattn_bq, L0_xattn_Wv, L0_xattn_bv, L0_xattn_Wck, L0_xattn_bck, L0_xattn_Wcq, L0_xattn_bcq, L0_xattn_Wcv, L0_xattn_bcv, L0_xattn_Wp, L0_xattn_bp)
    x = x + jnp.tanh(g_ffn[0]) * _L0_ffn_ref(_layernorm(x, axis=-1), L0_ffn_router_W, L0_ffn_router_b, L0_ffn_gate_bias, L0_ffn_exp_Wup, L0_ffn_exp_bup, L0_ffn_exp_Wg, L0_ffn_exp_bg, L0_ffn_exp_Wdown, L0_ffn_exp_bdown, L0_ffn_share_Wup, L0_ffn_share_bup, L0_ffn_share_Wg, L0_ffn_share_bg, L0_ffn_share_Wdown, L0_ffn_share_bdown, L0_ffn_norm_w)
    return x

_drawn_inputs = setup_inputs


def setup_inputs(seed=0):
    import zlib

    import numpy as np

    out = dict(_drawn_inputs(seed))
    spreads = {'L0_xattn_bk': (0.0, 0.8),
     'L0_xattn_bq': (0.0, 0.453),
     'L0_xattn_bv': (0.0, 0.1),
     'L0_xattn_bck': (0.0, 0.8),
     'L0_xattn_bcq': (0.0, 0.334),
     'L0_xattn_bcv': (0.0, 0.1),
     'L0_xattn_bp': (0.0, 0.1),
     'L0_ffn_exp_bup': (0.0, 0.8),
     'L0_ffn_exp_bg': (0.0, 0.602),
     'L0_ffn_exp_bdown': (0.0, 0.1),
     'L0_ffn_share_bup': (0.0, 0.506),
     'L0_ffn_share_bg': (0.0, 0.289),
     'L0_ffn_share_bdown': (0.0, 0.1),
     'L0_ffn_norm_w': (1.0, 0.2)}
    factors = {'L0_ffn_exp_Wup': 3.325, 'L0_ffn_exp_Wg': 4.328, 'L0_ffn_exp_Wdown': 3.128}
    for name, (base, spread) in spreads.items():
        noise = np.random.default_rng([zlib.crc32(name.encode()), seed]).standard_normal(out[name].shape)
        drawn = base * np.exp(spread * noise) if base else spread * noise
        out[name] = jnp.asarray(drawn.astype(out[name].dtype))
    for name, factor in factors.items():
        out[name] = (out[name] * factor).astype(out[name].dtype)
    return out
```

```python
from contextlib import ExitStack

import numpy as np

import concourse.bass as bass
import concourse.mybir as mybir
from concourse.alu_op_type import AluOpType as ALU

ACT = mybir.ActivationFunctionType
AX = mybir.AxisListType
F32, F32R, BF16 = mybir.dt.float32, mybir.dt.float32r, mybir.dt.bfloat16

P = 128
B, T, C = 8, 512, 256
H, D = 16, 16
TC, CC = 1601, 128
KC = C // P
QT = T // P
G = 4
NG = H // G
NI = B * NG
GC = G * D
NK = T + TC
CTXT = -(-TC // P)
NKT = QT + CTXT
LASTK = TC - (CTXT - 1) * P
TCE = TC + TC % 2
SCALE = 1.0 / float(np.sqrt(D))
NEG = -3.0e38
NE, NS, NL, IW = 6, 2, 2, 256
NX = NE + NS
LN_EPS, RMS_EPS = 1e-5, 1e-6

QPART = [0, 1, 2, 0, 1, 0]
KPART = [0, 0, 0, 1, 1, 2]
KROWS = D * len(QPART)
SROWS = KROWS + 3


def bcast(ap, n, axis):
    shape = list(ap.shape)
    shape[axis] = n
    return ap.to_broadcast(shape)


class Res:

    def __init__(self, nc, ctx, prefix):
        self.nc, self.ctx, self.prefix, self.spare, self.sems = nc, ctx, prefix, {}, []

    def sb(self, name, shape, dt=F32):
        return self.ctx.enter_context(self.nc.sbuf_tensor(self.prefix + name, shape, dt))

    def ps(self, name, shape, dt=F32):
        return self.ctx.enter_context(self.nc.psum_tensor(self.prefix + name, shape, dt))

    def sem(self, name):
        s = self.ctx.enter_context(self.nc.semaphore(self.prefix + name))
        self.sems.append(s)
        return s

    def prime(self, credit=()):
        extra = dict(credit)
        with self.nc.Block() as block:

            @block.gpsimd
            def _(pool):
                for s in self.sems:
                    pool.sem_inc(s, 1 + extra.get(s.name, 0))

    def carrier(self, eng):
        if id(eng) not in self.spare:
            self.spare[id(eng)] = self.sem(f"spare{len(self.spare)}")
        eng.sem_inc(self.spare[id(eng)], 1)


def wait(eng, sem, count):
    eng.wait_ge(sem, count + 1)


def mm3(pe, out, wH, wL, xH, xL, start, stop):
    pe.matmul(out, wL, xH, start=start, stop=False)
    pe.matmul(out, wH, xL, start=False, stop=False)
    return pe.matmul(out, wH, xH, start=False, stop=stop)


def stage_project(nc, a, QS, KS, VS, idf):
    with ExitStack() as ctx:
        r_ = Res(nc, ctx, "pj_")
        wraw = r_.sb("wraw", [P, 4, KC, C])
        craw = r_.sb("craw", [P, 2, C])
        wH, wL = r_.sb("wH", [P, 4, KC, C], F32R), r_.sb("wL", [P, 4, KC, C], F32R)
        cH, cL = r_.sb("cH", [P, 2, C], F32R), r_.sb("cL", [P, 2, C], F32R)
        bcol = r_.sb("bcol", [P, 4, KC])
        bvrow = r_.sb("bvrow", [P, 2, C])
        xin, xn = r_.sb("xin", [P, QT, C]), r_.sb("xn", [P, QT, C])
        st6, st2 = r_.sb("st6", [P, QT, 6]), r_.sb("st2", [P, QT, 2])
        var, rstd, expo = r_.sb("var", [P, QT]), r_.sb("rstd", [P, QT]), r_.sb("expo", [P, QT])
        xH, xL = r_.sb("xH", [P, KC, T], F32R), r_.sb("xL", [P, KC, T], F32R)
        ctxr = r_.sb("ctxr", [P, TCE])
        ctxH, ctxL = r_.sb("ctxH", [P, TCE], F32R), r_.sb("ctxL", [P, TCE], F32R)
        qpart = r_.sb("qpart", [P, 3, KC, 2 * T], BF16)
        kpart = r_.sb("kpart", [P, 3, KC, NK], BF16)
        vbuf = r_.sb("vbuf", [P, NG, NKT, GC])
        NR = 7
        rem = r_.sb("rem", [P, NR, T])
        NBANK = 6
        acc = [r_.ps(f"acc{i}", [P, T]) for i in range(NBANK)]
        tps = [r_.ps(f"tps{c}", [P, T]) for c in range(KC)]

        s_w, s_wH, s_wL = r_.sem("w"), r_.sem("wH"), r_.sem("wL")
        s_x, s_c = r_.sem("x"), r_.sem("c")
        s_cst, s_ln, s_var, s_rstd, s_xn = (r_.sem(n) for n in ("cst", "ln", "var", "rstd", "xn"))
        s_T, s_xH, s_xL = r_.sem("T"), r_.sem("xH"), r_.sem("xL")
        s_ctxH, s_ctxL = r_.sem("ctxH"), r_.sem("ctxL")
        s_out, s_h, s_fin, s_m, s_l = (r_.sem(n) for n in ("out", "h", "fin", "m", "l"))
        s_wr = {n: r_.sem("wr_" + n) for n in ("q0", "q1", "k0", "k1", "c0", "c1", "v")}

        CH = [402, 400, 400, 400]
        outs = [("q", 0, 0, "q0"), ("q", 1, 0, "q0"), ("q", 0, 1, "q1"), ("q", 1, 1, "q1"),
                ("k", 2, 0, "k0"), ("k", 2, 1, "k1"), ("vs", 0), ("vs", 2)]
        NSELF = len(outs)
        for cg in range(KC):
            at = 0
            for n in CH:
                outs.append(("c", at, cg, f"c{cg}", n))
                at += n
        outs += [("vc", t) for t in range(0, CTXT, 2)]
        NO = len(outs)
        split = [k for k, o in enumerate(outs) if o[0] in "qkc"]
        rank = {k: j for j, k in enumerate(split)}
        NSP = len(split)
        assert NSP == 2 * NR

        def parts(o):
            if o[0] == "q":
                return qpart, o[2], o[1] * T, T, bcol[:, o[1], o[2]:o[2] + 1]
            if o[0] == "k":
                return kpart, o[2], 0, T, bcol[:, 2, o[2]:o[2] + 1]
            n = min(o[4], TC - o[1])
            return kpart, o[2], T + o[1], n, bcol[:, 3, o[2]:o[2] + 1]

        def writes(tag):
            return [k for k in split if outs[k][3] == tag]

        r_.prime({s_fin.name: NO})
        with nc.Block() as block:

            @block.sync
            def _(sp):
                sp.dma_start(xin[:, :, :], a["x"][0].rearrange("(t p) c -> p t c", p=P)).then_inc(s_x, 16)
                for n, w in enumerate(("Wq", "Wcq", "Wk", "Wv")):
                    sp.dma_start(wraw[:, n], a[w].rearrange("(k p) n -> p k n", p=P)).then_inc(s_w, 16)
                for n, w in enumerate(("Wck", "Wcv")):
                    sp.dma_start(craw[:, n], a[w]).then_inc(s_w, 16)
                sp.dma_start(bcol[:, :, :], a["bcol"]).then_inc(s_w, 16)
                for n, w in enumerate(("bv", "bcv")):
                    sp.dma_start(bvrow[:, n], a[w].rearrange("(o c) -> o c", o=1).to_broadcast([P, C])).then_inc(s_w, 16)
                sp.dma_start(ctxr[:, 0:TC], a["ctxT"][0]).then_inc(s_c, 16)

                def write(b, tag):
                    ks = writes(tag)
                    tile, cg, c0, _, _ = parts(outs[ks[0]])
                    n = sum(parts(outs[k])[3] for k in ks)
                    wait(sp, s_l, b * NSP + rank[ks[-1]] + 1)
                    for part in range(3):
                        dst = QS if tile is qpart else KS
                        row = dst[part].rearrange("(b r) c -> b r c", b=B)[bass.ds(b, 1), cg * P:(cg + 1) * P, c0:c0 + n]
                        sp.dma_start(row.rearrange("o r c -> (o r) c"), tile[:, part, cg, c0:c0 + n]).then_inc(s_wr[tag], 16)

                def body(b, more):
                    if more:
                        wait(sp, s_xn, QT * (b + 1))
                        sp.dma_start(xin[:, :, :], a["x"][bass.ds(b + 1, 1)].rearrange("o (t p) c -> p (o t) c", p=P)).then_inc(s_x, 16)
                        wait(sp, s_ctxL, b + 1)
                        wait(sp, s_ctxH, b + 1)
                        sp.dma_start(ctxr[:, 0:TC], a["ctxT"][bass.ds(b + 1, 1)].rearrange("o c t -> (o c) t")).then_inc(s_c, 16)
                    for tag in ("q0", "q1", "k0", "k1", "c0", "c1"):
                        write(b, tag)
                    wait(sp, s_fin, NO * (b + 2))
                    for g in range(NG):
                        dst = VS.rearrange("(b g) p t c -> b g p t c", b=B)[bass.ds(b, 1), g]
                        sp.dma_start(dst.rearrange("o p t c -> (o p) t c"), vbuf[:, g]).then_inc(s_wr["v"], 16)

                with sp.Fori(0, B - 1) as b:
                    body(b, True)
                body(B - 1, False)
                for tag, s in s_wr.items():
                    wait(sp, s, (64 if tag == "v" else 48) * B)

            @block.gpsimd
            def _(pool):
                pool.memset(expo[:, :], -0.5).then_inc(s_cst, 1)
                pool.memset(ctxr[:, TC:TCE], 0.0).then_inc(s_cst, 1)
                pool.memset(vbuf[:, :, NKT - 1, :], 0.0).then_inc(s_cst, 1)

                def power(n):
                    wait(pool, s_cst, 3)
                    wait(pool, s_var, n + 1)
                    pool.tensor_tensor(rstd[:, :], var[:, :], expo[:, :], ALU.pow).then_inc(s_rstd, 1)

                def body(b, more):
                    for j, k in enumerate(split):
                        if k == 3 and more:
                            power(b + 1)
                        tile, cg, c0, n, _ = parts(outs[k])
                        wait(pool, s_m, b * NSP + j + 1)
                        pool.tensor_tensor(tile[:, 2, cg, c0:c0 + n], rem[:, j % NR, 0:n], tile[:, 1, cg, c0:c0 + n],
                                           ALU.subtract).then_inc(s_l, 1)

                power(0)
                with pool.Fori(0, B - 1) as b:
                    body(b, True)
                body(B - 1, False)

            @block.vector
            def _(dve):
                wait(dve, s_cst, 3)
                wait(dve, s_wH, 6)
                for n in range(4):
                    dve.tensor_tensor(wL[:, n], wraw[:, n], wH[:, n].bitcast(F32), ALU.subtract).then_inc(s_wL, 1)
                for n in range(2):
                    dve.tensor_tensor(cL[:, n], craw[:, n], cH[:, n].bitcast(F32), ALU.subtract).then_inc(s_wL, 1)

                def layernorm(n):
                    wait(dve, s_x, 16 * (n + 1))
                    wait(dve, s_T, KC * n)
                    for t in range(QT):
                        dve.bn_stats(st6[:, t, :], xin[:, t, :]).then_inc(s_ln, 1)
                    wait(dve, s_ln, 2 * QT * n + QT)
                    r_.carrier(dve)
                    for t in range(QT):
                        dve.bn_aggr(st2[:, t, :], st6[:, t, :]).then_inc(s_ln, 1)
                    wait(dve, s_ln, 2 * QT * (n + 1))
                    dve.tensor_scalar(var[:, :], st2[:, :, 1], LN_EPS, None, ALU.add).then_inc(s_var, 1)
                    wait(dve, s_rstd, n + 1)
                    for t in range(QT):
                        dve.tensor_scalar(xn[:, t, :], xin[:, t, :], st2[:, t, 0:1], rstd[:, t:t + 1],
                                          ALU.subtract, ALU.mult).then_inc(s_xn, 1)

                def x_low(n):
                    for c in range(KC):
                        wait(dve, s_xH, KC * n + c + 1)
                        dve.tensor_tensor(xL[:, c, :], tps[c][:, :], xH[:, c, :].bitcast(F32), ALU.subtract).then_inc(s_xL, 1)

                def ctx_low(n):
                    wait(dve, s_ctxH, n + 1)
                    dve.tensor_tensor(ctxL[:, :], ctxr[:, :], ctxH[:, :].bitcast(F32), ALU.subtract).then_inc(s_ctxL, 1)

                def body(b, more):
                    for k, o in enumerate(outs):
                        bank = acc[k % NBANK]
                        if k == 3 and more:
                            layernorm(b + 1)
                        if k == NSELF + 1 and more:
                            x_low(b + 1)
                        if k in rank:
                            j = rank[k]
                            tile, cg, c0, n, bias = parts(o)
                            wait(dve, s_h, b * NSP + j + 1)
                            if j >= NR:
                                wait(dve, s_l, b * NSP + j - NR + 1)
                            else:
                                wait(dve, s_l, b * NSP)
                            dve.scalar_tensor_tensor(rem[:, j % NR, 0:n], bank[:, 0:n], bias, tile[:, 0, cg, c0:c0 + n],
                                                     ALU.add, ALU.subtract).then_inc(s_fin, 1)
                            continue
                        wait(dve, s_out, b * NO + k + 1)
                        if o == ("vs", 0):
                            wait(dve, s_wr["v"], 64 * b)
                        kind, t = o
                        row = 0 if kind == "vs" else 1
                        for i in range(2):
                            tt = t + i
                            if kind == "vc" and tt >= CTXT:
                                continue
                            rows = LASTK if kind == "vc" and tt == CTXT - 1 else P
                            slot = tt if kind == "vs" else QT + tt
                            ins = dve.tensor_tensor(vbuf[0:rows, :, slot, :],
                                                    bank[0:rows, i * C:(i + 1) * C].rearrange("p (g c) -> p g c", g=NG),
                                                    bvrow[0:rows, row, :].rearrange("p (g c) -> p g c", g=NG), ALU.add)
                        ins.then_inc(s_fin, 1)
                    if more:
                        ctx_low(b + 1)

                layernorm(0)
                x_low(0)
                ctx_low(0)
                with dve.Fori(0, B - 1) as b:
                    body(b, True)
                body(B - 1, False)

            @block.scalar
            def _(act):
                wait(act, s_w, 16 * 9)
                for n in range(4):
                    act.activation(wH[:, n], wraw[:, n], ACT.Copy).then_inc(s_wH, 1)
                for n in range(2):
                    act.activation(cH[:, n], craw[:, n], ACT.Copy).then_inc(s_wH, 1)

                def x_high(n):
                    wait(act, s_out, NO * n if isinstance(n, int) and n == 0 else NO * (n - 1) + NSELF)
                    for c in range(KC):
                        wait(act, s_T, KC * n + c + 1)
                        act.activation(xH[:, c, :], tps[c][:, :], ACT.Copy).then_inc(s_xH, 1)

                def ctx_high(n):
                    wait(act, s_c, 16 * (n + 1))
                    wait(act, s_cst, 3)
                    wait(act, s_out, NO * n)
                    act.activation(ctxH[:, :], ctxr[:, :], ACT.Copy).then_inc(s_ctxH, 1)

                def mid(b, k):
                    j = rank[k]
                    tile, cg, c0, n, _ = parts(outs[k])
                    wait(act, s_fin, NO * (b + 1) + k + 1)
                    act.activation(tile[:, 1, cg, c0:c0 + n], rem[:, j % NR, 0:n], ACT.Copy).then_inc(s_m, 1)

                def body(b, more):
                    seen, behind = set(), None
                    for k, o in enumerate(outs):
                        if k == NSELF:
                            mid(b, behind)
                            behind = None
                            if more:
                                x_high(b + 1)
                        if k not in rank:
                            continue
                        tile, cg, c0, n, bias = parts(o)
                        if o[3] not in seen:
                            wait(act, s_wr[o[3]], 48 * b)
                            seen.add(o[3])
                        wait(act, s_out, b * NO + k + 1)
                        act.activation(tile[:, 0, cg, c0:c0 + n], acc[k % NBANK][:, 0:n], ACT.Identity,
                                       bias=bias, scale=1.0).then_inc(s_h, 1)
                        if behind is not None:
                            mid(b, behind)
                        behind = k
                    mid(b, behind)
                    if more:
                        ctx_high(b + 1)

                x_high(0)
                ctx_high(0)
                with act.Fori(0, B - 1) as b:
                    body(b, True)
                body(B - 1, False)

            @block.tensor
            def _(pe):
                def transpose_x(n):
                    wait(pe, s_xn, QT * (n + 1))
                    wait(pe, s_xL, KC * n)
                    for c in range(KC):
                        for t in range(QT):
                            ins = pe.transpose(tps[c][:, t * P:(t + 1) * P], xn[:, t, c * P:(c + 1) * P], idf[:, :])
                        ins.then_inc(s_T, 1)

                def body(b, more):
                    for k, o in enumerate(outs):
                        if k == NSELF and more:
                            transpose_x(b + 1)
                        bank = acc[k % NBANK]
                        if k == 0:
                            wait(pe, s_xL, KC * (b + 1))
                        if k == NSELF:
                            wait(pe, s_ctxL, b + 1)
                        prev = k - NBANK if k >= NBANK else max(i for i in range(NO) if i % NBANK == k) - NO
                        wait(pe, s_fin, NO * (b + 1) + prev + 1)
                        if o[0] in "qk":
                            w, cg = o[1], o[2]
                            for c in range(KC):
                                cols = slice(cg * P, (cg + 1) * P)
                                ins = mm3(pe, bank[:, :], wH[:, w, c, cols], wL[:, w, c, cols], xH[:, c, :], xL[:, c, :],
                                          c == 0, c == KC - 1)
                        elif o[0] == "vs":
                            for i in range(2):
                                tok = slice((o[1] + i) * P, (o[1] + i + 1) * P)
                                for c in range(KC):
                                    ins = mm3(pe, bank[:, i * C:(i + 1) * C], xH[:, c, tok], xL[:, c, tok],
                                              wH[:, 3, c, :], wL[:, 3, c, :], c == 0, c == KC - 1)
                        elif o[0] == "c":
                            cols = slice(o[2] * P, (o[2] + 1) * P)
                            at, n = o[1], o[4]
                            ins = mm3(pe, bank[:, 0:n], cH[:, 0, cols], cL[:, 0, cols], ctxH[:, at:at + n],
                                      ctxL[:, at:at + n], True, True)
                        else:
                            for i in range(2):
                                tt = o[1] + i
                                if tt >= CTXT:
                                    continue
                                rows = LASTK if tt == CTXT - 1 else P
                                tok = slice(tt * P, tt * P + rows)
                                ins = mm3(pe, bank[0:rows, i * C:(i + 1) * C], ctxH[:, tok], ctxL[:, tok],
                                          cH[:, 1, :], cL[:, 1, :], True, True)
                        ins.then_inc(s_out, 1)

                wait(pe, s_wL, 6)
                transpose_x(0)
                with pe.Fori(0, B - 1) as b:
                    body(b, True)
                body(B - 1, False)


def stage_attend(nc, QS, KS, VS, YS, idf, idb, mq, mk):
    with ExitStack() as ctx:
        r_ = Res(nc, ctx, "at_")
        K = [r_.sb(f"K{u}", [SROWS, G, NK], BF16) for u in range(2)]
        Q = [r_.sb(f"Q{u}", [SROWS, 2, G, T], BF16) for u in range(2)]
        vraw = [r_.sb(f"vraw{u}", [P, NKT, GC]) for u in range(2)]
        V = [r_.sb(f"V{u}", [P, NKT, G, 2 * D]) for u in range(2)]
        Pt = [r_.sb(f"P{u}", [P, G, T]) for u in range(2)]
        part = r_.sb("part", [P, 2, G, QT, 2])
        mx = r_.sb("mx", [P, 2, G * QT])
        sh = [r_.sb(f"sh{k}", [G * QT, 3, P], BF16) for k in range(2)]
        rest = r_.sb("rest", [G * QT, 1, P])
        O = [r_.sb(f"O{k}", [P, T]) for k in range(2)]
        den = r_.sb("den", [P, 2, QT, G])
        yk = [r_.sb(f"y{k}", [P, QT, G, D]) for k in range(2)]
        ysum = [r_.sb(f"ysum{u}", [P, QT, GC]) for u in range(2)]
        ST = [r_.ps(f"ST{i}", [P, T]) for i in range(2)]
        M = [r_.ps(f"M{i}", [P, 2, T]) for i in range(2)]
        OP = r_.ps("OP", [P, T])
        TP = r_.ps("TP", [P, T])

        s_ld = [r_.sem(f"ld{u}") for u in range(2)]
        s_vld = [r_.sem(f"vld{u}") for u in range(2)]
        (s_cst, s_v, s_st, s_ex, s_av, s_mt, s_mr, s_oe, s_ya, s_pm, s_sr) = (
            r_.sem(n) for n in ("cst", "v", "st", "ex", "av", "mt", "mr", "oe", "ya", "pm", "sr"))
        s_y0 = r_.sem("y0")
        s_yst = [r_.sem(f"yst{u}") for u in range(2)]
        s_shT, s_shD, s_oT, s_oD, s_rc, s_shd = ([r_.sem(f"{n}{k}") for k in range(2)]
                                          for n in ("shT", "shD", "oT", "oD", "rc", "shd"))

        SELF, CROSS = 0, 1
        XC = -(-TC // 4)
        XOFF = [[0, TC // 4], [2 * (TC // 4), TC - XC]]
        assert all(o1 - o0 <= XC for o0, o1 in XOFF) and XOFF[1][0] <= XOFF[0][1] + XC and XC <= T
        mtiles = [("s", h, q) for h in range(G) for q in (0, 2)]
        NMS = len(mtiles)
        mtiles += [("x", h, q, half) for h in range(G) for q in range(QT) for half in range(2)]
        NM = len(mtiles)
        TAIL = 4
        S0 = 3
        NEXT = NM - TAIL
        NST = NKT * G

        def schedule():
            ev = []
            slots = NKT + 1 - S0
            done = 0
            for s in range(NKT + 1):
                last = s == NKT
                if not last:
                    ev += [("ST", s, 0), ("ST", s, 1)]
                n_next = (s - S0 + 1) * NEXT // slots - done if s >= S0 else 0
                tail = [2, 2][s] if s < 2 else 0
                ms = [("MT", NEXT + 2 * s + i) for i in range(tail)] + [("MN", done + i) for i in range(n_next)]
                done += n_next
                if last:
                    ev += ms[:1]
                if s > 0:
                    ev.append(("AV", s - 1))
                if not last:
                    ev += [("ST", s, 2), ("ST", s, 3)]
                if s == QT + 1:
                    ev.append(("O", SELF))
                ev += ms[1:] if last else ms
                if last:
                    ev.append(("O", CROSS))
                if s == 1:
                    ev.append(("SH", CROSS, 0))
                if s == 9:
                    ev.append(("SH", SELF, 1))
            assert done == NEXT
            return ev

        body_events = schedule()
        assert body_events.index(("MN", NMS - 1)) < body_events.index(("SH", SELF, 1))

        def loop(eng, body):
            with eng.Fori(0, NI // 2 - 1) as it:
                for u in range(2):
                    body(2 * it + u, it, u, True)
            body(NI - 2, NI // 2 - 1, 0, True)
            body(NI - 1, NI // 2 - 1, 1, False)

        def events(more):
            return [e for e in body_events if more or not (e[0] == "MN" or e[0] == "SH" and e[2])]

        def st_cols(s):
            return s * P if s < QT else 0

        r_.prime()
        with nc.Block() as block:

            @block.sync
            def _(sp):
                def load(i, it, u):
                    for r in range(len(QPART)):
                        rows = slice(r * D, (r + 1) * D)
                        k = KS[KPART[r]].rearrange("(i h d) c -> i h d c", i=NI, h=G)[bass.ds(i, 1)]
                        sp.dma_start(K[u][rows], k.rearrange("o h d c -> (o d) h c")).then_inc(s_ld[u], 16)
                        q = QS[QPART[r]].rearrange("(i h d) (k c) -> i h d k c", i=NI, h=G, k=2)[bass.ds(i, 1)]
                        for k2 in range(2):
                            sp.dma_start(Q[u][rows, k2], q[:, :, :, k2].rearrange("o h d c -> (o d) h c")).then_inc(s_ld[u], 16)
                    sp.dma_start(vraw[u][:, :, :], VS[bass.ds(i, 1)].rearrange("o p t c -> (o p) t c")).then_inc(s_vld[u], 16)

                def shift_rows(kind, n, u):
                    wait(sp, s_shD[kind], n + 1)
                    for p in range(3):
                        sp.dma_start(Q[u][KROWS + p:KROWS + p + 1, kind], sh[kind][:, p]).then_inc(s_shd[kind], 16)

                def body(i, it, u, more):
                    if more:
                        wait(sp, s_st, NST * i)
                        r_.carrier(sp)
                        wait(sp, s_v, i)
                        if u == 0:
                            load(i + 1, it, 1)
                        else:
                            load(i + 1, it + 1, 0)
                    store(i, 1 - u)
                    shift_rows(CROSS, i, u)
                    if more:
                        shift_rows(SELF, i + 1, 1 - u)

                def store(slot, u):
                    wait(sp, s_ya, slot)
                    sp.dma_start(YS[bass.ds(slot, 1)].rearrange("o p t c -> (o p) t c"), ysum[u][:, :, :]).then_inc(s_yst[u], 16)

                load(0, 0, 0)
                shift_rows(SELF, 0, 0)
                wait(sp, s_y0, 1)
                loop(sp, body)
                store(NI, 1)
                wait(sp, s_yst[0], 16 * (NI // 2))
                wait(sp, s_yst[1], 16 * (NI // 2 + 1))

            @block.gpsimd
            def _(pool):
                for u in range(2):
                    pool.memset(V[u][:, :, :, D:2 * D], 1.0).then_inc(s_cst, 1)
                pool.memset(ysum[1][:, :, :], 0.0).then_inc(s_y0, 1)

                def copy_v(n, it, u):
                    wait(pool, s_vld[u], 16 * (it + 1))
                    wait(pool, s_av, NKT * (n - 1) if not isinstance(n, int) or n > 1 else 0)
                    r_.carrier(pool)
                    pool.tensor_copy(V[u][:, :, :, 0:D], vraw[u][:, :, :].rearrange("p t (h d) -> p t h d", h=G)).then_inc(s_v, 1)

                def body(i, it, u, more):
                    for k in range(2):
                        wait(pool, s_oD[k], i + 1)
                    wait(pool, s_yst[u], 16 * (it + u))
                    pool.tensor_tensor(ysum[u][:, :, :].rearrange("p t c -> p (t c)"),
                                       yk[0][:, :, :, :].rearrange("p t h d -> p (t h d)"),
                                       yk[1][:, :, :, :].rearrange("p t h d -> p (t h d)"), ALU.add).then_inc(s_ya, 1)

                def pool_body(i, it, u, more):
                    if more:
                        if u == 0:
                            copy_v(i + 1, it, 1)
                        else:
                            copy_v(i + 1, it + 1, 0)
                    body(i, it, u, more)

                copy_v(0, 0, 0)
                loop(pool, pool_body)

            @block.vector
            def _(dve):
                for u in range(2):
                    dve.memset(K[u][KROWS:SROWS, :, :], 1.0).then_inc(s_cst, 1)

                def reduce_tile(n, m):
                    tile = mtiles[m]
                    buf = M[m % 2]
                    wait(dve, s_mt, NM * n + m + 1)
                    if tile[0] == "s":
                        _, h, q = tile
                        for j in range(2):
                            col = h * QT + q + j
                            ins = dve.tensor_reduce(mx[:, SELF, col:col + 1], buf[:, j, 0:(q + j + 1) * P], AX.X, ALU.max)
                    else:
                        _, h, q, half = tile
                        ins = dve.tensor_reduce(part[:, half, h, q, 0:1], buf[:, :, 0:XC], AX.XY, ALU.max)
                    ins.then_inc(s_mr, 1)

                def combine(n):
                    wait(dve, s_mr, NM * (n + 1))
                    wait(dve, s_shT[CROSS], n)
                    dve.tensor_tensor(mx[:, CROSS, :], part[:, 0, :, :, 0].rearrange("p h q -> p (h q)"),
                                      part[:, 1, :, :, 0].rearrange("p h q -> p (h q)"), ALU.max).then_inc(s_pm, 1)

                def shift_parts(kind, n):
                    t, rem, out = TP[0:G * QT, 0:P], rest[:, 0], sh[kind]
                    own = 6 * n + (3 if kind == CROSS else 0)
                    wait(dve, s_shT[kind], n + 1)
                    wait(dve, s_shd[kind], 48 * n)
                    dve.tensor_scalar(out[:, 0], t, -1.0, None, ALU.mult).then_inc(s_sr, 1)
                    wait(dve, s_sr, own + 1)
                    dve.scalar_tensor_tensor(rem, t, -1.0, out[:, 0], ALU.mult, ALU.subtract).then_inc(s_sr, 1)
                    wait(dve, s_sr, own + 2)
                    dve.tensor_copy(out[:, 1], rem).then_inc(s_sr, 1)
                    wait(dve, s_sr, own + 3)
                    dve.tensor_tensor(out[:, 2], rem, out[:, 1], ALU.subtract).then_inc(s_shD[kind], 1)

                def output(kind, n):
                    t = TP[:, :].rearrange("p (q h e) -> p q h e", q=QT, h=G)
                    wait(dve, s_oT[kind], n + 1)
                    dve.reciprocal(den[:, kind], t[:, :, :, D]).then_inc(s_rc[kind], 1)
                    wait(dve, s_rc[kind], n + 1)
                    wait(dve, s_ya, n)
                    dk = bcast(den[:, kind].rearrange("p q (h o) -> p (q h) o", o=1), D, 2)
                    dve.tensor_tensor(yk[kind][:, :, :, :].rearrange("p q h d -> p (q h) d"),
                                      t[:, :, :, 0:D].rearrange("p q h d -> p (q h) d"), dk, ALU.mult
                                      ).then_inc(s_oD[kind], 1)

                def body(i, it, u, more):
                    for e in events(more):
                        if e[0] == "MT":
                            reduce_tile(i, e[1])
                            if e[1] == NM - 1:
                                combine(i)
                        elif e[0] == "MN":
                            reduce_tile(i + 1, e[1])
                        elif e[0] == "SH":
                            shift_parts(e[1], i + e[2])
                        elif e[0] == "O":
                            output(e[1], i)

                for m in range(NMS):
                    reduce_tile(0, m)
                shift_parts(SELF, 0)
                for m in range(NMS, NEXT):
                    reduce_tile(0, m)
                loop(dve, body)

            @block.scalar
            def _(act):
                def body(i, it, u, more):
                    for _, s, h in (e for e in events(more) if e[0] == "ST"):
                        rows = LASTK if s == NKT - 1 else P
                        c0 = st_cols(s)
                        if (s, h) == (QT, 2):
                            evac(i, SELF)
                        wait(act, s_st, NST * i + s * G + h + 1)
                        if h == 0:
                            wait(act, s_av, NKT * i + max(s - 1, 0))
                        act.activation(Pt[s % 2][0:rows, h, c0:T], ST[h % 2][0:rows, c0:T], ACT.Exp,
                                       scale=SCALE).then_inc(s_ex, 1)
                    evac(i, CROSS)

                def evac(i, kind):
                    wait(act, s_av, NKT * i + (QT if kind == SELF else NKT))
                    wait(act, s_oT[kind], i)
                    act.activation(O[kind][:, :], OP[:, :], ACT.Copy).then_inc(s_oe, 1)

                loop(act, body)

            @block.tensor
            def _(pe):
                def max_tile(n, it, u, m):
                    tile = mtiles[m]
                    buf = M[m % 2]
                    wait(pe, s_mr, NM * n + m - 1 if not (isinstance(n, int) and n == 0 and m < 2) else 0)
                    if tile[0] == "s":
                        _, h, q = tile
                        for j in range(2):
                            w = (q + j + 1) * P
                            pe.matmul(buf[:, j, 0:w], Q[u][0:KROWS, SELF, h, (q + j) * P:w], K[u][0:KROWS, h, 0:w],
                                      start=True, stop=True)
                            ins = pe.matmul(buf[:, j, w - P:w], idb[:, :], mq[:, :], start=False, stop=True,
                                            skip_group_check=True)
                    else:
                        _, h, q, half = tile
                        for j in range(2):
                            at = T + XOFF[half][j]
                            ins = pe.matmul(buf[:, j, 0:XC], Q[u][0:KROWS, CROSS, h, q * P:(q + 1) * P],
                                            K[u][0:KROWS, h, at:at + XC], start=True, stop=True)
                    ins.then_inc(s_mt, 1)

                def shift(kind, n, first=False):
                    if kind == SELF:
                        wait(pe, s_mr, NM * n + NMS)
                        if not first:
                            wait(pe, s_oD[SELF], n)
                    else:
                        wait(pe, s_pm, n + 1)
                        wait(pe, s_oD[CROSS], n)
                        wait(pe, s_shD[SELF], n + 1)
                    pe.transpose(TP[0:G * QT, 0:P], mx[:, kind, :], idf[:, :]).then_inc(s_shT[kind], 1)

                def output(kind, n, more):
                    wait(pe, s_oe, 2 * n + 1 + kind)
                    if kind == SELF:
                        wait(pe, s_shD[CROSS], n + 1)
                    elif more:
                        wait(pe, s_shD[SELF], n + 2)
                    else:
                        wait(pe, s_oD[SELF], n + 1)
                    for q in range(QT):
                        ins = pe.transpose(TP[:, q * P:(q + 1) * P], O[kind][:, q * P:(q + 1) * P], idf[:, :])
                    ins.then_inc(s_oT[kind], 1)

                def scores(i, u, s, h):
                    kind = SELF if s < QT else CROSS
                    if h == 0 and s == 0:
                        wait(pe, s_shd[SELF], 48 * (i + 1))
                    if h == 0 and s == QT:
                        wait(pe, s_shd[CROSS], 48 * (i + 1))
                    n = NST * i + s * G + h
                    if isinstance(i, int) or s * G + h >= 2:
                        wait(pe, s_ex, n - 1)
                    else:
                        wait(pe, s_ex, NST * i + max(0, s * G + h - 1))
                    rows = LASTK if s == NKT - 1 else P
                    c0 = st_cols(s)
                    keys = slice(s * P, s * P + rows)
                    out = ST[h % 2]
                    ins = pe.matmul(out[0:rows, c0:T], K[u][:, h, keys], Q[u][:, kind, h, c0:T], start=True,
                                    stop=True)
                    if kind == SELF:
                        ins = pe.matmul(out[:, c0:c0 + P], idb[:, :], mk[:, :], start=False, stop=True,
                                        skip_group_check=True)
                    ins.then_inc(s_st, 1)

                def values(i, u, s):
                    wait(pe, s_ex, NST * i + (s + 1) * G)
                    if s == 0:
                        wait(pe, s_v, i + 1)
                        wait(pe, s_oe, 2 * i)
                    if s == QT:
                        wait(pe, s_oe, 2 * i + 1)
                    rows = LASTK if s == NKT - 1 else P
                    c0 = st_cols(s)
                    for h in range(G):
                        ins = pe.matmul(OP[32 * h:32 * h + 2 * D, c0:T], V[u][0:rows, s, h, :], Pt[s % 2][0:rows, h, c0:T],
                                        start=s in (0, QT), stop=s < QT or s == NKT - 1, skip_group_check=True)
                    ins.then_inc(s_av, 1)

                def body(i, it, u, more):
                    for e in events(more):
                        if e[0] == "ST":
                            scores(i, u, e[1], e[2])
                        elif e[0] == "AV":
                            values(i, u, e[1])
                        elif e[0] == "MT":
                            max_tile(i, it, u, e[1])
                        elif e[0] == "MN":
                            if e[1] == 0:
                                nit = it if u == 0 else it + 1
                                wait(pe, s_ld[1 - u], 16 * 3 * len(QPART) * (nit + 1))
                            max_tile(i + 1, it, 1 - u, e[1])
                        elif e[0] == "SH":
                            shift(e[1], i + e[2])
                        elif e[0] == "O":
                            output(e[1], i, more)

                wait(pe, s_cst, 4)
                wait(pe, s_ld[0], 16 * 3 * len(QPART))
                for m in range(NMS):
                    max_tile(0, 0, 0, m)
                shift(SELF, 0, first=True)
                for m in range(NMS, NEXT):
                    max_tile(0, 0, 0, m)
                loop(pe, body)


def stage_fold(nc, a, w):
    with ExitStack() as ctx:
        r_ = Res(nc, ctx, "fo_")
        NU = 2
        upT, up, wg, wd = ([r_.sb(f"{n}{u}", [P, KC, IW]) for u in range(NU)] for n in ("upT", "up", "wg", "wd"))
        bg = r_.sb("bg", [P, NX, KC])
        comb = [r_.ps(f"comb{u}", [P, KC, IW]) for u in range(NU)]
        bias = [r_.ps(f"bias{u}", [P, T]) for u in range(NU)]
        s_b, s_H, s_L, s_c, s_cH, s_cL, s_bi, s_bo = (r_.sem(n) for n in ("b", "H", "L", "c", "cH", "cL", "bi", "bo"))
        s_ld = [r_.sem(f"ld{u}") for u in range(NU)]
        NIT = NX // NU

        r_.prime()
        with nc.Block() as block:

            @block.sync
            def _(sp):
                sp.dma_start(bg[:, :, :], a["bg"]).then_inc(s_b, 16)
                sp.dma_start(w["bu"][:, :, :], a["bup"]).then_inc(s_b, 16)
                sp.dma_start(w["bd"][:, :], a["bd"]).then_inc(s_b, 16)
                wait(sp, s_b, 48)
                with sp.Fori(0, NIT) as it:
                    for u in range(NU):
                        e = NU * it + u
                        wait(sp, s_L, 2 * NU * it)
                        r_.carrier(sp)
                        wait(sp, s_bi, NU * it)
                        r_.carrier(sp)
                        for dst, src in ((upT, "WupT"), (up, "Wup"), (wg, "Wg"), (wd, "Wd")):
                            sp.dma_start(dst[u][:, :, :], a[src][bass.ds(e, 1)].rearrange("o (k p) n -> p (o k) n", p=P)
                                         ).then_inc(s_ld[u], 16)

            @block.scalar
            def _(act):
                with act.Fori(0, NIT) as it:
                    for u in range(NU):
                        e = NU * it + u
                        wait(act, s_ld[u], 64 * (it + 1))
                        for raw, h in ((up, "uH"), (wd, "dH")):
                            act.activation(w[h][:, bass.ds(e, 1)].rearrange("p o k n -> p (o k) n"), raw[u][:, :, :],
                                           ACT.Copy).then_inc(s_H, 1)
                        wait(act, s_c, e + 1)
                        act.activation(w["cH"][:, bass.ds(e, 1)].rearrange("p o k n -> p (o k) n"), comb[u][:, :, :],
                                       ACT.Copy).then_inc(s_cH, 1)

            @block.vector
            def _(dve):
                def low(dst, src, high, e):
                    v = lambda t: t[:, bass.ds(e, 1)].rearrange("p o k n -> p (o k n)")
                    return dve.tensor_tensor(v(w[dst]), src.rearrange("p k n -> p (k n)"), v(w[high]).bitcast(F32),
                                             ALU.subtract)

                wait(dve, s_b, 48)
                with dve.Fori(0, NIT) as it:
                    for u in range(NU):
                        e = NU * it + u
                        wait(dve, s_H, 2 * e + 2)
                        low("uL", up[u][:, :, :], "uH", e).then_inc(s_L, 1)
                        low("dL", wd[u][:, :, :], "dH", e).then_inc(s_L, 1)
                        wait(dve, s_cH, e + 1)
                        low("cL", comb[u][:, :, :], "cH", e).then_inc(s_cL, 1)
                        wait(dve, s_bi, e + 1)
                        dve.tensor_tensor(w["bc"][:, bass.ds(e, 1)].rearrange("p o k -> p (o k)"), bias[u][:, 0:KC],
                                          bg[:, bass.ds(e, 1)].rearrange("p o k -> p (o k)"), ALU.add).then_inc(s_bo, 1)

            @block.tensor
            def _(pe):
                wait(pe, s_b, 48)
                with pe.Fori(0, NIT) as it:
                    for u in range(NU):
                        e = NU * it + u
                        wait(pe, s_ld[u], 64 * (it + 1))
                        wait(pe, s_bo, NU * it)
                        for m in range(KC):
                            for k in range(KC):
                                ins = pe.matmul(comb[u][:, m, :], upT[u][:, k, m * P:(m + 1) * P], wg[u][:, k, :],
                                                start=k == 0, stop=k == KC - 1)
                        ins.then_inc(s_c, 1)
                        for m in range(KC):
                            for k in range(KC):
                                ins = pe.matmul(bias[u][:, m:m + 1], wg[u][:, k, m * P:(m + 1) * P],
                                                w["bu"][:, bass.ds(e, 1), k],
                                                start=k == 0, stop=k == KC - 1)
                        ins.then_inc(s_bi, 1)


def stage_mix(nc, a, YS, X1S, FS, tg, idf):
    with ExitStack() as ctx:
        r_ = Res(nc, ctx, "mx_")
        wraw, wH, wL = r_.sb("wraw", [P, KC, C]), r_.sb("wH", [P, KC, C], F32R), r_.sb("wL", [P, KC, C], F32R)
        bp = r_.sb("bp", [P, QT, C])
        NU = 2
        y, x, x1, xf = ([r_.sb(f"{n}{u}", [P, QT, C]) for u in range(NU)] for n in ("y", "x", "x1", "xf"))
        yH, yL = ([r_.sb(f"{n}{u}", [P, KC, T], F32R) for u in range(NU)] for n in ("yH", "yL"))
        st6, st2 = ([r_.sb(f"{n}{u}", [P, QT, m]) for u in range(NU)] for n, m in (("st6", 6), ("st2", 2)))
        var, rstd = ([r_.sb(f"{n}{u}", [P, QT]) for u in range(NU)] for n in ("var", "rstd"))
        expo = r_.sb("expo", [P, QT])
        tp = [r_.ps(f"tp{c}", [P, T]) for c in range(KC)]
        op = [[r_.ps(f"op{u}{i}", [P, 2, C]) for i in range(2)] for u in range(NU)]
        s_w, s_wH, s_wL, s_bp, s_xb, s_T, s_yH, s_yL, s_op, s_x1, s_st, s_ln, s_rs, s_xf, s_e = (
            r_.sem(n) for n in ("w", "wH", "wL", "bp", "xb", "T", "yH", "yL", "op", "x1", "st", "ln", "rs", "xf", "e"))
        s_ld, s_so = ([r_.sem(f"{n}{u}") for u in range(NU)] for n in ("ld", "so"))
        NIT = B // NU

        r_.prime()
        with nc.Block() as block:

            @block.sync
            def _(sp):
                sp.dma_start(wraw[:, :, :], a["Wp"].rearrange("(k p) n -> p k n", p=P)).then_inc(s_w, 16)
                for t in range(QT):
                    sp.dma_start(bp[:, t], a["bp"].rearrange("(o c) -> o c", o=1).to_broadcast([P, C])).then_inc(s_w, 16)
                with sp.Fori(0, NIT) as it:
                    for u in range(NU):
                        b = NU * it + u
                        wait(sp, s_T, KC * NU * it)
                        wait(sp, s_x1, QT // 2 * NU * it)
                        for g in range(NG):
                            sp.dma_start(y[u][:, :, g * GC:(g + 1) * GC],
                                         YS[bass.ds(NG * b + g + 1, 1)].rearrange("o p t c -> (o p) t c")).then_inc(s_ld[u], 16)
                        sp.dma_start(x[u][:, :, :], a["x"][bass.ds(b, 1)].rearrange("o (t p) c -> p (o t) c", p=P)
                                     ).then_inc(s_ld[u], 16)

            @block.gpsimd
            def _(pool):
                pool.memset(expo[:, :], -0.5).then_inc(s_e, 1)
                wait(pool, s_e, 1)
                wait(pool, s_bp, QT)
                with pool.Fori(0, NIT) as it:
                    for u in range(NU):
                        b = NU * it + u
                        wait(pool, s_ld[u], 16 * (NG + 1) * (it + 1))
                        pool.tensor_tensor(x[u][:, :, :], x[u][:, :, :], bp[:, :, :], ALU.add).then_inc(s_xb, 1)
                    for u in range(NU):
                        b = NU * it + u
                        wait(pool, s_ln, 2 * (b + 1))
                        pool.tensor_tensor(rstd[u][:, :], var[u][:, :], expo[:, :], ALU.pow).then_inc(s_rs, 1)

            @block.scalar
            def _(act):
                wait(act, s_w, 16 * (1 + QT))
                act.activation(wH[:, :, :], wraw[:, :, :], ACT.Copy).then_inc(s_wH, 1)
                for t in range(QT):
                    act.activation(bp[:, t], bp[:, t], ACT.Copy, scale=tg[:, 0:1]).then_inc(s_bp, 1)
                with act.Fori(0, NIT) as it:
                    for u in range(NU):
                        b = NU * it + u
                        wait(act, s_op, 2 * NU * it)
                        for c in range(KC):
                            wait(act, s_T, KC * b + c + 1)
                            act.activation(yH[u][:, c, :], tp[c][:, :], ACT.Copy).then_inc(s_yH, 1)
                    for u in range(NU):
                        b = NU * it + u
                        wait(act, s_x1, QT // 2 * (b + 1))
                        act.dma_start(X1S[bass.ds(b, 1)].rearrange("o p t c -> (o p) t c"), x1[u][:, :, :]).then_inc(s_so[u], 16)
                        wait(act, s_xf, QT * (b + 1))
                        act.dma_start(FS[bass.ds(b, 1)].rearrange("o p t c -> (o p) t c"), xf[u][:, :, :]).then_inc(s_so[u], 16)
                for u in range(NU):
                    wait(act, s_so[u], 32 * NIT)

            @block.vector
            def _(dve):
                wait(dve, s_wH, 1)
                dve.tensor_tensor(wL[:, :, :], wraw[:, :, :], wH[:, :, :].bitcast(F32), ALU.subtract).then_inc(s_wL, 1)
                with dve.Fori(0, NIT) as it:
                    for u in range(NU):
                        b = NU * it + u
                        for c in range(KC):
                            wait(dve, s_yH, KC * b + c + 1)
                            dve.tensor_tensor(yL[u][:, c, :], tp[c][:, :], yH[u][:, c, :].bitcast(F32), ALU.subtract
                                              ).then_inc(s_yL, 1)
                    for u in range(NU):
                        b = NU * it + u
                        wait(dve, s_xb, b + 1)
                        wait(dve, s_so[u], 32 * it)
                        for i in range(QT // 2):
                            wait(dve, s_op, 2 * b + i + 1)
                            dve.scalar_tensor_tensor(x1[u][:, 2 * i:2 * i + 2, :].rearrange("p t c -> p (t c)"),
                                                     op[u][i][:, :, :].rearrange("p t c -> p (t c)"), tg[:, 0:1],
                                                     x[u][:, 2 * i:2 * i + 2, :].rearrange("p t c -> p (t c)"),
                                                     ALU.mult, ALU.add).then_inc(s_x1, 1)
                        wait(dve, s_x1, QT // 2 * (b + 1))
                        for t in range(QT):
                            ins = dve.bn_stats(st6[u][:, t, :], x1[u][:, t, :])
                        ins.then_inc(s_st, 1)
                        wait(dve, s_st, b + 1)
                        r_.carrier(dve)
                        for t in range(QT):
                            ins = dve.bn_aggr(st2[u][:, t, :], st6[u][:, t, :])
                        ins.then_inc(s_ln, 1)
                        wait(dve, s_ln, 2 * b + 1)
                        dve.tensor_scalar(var[u][:, :], st2[u][:, :, 1], LN_EPS, None, ALU.add).then_inc(s_ln, 1)
                    for u in range(NU):
                        b = NU * it + u
                        wait(dve, s_rs, b + 1)
                        for t in range(QT):
                            dve.tensor_scalar(xf[u][:, t, :], x1[u][:, t, :], st2[u][:, t, 0:1], rstd[u][:, t:t + 1],
                                              ALU.subtract, ALU.mult).then_inc(s_xf, 1)

            @block.tensor
            def _(pe):
                wait(pe, s_wL, 1)
                with pe.Fori(0, NIT) as it:
                    for u in range(NU):
                        b = NU * it + u
                        wait(pe, s_ld[u], 16 * (NG + 1) * (it + 1))
                        wait(pe, s_yL, KC * b)
                        for c in range(KC):
                            for t in range(QT):
                                ins = pe.transpose(tp[c][:, t * P:(t + 1) * P], y[u][:, t, c * P:(c + 1) * P], idf[:, :])
                            ins.then_inc(s_T, 1)
                    for u in range(NU):
                        b = NU * it + u
                        wait(pe, s_yL, KC * (b + 1))
                        wait(pe, s_x1, QT // 2 * NU * it)
                        for t in range(QT):
                            tok = slice(t * P, (t + 1) * P)
                            for c in range(KC):
                                ins = mm3(pe, op[u][t // 2][:, t % 2, :], yH[u][:, c, tok], yL[u][:, c, tok],
                                          wH[:, c, :], wL[:, c, :], c == 0, c == KC - 1)
                            if t % 2:
                                ins.then_inc(s_op, 1)


def stage_experts(nc, a, FS, w, idf):
    with ExitStack() as ctx:
        r_ = Res(nc, ctx, "ex_")
        rraw = r_.sb("rraw", [P, NL, KC, NE])
        rw = r_.sb("rw", [P, NL, KC, 2 * NE], F32R)
        rb, gb = r_.sb("rb", [P, NL, QT, NE]), r_.sb("gb", [P, NL, QT, NE])
        nw = r_.sb("nw", [P, NL, C])
        prio, expo = r_.sb("prio", [P, QT, NE]), r_.sb("expo", [P, QT])
        xs = [r_.sb(f"xs{u}", [P, QT, C]) for u in range(2)]
        xH, xL = ([r_.sb(f"{n}{u}", [P, KC, T], F32R) for u in range(2)] for n in ("xH", "xL"))
        sg = [r_.sb(f"sg{c}", [P, T]) for c in range(KC)]
        af = [[r_.sb(f"af{u}{c}", [P, T]) for c in range(KC)] for u in range(2)]
        RA = 4
        aH, aL = ([[r_.sb(f"{n}{i}{c}", [P, T], F32R) for c in range(KC)] for i in range(RA)] for n in ("aH", "aL"))
        wt = [r_.sb(f"wt{u}", [P, QT, NE + 1]) for u in range(2)]
        wT = r_.sb("wT", [NE + 1, T])
        Z = [r_.sb(f"Z{u}", [P, QT, C]) for u in range(2)]
        sq = r_.sb("sq", [P, QT, C])
        ss, ms, rr = ([r_.sb(f"{n}{u}", [P, QT]) for u in range(2)] for n in ("ss", "ms", "rr"))
        sm = {n: r_.sb("g_" + n, [P, QT, NE]) for n in ("gt", "bi", "eq", "s1", "s2", "tmp")}
        s4 = {n: r_.sb("g4_" + n, [P, QT, 1]) for n in ("m", "v1", "v2", "d", "th", "w1", "w2")}
        GH = [r_.ps(f"GH{i}", [P, T]) for i in range(4)]
        Dn = [r_.ps(f"D{i}", [P, 2, C]) for i in range(2)]
        XT, RB = r_.ps("XT", [P, T]), r_.ps("RB", [P, T])

        (s_c, s_pool, s_rw, s_T, s_xH, s_xL, s_G, s_gate, s_d, s_th, s_WT, s_wT, s_up, s_sg, s_a, s_aH, s_aL, s_dn, s_z,
         s_ss, s_ms, s_rr, s_y, s_rwH, s_wt, s_nrm) = (
            r_.sem(n) for n in ("c", "pool", "rw", "T", "xH", "xL", "G", "gate", "d", "th", "WT", "wT", "up", "sg", "a",
                                "aH", "aL", "dn", "z", "ss", "ms", "rr", "y", "rwH", "wt", "nrm"))
        s_ld, s_st = ([r_.sem(f"{n}{u}") for u in range(2)] for n in ("ld", "st"))

        NM = NL * B
        ORDER = [NE + i for i in range(NS)] + list(range(NE))
        NDN = NX - NS + 1
        NDB = 2 * NDN
        LAST = NX - 1
        assert NX == 8 and NS == 2 and RA == 4
        REST = [("U", 1), ("tSq",), ("WT",), ("U", 2), ("tMs",), ("D", 1), ("U", 3), ("tNorm",), ("D", 2), ("tSt",),
                ("nT", 0), ("U", 4), ("D", 3), ("nT", 1), ("U", 5), ("D", 4), ("nR",), ("U", 6), ("nTh",), ("D", 5),
                ("U", 7), ("nGate",), ("D", 6), ("nU",), ("D", 7)]
        HEAD = [("nT", 0), ("nT", 1), ("nR",), ("nTh",), ("nGate",), ("nU",)]
        TAILS = [("tSq",), ("tMs",), ("tNorm",), ("tSt",)]

        def run(eng, do):
            def unit(m, h, u, prev, nxt):
                hp, hn = (h - 1 if u == 0 else h), (h if u == 0 else h + 1)
                for e in REST:
                    if e[0][0] == "n":
                        if nxt:
                            do(e, m + 1, 1 - u, hn)
                    elif e[0][0] == "t":
                        if prev:
                            do(e, m - 1, 1 - u, hp)
                    else:
                        do(e, m, u, h)

            for e in HEAD:
                do(e, 0, 0, 0)
            unit(0, 0, 0, False, True)
            with eng.Fori(0, NM // 2 - 1) as it:
                unit(2 * it + 1, it, 1, True, True)
                unit(2 * it + 2, it + 1, 0, True, True)
            unit(NM - 1, NM // 2 - 1, 1, True, False)
            for e in TAILS:
                do(e, NM - 1, 1, NM // 2 - 1)

        def freed_by(m, x):
            if x < RA:
                return NDB * m + 2 * (x + RA - 1)
            return NDB * (m + 1) + 2 * max(1, x - RA)

        r_.prime({s_aL.name: 4, s_a.name: 2, s_z.name: 2, s_sg.name: 2, s_dn.name: NDB})
        with nc.Block() as block:

            @block.sync
            def _(sp):
                sp.dma_start(rraw[:, :, :, :], a["router_W"]).then_inc(s_c, 16)
                for dst, src in ((rb, "router_b"), (gb, "gate_bias")):
                    for j in range(NL):
                        for t in range(QT):
                            sp.dma_start(dst[:, j, t], a[src][j:j + 1, :].to_broadcast([P, NE])).then_inc(s_c, 16)
                for j in range(NL):
                    sp.dma_start(nw[:, j], a["norm_w"][j:j + 1, :].to_broadcast([P, C])).then_inc(s_c, 16)

                def load(m, u):
                    sp.dma_start(xs[u][:, :, :], FS[bass.ds(m % B, 1)].rearrange("o p t c -> (o p) t c")).then_inc(s_ld[u], 16)

                for m in range(2):
                    load(m, m)
                with sp.Fori(1, B // 2) as h:
                    for u in range(2):
                        m = 2 * h + u
                        wait(sp, s_z, 2 + NDB * (m - 2) + 2)
                        load(m, u)
                with sp.Fori(B // 2, NM // 2) as h:
                    for u in range(2):
                        m = 2 * h + u
                        wait(sp, s_z, 2 + NDB * (m - 2) + 2)
                        wait(sp, s_st[u], 16 * (h - B // 2 + 1))
                        load(m, u)
                for u in range(2):
                    wait(sp, s_st[u], 16 * (NM // 2))

            @block.gpsimd
            def _(pool):
                pool.memset(expo[:, :], -0.5).then_inc(s_pool, 1)
                for e in range(NE):
                    pool.memset(prio[:, :, e:e + 1], float(NE - e)).then_inc(s_pool, 1)
                for u in range(2):
                    pool.memset(wt[u][:, :, NE:NE + 1], float(NS)).then_inc(s_pool, 1)
                wait(pool, s_pool, 1)

                def do(e, m, u, h):
                    if e[0] in ("U", "nU"):
                        x = e[1] if e[0] == "U" else 0
                        for c in range(KC):
                            wait(pool, s_aH, 2 * (NX * m + x) + c + 1)
                            pool.tensor_tensor(aL[x % RA][c][:, :], af[x % 2][c][:, :],
                                               aH[x % RA][c][:, :].bitcast(F32), ALU.subtract).then_inc(s_aL, 1)
                    elif e[0] == "tMs":
                        wait(pool, s_ms, m + 1)
                        pool.tensor_tensor(rr[u][:, :], ms[u][:, :], expo[:, :], ALU.pow).then_inc(s_rr, 1)

                run(pool, do)

            @block.vector
            def _(dve):
                wait(dve, s_c, 16 * (1 + 2 * NL * QT + NL))
                wait(dve, s_rwH, 1)
                dve.tensor_tensor(rw[:, :, :, NE:2 * NE], rraw[:, :, :, :], rw[:, :, :, 0:NE].bitcast(F32), ALU.subtract
                                  ).then_inc(s_rw, 1)
                wait(dve, s_pool, NE + 3)
                GN = 18

                def wide(t):
                    return t[:, :, :].to_broadcast([P, QT, NE])

                def router_choice(m):
                    k = [0]

                    def link(ins):
                        k[0] += 1
                        ins.then_inc(s_gate, 1)
                        wait(dve, s_gate, GN * m + k[0])

                    gt, bi, eq, tmp = (sm[n][:, :, :] for n in ("gt", "bi", "eq", "tmp"))
                    j = m // B
                    lay = lambda t: t[:, bass.ds(j, 1)].rearrange("p o t e -> p (o t) e")
                    logits = RB[:, 0:QT * 2 * NE].rearrange("p (t e) -> p t e", t=QT)
                    wait(dve, s_G, m + 1)
                    wait(dve, s_WT, m)
                    link(dve.tensor_tensor(tmp, logits[:, :, 0:NE], lay(rb), ALU.add))
                    link(dve.tensor_tensor(gt, logits[:, :, NE:2 * NE], tmp, ALU.add))
                    link(dve.tensor_tensor(bi, gt, lay(gb), ALU.add))
                    for n, v in (("s1", "v1"), ("s2", "v2")):
                        s = sm[n][:, :, :]
                        link(dve.tensor_reduce(s4["m"][:, :, :], bi, AX.X, ALU.max))
                        link(dve.tensor_tensor(eq, bi, wide(s4["m"]), ALU.is_ge))
                        link(dve.tensor_tensor(eq, eq, prio[:, :, :], ALU.mult))
                        link(dve.tensor_reduce(s4["m"][:, :, :], eq, AX.X, ALU.max))
                        link(dve.tensor_tensor(s, eq, wide(s4["m"]), ALU.is_equal))
                        link(dve.tensor_tensor(tmp, s, gt, ALU.mult))
                        link(dve.tensor_reduce(s4[v][:, :, :], tmp, AX.X, ALU.add))
                        if n == "s1":
                            link(dve.scalar_tensor_tensor(bi, s, NEG, bi, ALU.mult, ALU.add))
                    assert k[0] == GN
                    dve.tensor_tensor(s4["d"][:, :, :], s4["v1"][:, :, :], s4["v2"][:, :, :], ALU.subtract).then_inc(s_d, 1)

                def router_weights(m, u):
                    w1, w2, th = (s4[n][:, :, :] for n in ("w1", "w2", "th"))
                    s1, s2 = sm["s1"][:, :, :], sm["s2"][:, :, :]
                    wait(dve, s_th, m + 1)
                    dve.tensor_scalar(w1, th, 0.5, 0.5, ALU.mult, ALU.add).then_inc(s_y, 1)
                    dve.tensor_scalar(w2, th, -0.5, 0.5, ALU.mult, ALU.add).then_inc(s_y, 1)
                    wait(dve, s_y, 4 * m + 2)
                    dve.tensor_tensor(s1, s1, wide(s4["w1"]), ALU.mult).then_inc(s_y, 1)
                    dve.tensor_tensor(s2, s2, wide(s4["w2"]), ALU.mult).then_inc(s_y, 1)
                    wait(dve, s_y, 4 * m + 4)
                    dve.tensor_tensor(wt[u][:, :, 0:NE], s1, s2, ALU.add).then_inc(s_wt, 1)

                def do(e, m, u, h):
                    if e[0] == "nT":
                        c = e[1]
                        wait(dve, s_xH, KC * m + c + 1)
                        dve.tensor_tensor(xL[u][:, c, :], XT[:, :], xH[u][:, c, :].bitcast(F32), ALU.subtract).then_inc(s_xL, 1)
                    elif e[0] == "nR":
                        router_choice(m)
                    elif e[0] == "nGate":
                        router_weights(m, u)
                    elif e[0] == "WT":
                        wait(dve, s_WT, m + 1)
                        wait(dve, s_dn, NDB * m + 2)
                        dve.tensor_copy(wT[:, :], RB[0:NE + 1, :]).then_inc(s_wT, 1)
                    elif e[0] in ("U", "nU"):
                        x = e[1] if e[0] == "U" else 0
                        for c in range(KC):
                            n = NX * m + x
                            wait(dve, s_up, 4 * n + 2 * c + 2)
                            wait(dve, s_sg, 2 + 2 * n + c + 1)
                            wait(dve, s_aL, 2 * n + c + 1)
                            dve.scalar_tensor_tensor(af[x % 2][c][:, :], GH[2 * c + 1][:, :], w["bu"][:, ORDER[x], c:c + 1],
                                                     sg[c][:, :], ALU.add, ALU.mult).then_inc(s_a, 1)
                    elif e[0] == "D":
                        d = e[1] - 1
                        for k in range(2):
                            wait(dve, s_dn, NDB * (m + 1) + 2 * d + k + 1)
                            if d == 0:
                                if k == 0:
                                    wait(dve, s_st[u], 16 * h)
                                ins = dve.tensor_tensor(Z[u][:, 2 * k:2 * k + 2, :], Dn[k][:, :, :],
                                                        xs[u][:, 2 * k:2 * k + 2, :], ALU.add)
                            else:
                                wait(dve, s_z, NDB * m + 2 * d + k + 1)
                                for t in (2 * k, 2 * k + 1):
                                    ex = ORDER[e[1]]
                                    ins = dve.scalar_tensor_tensor(Z[u][:, t, :], Dn[k][:, t % 2, :], wt[u][:, t, ex:ex + 1],
                                                                   Z[u][:, t, :], ALU.mult, ALU.add)
                            ins.then_inc(s_z, 1)
                    elif e[0] == "tMs":
                        wait(dve, s_ss, m + 1)
                        dve.tensor_scalar(ms[u][:, :], ss[u][:, :], 1.0 / C, RMS_EPS, ALU.mult, ALU.add).then_inc(s_ms, 1)
                    elif e[0] == "tNorm":
                        wait(dve, s_rr, m + 1)
                        for t in range(QT):
                            ins = dve.scalar_tensor_tensor(
                                Z[u][:, t, :], Z[u][:, t, :], rr[u][:, t:t + 1],
                                nw[:, bass.ds(m // B, 1), :].rearrange("p o c -> p (o c)"), ALU.mult, ALU.mult)
                        ins.then_inc(s_nrm, 1)

                run(dve, do)

            @block.scalar
            def _(act):
                wait(act, s_c, 16 * (1 + 2 * NL * QT + NL))
                act.activation(rw[:, :, :, 0:NE], rraw[:, :, :, :], ACT.Copy).then_inc(s_rwH, 1)

                def do(e, m, u, h):
                    if e[0] == "nT":
                        c = e[1]
                        wait(act, s_T, KC * m + c + 1)
                        act.activation(xH[u][:, c, :], XT[:, :], ACT.Copy).then_inc(s_xH, 1)
                    elif e[0] == "nTh":
                        wait(act, s_d, m + 1)
                        act.activation(s4["th"][:, :, :], s4["d"][:, :, :], ACT.Tanh, scale=0.5).then_inc(s_th, 1)
                    elif e[0] in ("U", "nU"):
                        x = e[1] if e[0] == "U" else 0
                        n = NX * m + x
                        for c in range(KC):
                            wait(act, s_up, 4 * n + 2 * c + 1)
                            wait(act, s_a, 2 * n + c + 1)
                            act.activation(sg[c][:, :], GH[2 * c][:, :], ACT.Silu, bias=w["bc"][:, ORDER[x], c:c + 1],
                                           scale=1.0).then_inc(s_sg, 1)
                        wait(act, s_dn, freed_by(m, x))
                        for c in range(KC):
                            wait(act, s_a, 2 + 2 * n + c + 1)
                            act.activation(aH[x % RA][c][:, :], af[x % 2][c][:, :], ACT.Copy).then_inc(s_aH, 1)
                    elif e[0] == "tSq":
                        wait(act, s_z, 2 + NDB * (m + 1))
                        for t in range(QT):
                            ins = act.activation(sq[:, t, :], Z[u][:, t, :], ACT.Square, accum_out=ss[u][:, t:t + 1])
                        ins.then_inc(s_ss, 1)
                    elif e[0] == "tSt":
                        wait(act, s_nrm, m + 1)
                        act.dma_start(FS[bass.ds(m % B, 1)].rearrange("o p t c -> (o p) t c"), Z[u][:, :, :]
                                      ).then_inc(s_st[u], 16)

                run(act, do)

            @block.tensor
            def _(pe):
                wait(pe, s_rw, 1)

                def up(m, x):
                    e, n = ORDER[x], NX * m + x
                    u = UP[0]
                    for c in range(KC):
                        cols = slice(c * P, (c + 1) * P)
                        for i, (wh, wl) in enumerate(((w["cH"], w["cL"]), (w["uH"], w["uL"]))):
                            wait(pe, (s_sg, s_a)[i], 2 * n + c + 1)
                            for k in range(KC):
                                ins = mm3(pe, GH[2 * c + i][:, :], wh[:, e, k, cols], wl[:, e, k, cols], xH[u][:, k, :],
                                          xL[u][:, k, :], k == 0, k == KC - 1)
                            ins.then_inc(s_up, 1)

                UP = [0]

                def do(e, m, u, h):
                    if e[0] == "nT":
                        c = e[1]
                        if c == 0:
                            wait(pe, s_ld[u], 16 * (h + 1))
                        wait(pe, s_xL, KC * m + c)
                        for t in range(QT):
                            ins = pe.transpose(XT[:, t * P:(t + 1) * P], xs[u][:, t, c * P:(c + 1) * P], idf[:, :])
                        ins.then_inc(s_T, 1)
                    elif e[0] == "nR":
                        wait(pe, s_xL, KC * (m + 1))
                        wait(pe, s_wT, m)
                        for t in range(QT):
                            tok = slice(t * P, (t + 1) * P)
                            for k in range(KC):
                                for i, x in enumerate((xL, xH)):
                                    ins = pe.matmul(RB[:, t * 2 * NE:(t + 1) * 2 * NE], x[u][:, k, tok],
                                                    rw[:, bass.ds(m // B, 1), k, :].rearrange("p o e -> p (o e)"),
                                                    start=k == 0 and i == 0, stop=k == KC - 1 and i == 1)
                        ins.then_inc(s_G, 1)
                    elif e[0] in ("U", "nU"):
                        UP[0] = u
                        up(m, e[1] if e[0] == "U" else 0)
                    elif e[0] == "WT":
                        wait(pe, s_wt, m + 1)
                        for t in range(QT):
                            ins = pe.transpose(RB[0:NE + 1, t * P:(t + 1) * P], wt[u][:, t, :], idf[:, :])
                        ins.then_inc(s_WT, 1)
                    elif e[0] == "D":
                        d = e[1] - 1
                        xs_ = [0, 1] if d == 0 else [e[1]]
                        wait(pe, s_aL, 4 + 2 * (NX * m + xs_[-1]) + 2)
                        if d == 0:
                            wait(pe, s_wT, m + 1)
                        for k in range(2):
                            wait(pe, s_z, NDB * m + 2 * d + k + 1)
                            for t in (2 * k, 2 * k + 1):
                                tok = slice(t * P, (t + 1) * P)
                                out = Dn[k][:, t % 2, :]
                                if d == 0:
                                    pe.matmul(out, wT[:, tok], w["bd"][:, :], start=True, stop=False)
                                for x in xs_:
                                    for c in range(KC):
                                        ins = mm3(pe, out, aH[x % RA][c][:, tok], aL[x % RA][c][:, tok],
                                                  w["dH"][:, ORDER[x], c, :], w["dL"][:, ORDER[x], c, :],
                                                  d > 0 and c == 0, x == xs_[-1] and c == KC - 1)
                            ins.then_inc(s_dn, 1)

                run(pe, do)


def stage_finish(nc, X1S, FS, tg, out):
    with ExitStack() as ctx:
        r_ = Res(nc, ctx, "fi_")
        NU = 2
        x1, y = ([r_.sb(f"{n}{u}", [P, QT, C]) for u in range(NU)] for n in ("x1", "y"))
        s_ld, s_so = ([r_.sem(f"{n}{u}") for u in range(NU)] for n in ("ld", "so"))
        s_s = r_.sem("s")
        flat = lambda t: t[:, :, :].rearrange("p t c -> p (t c)")

        r_.prime()
        with nc.Block() as block:

            @block.sync
            def _(sp):
                with sp.Fori(0, B // NU) as it:
                    for u in range(NU):
                        b = NU * it + u
                        wait(sp, s_so[u], 16 * it)
                        sp.dma_start(x1[u][:, :, :], X1S[bass.ds(b, 1)].rearrange("o p t c -> (o p) t c")).then_inc(s_ld[u], 16)
                        sp.dma_start(y[u][:, :, :], FS[bass.ds(b, 1)].rearrange("o p t c -> (o p) t c")).then_inc(s_ld[u], 16)

            @block.vector
            def _(dve):
                with dve.Fori(0, B // NU) as it:
                    for u in range(NU):
                        b = NU * it + u
                        wait(dve, s_ld[u], 32 * (it + 1))
                        dve.scalar_tensor_tensor(flat(y[u]), flat(y[u]), tg[:, 1:2], flat(x1[u]), ALU.mult, ALU.add
                                                 ).then_inc(s_s, 1)

            @block.scalar
            def _(act):
                with act.Fori(0, B // NU) as it:
                    for u in range(NU):
                        b = NU * it + u
                        wait(act, s_s, b + 1)
                        act.dma_start(out[bass.ds(b, 1)].rearrange("o (t p) c -> p (o t) c", p=P), y[u][:, :, :]
                                      ).then_inc(s_so[u], 16)
                for u in range(NU):
                    wait(act, s_so[u], 16 * (B // NU))


def stage_constants(nc, a, idf, idb, mq, mk, tg, graw):
    with ExitStack() as ctx:
        r_ = Res(nc, ctx, "co_")
        s_g, s_m, s_t = r_.sem("g"), r_.sem("m"), r_.sem("t")
        r_.prime()
        with nc.Block() as block:

            @block.sync
            def _(sp):
                for n, g in enumerate(("g_xattn", "g_ffn")):
                    sp.dma_start(graw[:, n:n + 1], a[g].rearrange("(o c) -> o c", o=1).to_broadcast([P, 1])).then_inc(s_g, 16)

            @block.gpsimd
            def _(pool):
                for t, v in ((idf, 1.0), (idb, 1.0), (mq, 0.0), (mk, 0.0)):
                    pool.memset(t[:, :], v).then_inc(s_m, 1)
                wait(pool, s_m, 4)
                for t in (idf, idb):
                    pool.affine_select(out=t[:, :], in_=t[:, :], compare_op=ALU.is_equal, fill=0.0, base=0,
                                       pattern=[[-1, P]], channel_multiplier=1)
                pool.affine_select(out=mq[:, :], in_=mq[:, :], compare_op=ALU.is_ge, fill=NEG, base=0,
                                   pattern=[[-1, P]], channel_multiplier=1)
                pool.affine_select(out=mk[:, :], in_=mk[:, :], compare_op=ALU.is_ge, fill=NEG, base=0,
                                   pattern=[[1, P]], channel_multiplier=-1)

            @block.scalar
            def _(act):
                wait(act, s_g, 32)
                act.activation(tg[:, :], graw[:, :], ACT.Tanh).then_inc(s_t, 1)


def build(nc, a, out):
    QS = nc.dram_tensor("q_parts", [3, NI * GC, 2 * T], BF16).ap()
    KS = nc.dram_tensor("k_parts", [3, NI * GC, NK], BF16).ap()
    VS = nc.dram_tensor("v_items", [NI, P, NKT, GC], F32).ap()
    YS = nc.dram_tensor("y_items", [NI + 1, P, QT, GC], F32).ap()
    X1S = nc.dram_tensor("x1_blocks", [B, P, QT, C], F32).ap()
    FS = nc.dram_tensor("ffn_blocks", [B, P, QT, C], F32).ap()
    with ExitStack() as ctx:
        r_ = Res(nc, ctx, "c_")
        idf, idb = r_.sb("idf", [P, P]), r_.sb("idb", [P, P], BF16)
        mq, mk = r_.sb("mq", [P, P], BF16), r_.sb("mk", [P, P], BF16)
        tg, graw = r_.sb("tg", [P, 2]), r_.sb("graw", [P, 2])
        stage_constants(nc, a, idf, idb, mq, mk, tg, graw)
        stage_project(nc, a, QS, KS, VS, idf)
        stage_attend(nc, QS, KS, VS, YS, idf, idb, mq, mk)
        stage_mix(nc, a, YS, X1S, FS, tg, idf)
        w = {n: r_.sb(n, [P, NX, KC, IW], F32R) for n in ("uH", "uL", "cH", "cL", "dH", "dL")}
        w.update(bu=r_.sb("bu", [P, NX, KC]), bc=r_.sb("bc", [P, NX, KC]), bd=r_.sb("bd", [NE + 1, C]))
        stage_fold(nc, a, w)
        stage_experts(nc, a, FS, w, idf)
        stage_finish(nc, X1S, FS, tg, out)


def lay_out(i):
    f = lambda n: np.ascontiguousarray(np.asarray(i[n], np.float32))
    att, ffn = (lambda n: f("L0_xattn_" + n)), (lambda n: f("L0_ffn_" + n))
    up = np.concatenate([ffn("exp_Wup"), ffn("share_Wup").reshape(C, NS, IW).transpose(1, 0, 2)])
    shared = lambda e, s: np.concatenate([ffn(e)] + [ffn(s)[None]] * NS)
    cols = lambda v: v.reshape(*v.shape[:-1], KC, P)
    bup = np.concatenate([ffn("exp_bup"), ffn("share_bup").reshape(NS, IW)])
    d = {n: att(n) for n in ("Wk", "Wq", "Wv", "bv", "Wck", "Wcq", "Wcv", "bcv", "Wp", "bp")}
    d["bcol"] = cols(np.stack([att(n) for n in ("bq", "bcq", "bk", "bck")])).transpose(2, 0, 1)
    d.update(x=f("x"), ctxT=f("ctx_512").transpose(0, 2, 1), g_xattn=f("g_xattn"), g_ffn=f("g_ffn"),
             Wup=up, WupT=up.transpose(0, 2, 1), Wg=shared("exp_Wg", "share_Wg"), Wd=shared("exp_Wdown", "share_Wdown"),
             bup=cols(bup).transpose(2, 0, 1), bg=cols(shared("exp_bg", "share_bg")).transpose(2, 0, 1),
             bd=np.concatenate([ffn("exp_bdown"), ffn("share_bdown")[None]]),
             router_W=ffn("router_W").reshape(NL, KC, P, NE).transpose(2, 0, 1, 3), router_b=ffn("router_b"), gate_bias=ffn("gate_bias"), norm_w=ffn("norm_w"))
    return {n: np.ascontiguousarray(v) for n, v in d.items()}


def kernel(**inputs):
    import concourse.bacc as bacc
    from concourse.bass_utils import run_bass_kernel_spmd

    nc = bacc.Bacc("TRN2", target_bir_lowering=False, num_devices=1)
    arrays = lay_out(inputs)
    aps = {n: nc.dram_tensor("in_" + n, v.shape, mybir.dt.from_np(v.dtype), kind="ExternalInput").ap()
           for n, v in arrays.items()}
    out = nc.dram_tensor("out", (B, T, C), F32, kind="ExternalOutput").ap()
    build(nc, aps, out)
    r = run_bass_kernel_spmd(nc, [{"in_" + n: v for n, v in arrays.items()}], core_ids=[0])
    return r.results[0]["out"]
```

```python
from contextlib import ExitStack

import numpy as np

import concourse.bass as bass
import concourse.mybir as mybir
from concourse.alu_op_type import AluOpType as ALU

ACT = mybir.ActivationFunctionType
AX = mybir.AxisListType
F32, F32R, BF16 = mybir.dt.float32, mybir.dt.float32r, mybir.dt.bfloat16

P = 128
B, T, C = 8, 512, 256
H, D = 16, 16
TC, CC = 1601, 128
KC = C // P
QT = T // P
G = 4
NG = H // G
NI = B * NG
GC = G * D
NK = T + TC
CTXT = -(-TC // P)
NKT = QT + CTXT
LASTK = TC - (CTXT - 1) * P
TCE = TC + TC % 2
SCALE = 1.0 / float(np.sqrt(D))
NEG = -3.0e38
NE, NS, NL, IW = 6, 2, 2, 256
NX = NE + NS
LN_EPS, RMS_EPS = 1e-5, 1e-6

QPART = [0, 1, 2, 0, 1, 0]
KPART = [0, 0, 0, 1, 1, 2]
KROWS = D * len(QPART)
SROWS = KROWS + 3


def bcast(ap, n, axis):
    shape = list(ap.shape)
    shape[axis] = n
    return ap.to_broadcast(shape)


class Res:

    def __init__(self, nc, ctx, prefix):
        self.nc, self.ctx, self.prefix, self.spare, self.sems = nc, ctx, prefix, {}, []

    def sb(self, name, shape, dt=F32):
        return self.ctx.enter_context(self.nc.sbuf_tensor(self.prefix + name, shape, dt))

    def ps(self, name, shape, dt=F32):
        return self.ctx.enter_context(self.nc.psum_tensor(self.prefix + name, shape, dt))

    def sem(self, name):
        s = self.ctx.enter_context(self.nc.semaphore(self.prefix + name))
        self.sems.append(s)
        return s

    def prime(self, credit=()):
        extra = dict(credit)
        with self.nc.Block() as block:

            @block.gpsimd
            def _(pool):
                for s in self.sems:
                    pool.sem_inc(s, 1 + extra.get(s.name, 0))

    def carrier(self, eng):
        if id(eng) not in self.spare:
            self.spare[id(eng)] = self.sem(f"spare{len(self.spare)}")
        eng.sem_inc(self.spare[id(eng)], 1)


def wait(eng, sem, count):
    eng.wait_ge(sem, count + 1)


def mm3(pe, out, wH, wL, xH, xL, start, stop):
    pe.matmul(out, wL, xH, start=start, stop=False)
    pe.matmul(out, wH, xL, start=False, stop=False)
    return pe.matmul(out, wH, xH, start=False, stop=stop)


def stage_project(nc, a, QS, KS, VS, idf):
    with ExitStack() as ctx:
        r_ = Res(nc, ctx, "pj_")
        wraw = r_.sb("wraw", [P, 4, KC, C])
        craw = r_.sb("craw", [P, 2, C])
        wH, wL = r_.sb("wH", [P, 4, KC, C], F32R), r_.sb("wL", [P, 4, KC, C], F32R)
        cH, cL = r_.sb("cH", [P, 2, C], F32R), r_.sb("cL", [P, 2, C], F32R)
        bcol = r_.sb("bcol", [P, 4, KC])
        bvrow = r_.sb("bvrow", [P, 2, C])
        xin, xn = r_.sb("xin", [P, QT, C]), r_.sb("xn", [P, QT, C])
        st6, st2 = r_.sb("st6", [P, QT, 6]), r_.sb("st2", [P, QT, 2])
        var, rstd, expo = r_.sb("var", [P, QT]), r_.sb("rstd", [P, QT]), r_.sb("expo", [P, QT])
        xH, xL = r_.sb("xH", [P, KC, T], F32R), r_.sb("xL", [P, KC, T], F32R)
        ctxr = r_.sb("ctxr", [P, TCE])
        ctxH, ctxL = r_.sb("ctxH", [P, TCE], F32R), r_.sb("ctxL", [P, TCE], F32R)
        qpart = r_.sb("qpart", [P, 3, KC, 2 * T], BF16)
        kpart = r_.sb("kpart", [P, 3, KC, NK], BF16)
        vbuf = r_.sb("vbuf", [P, NG, NKT, GC])
        NR = 7
        rem = r_.sb("rem", [P, NR, T])
        NBANK = 6
        acc = [r_.ps(f"acc{i}", [P, T]) for i in range(NBANK)]
        tps = [r_.ps(f"tps{c}", [P, T]) for c in range(KC)]

        s_w, s_wH, s_wL = r_.sem("w"), r_.sem("wH"), r_.sem("wL")
        s_x, s_c = r_.sem("x"), r_.sem("c")
        s_cst, s_ln, s_var, s_rstd, s_xn = (r_.sem(n) for n in ("cst", "ln", "var", "rstd", "xn"))
        s_T, s_xH, s_xL = r_.sem("T"), r_.sem("xH"), r_.sem("xL")
        s_ctxH, s_ctxL = r_.sem("ctxH"), r_.sem("ctxL")
        s_out, s_h, s_fin, s_m, s_l = (r_.sem(n) for n in ("out", "h", "fin", "m", "l"))
        s_wr = {n: r_.sem("wr_" + n) for n in ("q0", "q1", "k0", "k1", "c0", "c1", "v")}

        CH = [402, 400, 400, 400]
        outs = [("q", 0, 0, "q0"), ("q", 1, 0, "q0"), ("q", 0, 1, "q1"), ("q", 1, 1, "q1"),
                ("k", 2, 0, "k0"), ("k", 2, 1, "k1"), ("vs", 0), ("vs", 2)]
        NSELF = len(outs)
        for cg in range(KC):
            at = 0
            for n in CH:
                outs.append(("c", at, cg, f"c{cg}", n))
                at += n
        outs += [("vc", t) for t in range(0, CTXT, 2)]
        NO = len(outs)
        split = [k for k, o in enumerate(outs) if o[0] in "qkc"]
        rank = {k: j for j, k in enumerate(split)}
        NSP = len(split)
        assert NSP == 2 * NR

        def parts(o):
            if o[0] == "q":
                return qpart, o[2], o[1] * T, T, bcol[:, o[1], o[2]:o[2] + 1]
            if o[0] == "k":
                return kpart, o[2], 0, T, bcol[:, 2, o[2]:o[2] + 1]
            n = min(o[4], TC - o[1])
            return kpart, o[2], T + o[1], n, bcol[:, 3, o[2]:o[2] + 1]

        def writes(tag):
            return [k for k in split if outs[k][3] == tag]

        r_.prime({s_fin.name: NO})
        with nc.Block() as block:

            @block.sync
            def _(sp):
                sp.dma_start(xin[:, :, :], a["x"][0].rearrange("(t p) c -> p t c", p=P)).then_inc(s_x, 16)
                for n, w in enumerate(("Wq", "Wcq", "Wk", "Wv")):
                    sp.dma_start(wraw[:, n], a[w].rearrange("(k p) n -> p k n", p=P)).then_inc(s_w, 16)
                for n, w in enumerate(("Wck", "Wcv")):
                    sp.dma_start(craw[:, n], a[w]).then_inc(s_w, 16)
                sp.dma_start(bcol[:, :, :], a["bcol"]).then_inc(s_w, 16)
                for n, w in enumerate(("bv", "bcv")):
                    sp.dma_start(bvrow[:, n], a[w].rearrange("(o c) -> o c", o=1).to_broadcast([P, C])).then_inc(s_w, 16)
                sp.dma_start(ctxr[:, 0:TC], a["ctxT"][0]).then_inc(s_c, 16)

                def write(b, tag):
                    ks = writes(tag)
                    tile, cg, c0, _, _ = parts(outs[ks[0]])
                    n = sum(parts(outs[k])[3] for k in ks)
                    wait(sp, s_l, b * NSP + rank[ks[-1]] + 1)
                    for part in range(3):
                        dst = QS if tile is qpart else KS
                        row = dst[part].rearrange("(b r) c -> b r c", b=B)[bass.ds(b, 1), cg * P:(cg + 1) * P, c0:c0 + n]
                        sp.dma_start(row.rearrange("o r c -> (o r) c"), tile[:, part, cg, c0:c0 + n]).then_inc(s_wr[tag], 16)

                def body(b, more):
                    if more:
                        wait(sp, s_xn, QT * (b + 1))
                        sp.dma_start(xin[:, :, :], a["x"][bass.ds(b + 1, 1)].rearrange("o (t p) c -> p (o t) c", p=P)).then_inc(s_x, 16)
                        wait(sp, s_ctxL, b + 1)
                        wait(sp, s_ctxH, b + 1)
                        sp.dma_start(ctxr[:, 0:TC], a["ctxT"][bass.ds(b + 1, 1)].rearrange("o c t -> (o c) t")).then_inc(s_c, 16)
                    for tag in ("q0", "q1", "k0", "k1", "c0", "c1"):
                        write(b, tag)
                    wait(sp, s_fin, NO * (b + 2))
                    for g in range(NG):
                        dst = VS.rearrange("(b g) p t c -> b g p t c", b=B)[bass.ds(b, 1), g]
                        sp.dma_start(dst.rearrange("o p t c -> (o p) t c"), vbuf[:, g]).then_inc(s_wr["v"], 16)

                with sp.Fori(0, B - 1) as b:
                    body(b, True)
                body(B - 1, False)
                for tag, s in s_wr.items():
                    wait(sp, s, (64 if tag == "v" else 48) * B)

            @block.gpsimd
            def _(pool):
                pool.memset(expo[:, :], -0.5).then_inc(s_cst, 1)
                pool.memset(ctxr[:, TC:TCE], 0.0).then_inc(s_cst, 1)
                pool.memset(vbuf[:, :, NKT - 1, :], 0.0).then_inc(s_cst, 1)

                def power(n):
                    wait(pool, s_cst, 3)
                    wait(pool, s_var, n + 1)
                    pool.tensor_tensor(rstd[:, :], var[:, :], expo[:, :], ALU.pow).then_inc(s_rstd, 1)

                def body(b, more):
                    for j, k in enumerate(split):
                        if k == 3 and more:
                            power(b + 1)
                        tile, cg, c0, n, _ = parts(outs[k])
                        wait(pool, s_m, b * NSP + j + 1)
                        pool.tensor_tensor(tile[:, 2, cg, c0:c0 + n], rem[:, j % NR, 0:n], tile[:, 1, cg, c0:c0 + n],
                                           ALU.subtract).then_inc(s_l, 1)

                power(0)
                with pool.Fori(0, B - 1) as b:
                    body(b, True)
                body(B - 1, False)

            @block.vector
            def _(dve):
                wait(dve, s_cst, 3)
                wait(dve, s_wH, 6)
                for n in range(4):
                    dve.tensor_tensor(wL[:, n], wraw[:, n], wH[:, n].bitcast(F32), ALU.subtract).then_inc(s_wL, 1)
                for n in range(2):
                    dve.tensor_tensor(cL[:, n], craw[:, n], cH[:, n].bitcast(F32), ALU.subtract).then_inc(s_wL, 1)

                def layernorm(n):
                    wait(dve, s_x, 16 * (n + 1))
                    wait(dve, s_T, KC * n)
                    for t in range(QT):
                        dve.bn_stats(st6[:, t, :], xin[:, t, :]).then_inc(s_ln, 1)
                    wait(dve, s_ln, 2 * QT * n + QT)
                    r_.carrier(dve)
                    for t in range(QT):
                        dve.bn_aggr(st2[:, t, :], st6[:, t, :]).then_inc(s_ln, 1)
                    wait(dve, s_ln, 2 * QT * (n + 1))
                    dve.tensor_scalar(var[:, :], st2[:, :, 1], LN_EPS, None, ALU.add).then_inc(s_var, 1)
                    wait(dve, s_rstd, n + 1)
                    for t in range(QT):
                        dve.tensor_scalar(xn[:, t, :], xin[:, t, :], st2[:, t, 0:1], rstd[:, t:t + 1],
                                          ALU.subtract, ALU.mult).then_inc(s_xn, 1)

                def x_low(n):
                    for c in range(KC):
                        wait(dve, s_xH, KC * n + c + 1)
                        dve.tensor_tensor(xL[:, c, :], tps[c][:, :], xH[:, c, :].bitcast(F32), ALU.subtract).then_inc(s_xL, 1)

                def ctx_low(n):
                    wait(dve, s_ctxH, n + 1)
                    dve.tensor_tensor(ctxL[:, :], ctxr[:, :], ctxH[:, :].bitcast(F32), ALU.subtract).then_inc(s_ctxL, 1)

                def body(b, more):
                    for k, o in enumerate(outs):
                        bank = acc[k % NBANK]
                        if k == 3 and more:
                            layernorm(b + 1)
                        if k == NSELF + 1 and more:
                            x_low(b + 1)
                        if k in rank:
                            j = rank[k]
                            tile, cg, c0, n, bias = parts(o)
                            wait(dve, s_h, b * NSP + j + 1)
                            if j >= NR:
                                wait(dve, s_l, b * NSP + j - NR + 1)
                            else:
                                wait(dve, s_l, b * NSP)
                            dve.scalar_tensor_tensor(rem[:, j % NR, 0:n], bank[:, 0:n], bias, tile[:, 0, cg, c0:c0 + n],
                                                     ALU.add, ALU.subtract).then_inc(s_fin, 1)
                            continue
                        wait(dve, s_out, b * NO + k + 1)
                        if o == ("vs", 0):
                            wait(dve, s_wr["v"], 64 * b)
                        kind, t = o
                        row = 0 if kind == "vs" else 1
                        for i in range(2):
                            tt = t + i
                            if kind == "vc" and tt >= CTXT:
                                continue
                            rows = LASTK if kind == "vc" and tt == CTXT - 1 else P
                            slot = tt if kind == "vs" else QT + tt
                            ins = dve.tensor_tensor(vbuf[0:rows, :, slot, :],
                                                    bank[0:rows, i * C:(i + 1) * C].rearrange("p (g c) -> p g c", g=NG),
                                                    bvrow[0:rows, row, :].rearrange("p (g c) -> p g c", g=NG), ALU.add)
                        ins.then_inc(s_fin, 1)
                    if more:
                        ctx_low(b + 1)

                layernorm(0)
                x_low(0)
                ctx_low(0)
                with dve.Fori(0, B - 1) as b:
                    body(b, True)
                body(B - 1, False)

            @block.scalar
            def _(act):
                wait(act, s_w, 16 * 9)
                for n in range(4):
                    act.activation(wH[:, n], wraw[:, n], ACT.Copy).then_inc(s_wH, 1)
                for n in range(2):
                    act.activation(cH[:, n], craw[:, n], ACT.Copy).then_inc(s_wH, 1)

                def x_high(n):
                    wait(act, s_out, NO * n if isinstance(n, int) and n == 0 else NO * (n - 1) + NSELF)
                    for c in range(KC):
                        wait(act, s_T, KC * n + c + 1)
                        act.activation(xH[:, c, :], tps[c][:, :], ACT.Copy).then_inc(s_xH, 1)

                def ctx_high(n):
                    wait(act, s_c, 16 * (n + 1))
                    wait(act, s_cst, 3)
                    wait(act, s_out, NO * n)
                    act.activation(ctxH[:, :], ctxr[:, :], ACT.Copy).then_inc(s_ctxH, 1)

                def mid(b, k):
                    j = rank[k]
                    tile, cg, c0, n, _ = parts(outs[k])
                    wait(act, s_fin, NO * (b + 1) + k + 1)
                    act.activation(tile[:, 1, cg, c0:c0 + n], rem[:, j % NR, 0:n], ACT.Copy).then_inc(s_m, 1)

                def body(b, more):
                    seen, behind = set(), None
                    for k, o in enumerate(outs):
                        if k == NSELF:
                            mid(b, behind)
                            behind = None
                            if more:
                                x_high(b + 1)
                        if k not in rank:
                            continue
                        tile, cg, c0, n, bias = parts(o)
                        if o[3] not in seen:
                            wait(act, s_wr[o[3]], 48 * b)
                            seen.add(o[3])
                        wait(act, s_out, b * NO + k + 1)
                        act.activation(tile[:, 0, cg, c0:c0 + n], acc[k % NBANK][:, 0:n], ACT.Identity,
                                       bias=bias, scale=1.0).then_inc(s_h, 1)
                        if behind is not None:
                            mid(b, behind)
                        behind = k
                    mid(b, behind)
                    if more:
                        ctx_high(b + 1)

                x_high(0)
                ctx_high(0)
                with act.Fori(0, B - 1) as b:
                    body(b, True)
                body(B - 1, False)

            @block.tensor
            def _(pe):
                def transpose_x(n):
                    wait(pe, s_xn, QT * (n + 1))
                    wait(pe, s_xL, KC * n)
                    for c in range(KC):
                        for t in range(QT):
                            ins = pe.transpose(tps[c][:, t * P:(t + 1) * P], xn[:, t, c * P:(c + 1) * P], idf[:, :])
                        ins.then_inc(s_T, 1)

                def body(b, more):
                    for k, o in enumerate(outs):
                        if k == NSELF and more:
                            transpose_x(b + 1)
                        bank = acc[k % NBANK]
                        if k == 0:
                            wait(pe, s_xL, KC * (b + 1))
                        if k == NSELF:
                            wait(pe, s_ctxL, b + 1)
                        prev = k - NBANK if k >= NBANK else max(i for i in range(NO) if i % NBANK == k) - NO
                        wait(pe, s_fin, NO * (b + 1) + prev + 1)
                        if o[0] in "qk":
                            w, cg = o[1], o[2]
                            for c in range(KC):
                                cols = slice(cg * P, (cg + 1) * P)
                                ins = mm3(pe, bank[:, :], wH[:, w, c, cols], wL[:, w, c, cols], xH[:, c, :], xL[:, c, :],
                                          c == 0, c == KC - 1)
                        elif o[0] == "vs":
                            for i in range(2):
                                tok = slice((o[1] + i) * P, (o[1] + i + 1) * P)
                                for c in range(KC):
                                    ins = mm3(pe, bank[:, i * C:(i + 1) * C], xH[:, c, tok], xL[:, c, tok],
                                              wH[:, 3, c, :], wL[:, 3, c, :], c == 0, c == KC - 1)
                        elif o[0] == "c":
                            cols = slice(o[2] * P, (o[2] + 1) * P)
                            at, n = o[1], o[4]
                            ins = mm3(pe, bank[:, 0:n], cH[:, 0, cols], cL[:, 0, cols], ctxH[:, at:at + n],
                                      ctxL[:, at:at + n], True, True)
                        else:
                            for i in range(2):
                                tt = o[1] + i
                                if tt >= CTXT:
                                    continue
                                rows = LASTK if tt == CTXT - 1 else P
                                tok = slice(tt * P, tt * P + rows)
                                ins = mm3(pe, bank[0:rows, i * C:(i + 1) * C], ctxH[:, tok], ctxL[:, tok],
                                          cH[:, 1, :], cL[:, 1, :], True, True)
                        ins.then_inc(s_out, 1)

                wait(pe, s_wL, 6)
                transpose_x(0)
                with pe.Fori(0, B - 1) as b:
                    body(b, True)
                body(B - 1, False)


def stage_attend(nc, QS, KS, VS, YS, idf, idb, mq, mk):
    with ExitStack() as ctx:
        r_ = Res(nc, ctx, "at_")
        K = [r_.sb(f"K{u}", [SROWS, G, NK], BF16) for u in range(2)]
        Q = [r_.sb(f"Q{u}", [SROWS, 2, G, T], BF16) for u in range(2)]
        vraw = [r_.sb(f"vraw{u}", [P, NKT, GC]) for u in range(2)]
        V = [r_.sb(f"V{u}", [P, NKT, G, 2 * D]) for u in range(2)]
        Pt = [r_.sb(f"P{u}", [P, G, T]) for u in range(2)]
        part = r_.sb("part", [P, 2, G, QT, 2])
        mx = r_.sb("mx", [P, 2, G * QT])
        sh = [r_.sb(f"sh{k}", [G * QT, 3, P], BF16) for k in range(2)]
        rest = r_.sb("rest", [G * QT, 1, P])
        O = [r_.sb(f"O{k}", [P, T]) for k in range(2)]
        den = r_.sb("den", [P, 2, QT, G])
        yk = [r_.sb(f"y{k}", [P, QT, G, D]) for k in range(2)]
        ysum = [r_.sb(f"ysum{u}", [P, QT, GC]) for u in range(2)]
        NB = 3
        ST = [r_.ps(f"ST{i}", [P, T]) for i in range(NB)]
        R = [r_.ps(f"R{i}", [P, 2, T]) for i in range(2)]
        OP = r_.ps("OP", [P, T])

        s_ld = [[r_.sem(f"ld{k}{u}") for u in range(2)] for k in range(2)]
        s_vld = [r_.sem(f"vld{u}") for u in range(2)]
        (s_cst, s_v, s_st, s_ex, s_av, s_fill, s_drain, s_oe, s_ya, s_pm, s_sr, s_rc) = (
            r_.sem(n) for n in ("cst", "v", "st", "ex", "av", "fill", "drain", "oe", "ya", "pm", "sr", "rc"))
        s_y0 = r_.sem("y0")
        s_yst = [r_.sem(f"yst{u}") for u in range(2)]
        s_shD, s_shd = ([r_.sem(f"{n}{k}") for k in range(2)] for n in ("shD", "shd"))

        SELF, CROSS = 0, 1
        LAST = NKT - 1

        def key_tile(s):
            return QT + s if s < CTXT else s - CTXT

        def kind_of(s):
            return CROSS if s < CTXT else SELF

        XC = -(-TC // 4)
        XOFF = [[0, TC // 4], [2 * (TC // 4), TC - XC]]
        assert all(o1 - o0 <= XC for o0, o1 in XOFF) and XOFF[1][0] <= XOFF[0][1] + XC and XC <= T
        mtiles = [("x", h, q, half) for h in range(G) for q in range(QT) for half in range(2)]
        NMX = len(mtiles)
        mtiles += [("s", h, q) for h in range(G) for q in (0, 2)]
        NM = len(mtiles)
        NST = NKT * G

        def schedule():
            tail = {2: 1, 5: 1}
            nxt = {12: 1, 13: 1, 14: 1, 15: 1, 16: 2}
            last = 11
            mt, mn, upto = NM - sum(tail.values()), 0, 0
            assert sum(nxt.values()) == mt - NMX
            ev = []
            for s in range(NKT):
                ms = [("MAX", mt + k, 0) for k in range(tail.get(s, 0))]
                mt += len(ms)
                upto = (s + 1) * NMX // (last + 1) if s <= last else upto + nxt.get(s, 0)
                ms += [("MAX", m, 1) for m in range(mn, upto)]
                mn = upto
                n_st = (s + 1, 0) if s < LAST else (0, 1)
                st = [("ST", n_st[0], n_st[1], h) for h in range(G)]
                after_av = max(len(ms) - 2, 1)
                if s == LAST:
                    after_av = len(ms)
                before = ms[:len(ms) - after_av]
                ev += [st[0]] + before[:1] + [st[1], st[2]] + before[1:]
                if s == 12:
                    ev.append(("SHIFT", CROSS, 1))
                ev += [("AV", s, 0)] + ms[len(before):] + [st[3]]
                if s == 7:
                    ev.append(("SHIFT", SELF, 0))
                if s in (CTXT, LAST):
                    ev.append(("OUT", CROSS if s == CTXT else SELF, 0))
            assert mt == NM and mn == NM - sum(tail.values())
            return ev

        body_events = schedule()
        first_events = [e for e in body_events if e[0] in ("MAX", "SHIFT") and e[2] == 1]
        first_events += [("ST", 0, 1, h) for h in range(G)]
        last_events = [e for e in body_events if e[2] == 0]

        def slots(evs):
            return [e for e in evs if e[0] in ("MAX", "SHIFT", "OUT")]

        n_first, n_body = len(slots(first_events)), len(slots(body_events))
        assert n_body % 2 == 0

        def slot(i, evs, e):
            k = slots(evs).index(e) + (0 if evs is first_events else n_first)
            return (k if evs is first_events else n_body * i + k), R[k % 2]

        def loop(eng, body):
            body(-1, -1, 1, first_events)
            with eng.Fori(0, NI // 2 - 1) as it:
                for u in range(2):
                    body(2 * it + u, it, u, body_events)
            body(NI - 2, NI // 2 - 1, 0, body_events)
            body(NI - 1, NI // 2 - 1, 1, last_events)

        def st_cols(s):
            return 0 if s < CTXT else key_tile(s) * P

        def st_rows(s):
            return LASTK if s == CTXT - 1 else P

        r_.prime()
        with nc.Block() as block:

            @block.sync
            def _(sp):
                def load(kind, n, u):
                    cols = slice(T, NK) if kind == CROSS else slice(0, T)
                    for r in range(len(QPART)):
                        rows = slice(r * D, (r + 1) * D)
                        k = KS[KPART[r]].rearrange("(i h d) c -> i h d c", i=NI, h=G)[bass.ds(n, 1)]
                        sp.dma_start(K[u][rows, :, cols], k[:, :, :, cols].rearrange("o h d c -> (o d) h c")
                                     ).then_inc(s_ld[kind][u], 16)
                        q = QS[QPART[r]].rearrange("(i h d) (k c) -> i h d k c", i=NI, h=G, k=2)[bass.ds(n, 1)]
                        sp.dma_start(Q[u][rows, kind], q[:, :, :, kind].rearrange("o h d c -> (o d) h c")
                                     ).then_inc(s_ld[kind][u], 16)

                def load_values(n, u):
                    sp.dma_start(vraw[u][:, :, :], VS[bass.ds(n, 1)].rearrange("o p t c -> (o p) t c")).then_inc(s_vld[u], 16)

                def shift_rows(kind, n, u):
                    wait(sp, s_shD[kind], n + 1)
                    for p in range(3):
                        sp.dma_start(Q[u][KROWS + p:KROWS + p + 1, kind], sh[kind][:, p]).then_inc(s_shd[kind], 16)

                def store(n, u):
                    wait(sp, s_ya, n)
                    sp.dma_start(YS[bass.ds(n, 1)].rearrange("o p t c -> (o p) t c"), ysum[u][:, :, :]).then_inc(s_yst[u], 16)

                def body(i, it, u, evs):
                    if evs is first_events:
                        load(CROSS, 0, 0)
                        load(SELF, 0, 0)
                        load_values(0, 0)
                        load(CROSS, 1, 1)
                        shift_rows(CROSS, 0, 0)
                        wait(sp, s_y0, 1)
                        return
                    if evs is body_events:
                        wait(sp, s_st, NST * i)
                        r_.carrier(sp)
                        load(SELF, i + 1, 1 - u)
                        wait(sp, s_v, i)
                        load_values(i + 1, 1 - u)
                    store(i, 1 - u)
                    shift_rows(SELF, i, u)
                    if not isinstance(i, int):
                        wait(sp, s_st, NST * i + CTXT * G)
                        r_.carrier(sp)
                        load(CROSS, i + 2, u)
                    if evs is body_events:
                        shift_rows(CROSS, i + 1, 1 - u)

                loop(sp, body)
                store(NI, 1)
                wait(sp, s_yst[0], 16 * (NI // 2))
                wait(sp, s_yst[1], 16 * (NI // 2 + 1))

            @block.gpsimd
            def _(pool):
                for u in range(2):
                    pool.memset(V[u][:, :, :, D:2 * D], 1.0).then_inc(s_cst, 1)
                pool.memset(ysum[1][:, :, :], 0.0).then_inc(s_y0, 1)

                def body(i, it, u, evs):
                    if evs is not last_events:
                        nit = it if u == 0 else it + 1
                        wait(pool, s_vld[1 - u], 16 * (nit + 1))
                        if evs is body_events:
                            wait(pool, s_av, NKT * i)
                        r_.carrier(pool)
                        pool.tensor_copy(V[1 - u][:, :, :, 0:D],
                                         vraw[1 - u][:, :, :].rearrange("p t (h d) -> p t h d", h=G)).then_inc(s_v, 1)
                    if evs is first_events:
                        return
                    k, _ = slot(i, evs, ("OUT", SELF, 0))
                    wait(pool, s_drain, k + 1)
                    wait(pool, s_yst[u], 16 * (it + u))
                    pool.tensor_tensor(ysum[u][:, :, :].rearrange("p t c -> p (t c)"),
                                       yk[0][:, :, :, :].rearrange("p t h d -> p (t h d)"),
                                       yk[1][:, :, :, :].rearrange("p t h d -> p (t h d)"), ALU.add).then_inc(s_ya, 1)

                loop(pool, body)

            @block.vector
            def _(dve):
                for u in range(2):
                    dve.memset(K[u][KROWS:SROWS, :, :], 1.0).then_inc(s_cst, 1)

                def reduce_tile(m, k, buf, n):
                    tile = mtiles[m]
                    if tile[0] == "s":
                        _, h, q = tile
                        for j in range(2):
                            col = h * QT + q + j
                            ins = dve.tensor_reduce(mx[:, SELF, col:col + 1], buf[:, j, 0:(q + j + 1) * P], AX.X, ALU.max)
                    else:
                        _, h, q, half = tile
                        ins = dve.tensor_reduce(part[:, half, h, q, 0:1], buf[:, :, 0:XC], AX.XY, ALU.max)
                    ins.then_inc(s_drain, 1)
                    if m == NMX - 1:
                        wait(dve, s_drain, k + 1)
                        dve.tensor_tensor(mx[:, CROSS, :], part[:, 0, :, :, 0].rearrange("p h q -> p (h q)"),
                                          part[:, 1, :, :, 0].rearrange("p h q -> p (h q)"), ALU.max).then_inc(s_pm, 1)

                def shift_parts(kind, n, k, buf):
                    t, rem, out = buf[0:G * QT, 0, 0:P], rest[:, 0], sh[kind]
                    own = 2 * (2 * n + (1 if kind == SELF else 0))
                    wait(dve, s_shd[kind], 48 * n)
                    dve.tensor_scalar(out[:, 0], t, -1.0, None, ALU.mult).then_inc(s_sr, 1)
                    wait(dve, s_sr, own + 1)
                    dve.scalar_tensor_tensor(rem, t, -1.0, out[:, 0], ALU.mult, ALU.subtract).then_inc(s_drain, 1)
                    wait(dve, s_drain, k + 1)
                    dve.tensor_copy(out[:, 1], rem).then_inc(s_sr, 1)
                    wait(dve, s_sr, own + 2)
                    dve.tensor_tensor(out[:, 2], rem, out[:, 1], ALU.subtract).then_inc(s_shD[kind], 1)

                def output(kind, n, buf):
                    t = buf[:, 0, :].rearrange("p (q h e) -> p q h e", q=QT, h=G)
                    dve.reciprocal(den[:, kind], t[:, :, :, D]).then_inc(s_rc, 1)
                    wait(dve, s_rc, 2 * n + (2 if kind == SELF else 1))
                    wait(dve, s_ya, n)
                    dk = bcast(den[:, kind].rearrange("p q (h o) -> p (q h) o", o=1), D, 2)
                    dve.tensor_tensor(yk[kind][:, :, :, :].rearrange("p q h d -> p (q h) d"),
                                      t[:, :, :, 0:D].rearrange("p q h d -> p (q h) d"), dk, ALU.mult
                                      ).then_inc(s_drain, 1)

                def body(i, it, u, evs):
                    for e in slots(evs):
                        k, buf = slot(i, evs, e)
                        wait(dve, s_fill, k + 1)
                        if e[0] == "MAX":
                            reduce_tile(e[1], k, buf, i + e[2])
                        elif e[0] == "SHIFT":
                            shift_parts(e[1], i + e[2], k, buf)
                        else:
                            output(e[1], i, buf)

                loop(dve, body)

            @block.scalar
            def _(act):
                def exp(n, u, s, h, first):
                    rows, c0 = st_rows(s), st_cols(s)
                    wait(act, s_st, NST * n + s * G + h + 1)
                    if h == 0 and not first:
                        wait(act, s_av, NKT * n + s - 1)
                    act.activation(Pt[(s + u) % 2][0:rows, h, c0:T], ST[(s * G + h) % NB][0:rows, c0:T], ACT.Exp,
                                   scale=SCALE).then_inc(s_ex, 1)

                def body(i, it, u, evs):
                    for e in evs:
                        if e[0] == "ST":
                            exp(i + e[2], u if e[2] == 0 else 1 - u, e[1], e[3], evs is first_events)
                        elif e[0] == "AV" and e[1] in (CTXT - 1, LAST):
                            kind = kind_of(e[1])
                            wait(act, s_av, NKT * i + e[1] + 1)
                            act.activation(O[kind][:, :], OP[:, :], ACT.Copy).then_inc(s_oe, 1)

                loop(act, body)

            @block.tensor
            def _(pe):
                def max_tile(u, m, buf):
                    tile = mtiles[m]
                    if tile[0] == "s":
                        _, h, q = tile
                        for j in range(2):
                            w = (q + j + 1) * P
                            pe.matmul(buf[:, j, 0:w], Q[u][0:KROWS, SELF, h, (q + j) * P:w], K[u][0:KROWS, h, 0:w],
                                      start=True, stop=True)
                            ins = pe.matmul(buf[:, j, w - P:w], idb[:, :], mq[:, :], start=False, stop=True,
                                            skip_group_check=True)
                    else:
                        _, h, q, half = tile
                        for j in range(2):
                            at = T + XOFF[half][j]
                            ins = pe.matmul(buf[:, j, 0:XC], Q[u][0:KROWS, CROSS, h, q * P:(q + 1) * P],
                                            K[u][0:KROWS, h, at:at + XC], start=True, stop=True)
                    return ins

                def scores(n, u, s, h):
                    kind, t = kind_of(s), s * G + h
                    if h == 0 and s in (0, CTXT):
                        wait(pe, s_shd[kind], 48 * (n + 1))
                    if t >= NB:
                        wait(pe, s_ex, NST * n + t - NB + 1)
                    elif not isinstance(n, int) or n > 0:
                        wait(pe, s_ex, NST * (n - 1) + max(x for x in range(NST) if x % NB == t % NB) + 1)
                    rows, c0 = st_rows(s), st_cols(s)
                    keys = slice(key_tile(s) * P, key_tile(s) * P + rows)
                    out = ST[t % NB]
                    ins = pe.matmul(out[0:rows, c0:T], K[u][:, h, keys], Q[u][:, kind, h, c0:T], start=True,
                                    stop=True)
                    if kind == SELF:
                        ins = pe.matmul(out[:, c0:c0 + P], idb[:, :], mk[:, :], start=False, stop=True,
                                        skip_group_check=True)
                    ins.then_inc(s_st, 1)

                def values(i, u, s):
                    wait(pe, s_ex, NST * i + (s + 1) * G)
                    if s == 0:
                        wait(pe, s_v, i + 1)
                        wait(pe, s_oe, 2 * i)
                    if s == CTXT:
                        wait(pe, s_oe, 2 * i + 1)
                    rows, c0 = st_rows(s), st_cols(s)
                    for h in range(G):
                        ins = pe.matmul(OP[32 * h:32 * h + 2 * D, c0:T], V[u][0:rows, key_tile(s), h, :],
                                        Pt[(s + u) % 2][0:rows, h, c0:T],
                                        start=s in (0, CTXT), stop=s >= CTXT or s == CTXT - 1, skip_group_check=True)
                    ins.then_inc(s_av, 1)

                def body(i, it, u, evs):
                    for e in evs:
                        n, un = i + e[2], u if e[2] == 0 else 1 - u
                        if e[0] == "ST":
                            scores(n, un, e[1], e[3])
                            continue
                        if e[0] == "AV":
                            values(i, u, e[1])
                            continue
                        k, buf = slot(i, evs, e)
                        if evs is not first_events or k >= 2:
                            wait(pe, s_drain, k - 1)
                        if e[0] == "MAX":
                            if e[1:] in ((0, 1), (NMX, 1)):
                                nit = it if u == 0 else it + 1
                                wait(pe, s_ld[CROSS if e[1] == 0 else SELF][1 - u], 16 * 2 * len(QPART) * (nit + 1))
                            ins = max_tile(un, e[1], buf)
                        elif e[0] == "SHIFT":
                            if e[1] == SELF:
                                wait(pe, s_drain, slot(i, evs, ("MAX", NM - 1, 0))[0] + 1)
                            else:
                                wait(pe, s_pm, n + 1)
                            ins = pe.transpose(buf[0:G * QT, 0, 0:P], mx[:, e[1], :], idf[:, :])
                        else:
                            wait(pe, s_oe, 2 * n + (1 if e[1] == CROSS else 2))
                            for q in range(QT):
                                ins = pe.transpose(buf[:, 0, q * P:(q + 1) * P], O[e[1]][:, q * P:(q + 1) * P], idf[:, :])
                        ins.then_inc(s_fill, 1)

                wait(pe, s_cst, 4)
                loop(pe, body)


def stage_fold(nc, a, w):
    with ExitStack() as ctx:
        r_ = Res(nc, ctx, "fo_")
        NU = 2
        upT, up, wg, wd = ([r_.sb(f"{n}{u}", [P, KC, IW]) for u in range(NU)] for n in ("upT", "up", "wg", "wd"))
        bg = r_.sb("bg", [P, NX, KC])
        comb = [r_.ps(f"comb{u}", [P, KC, IW]) for u in range(NU)]
        bias = [r_.ps(f"bias{u}", [P, T]) for u in range(NU)]
        s_b, s_H, s_L, s_c, s_cH, s_cL, s_bi, s_bo = (r_.sem(n) for n in ("b", "H", "L", "c", "cH", "cL", "bi", "bo"))
        s_ld = [r_.sem(f"ld{u}") for u in range(NU)]
        NIT = NX // NU

        r_.prime()
        with nc.Block() as block:

            @block.sync
            def _(sp):
                sp.dma_start(bg[:, :, :], a["bg"]).then_inc(s_b, 16)
                sp.dma_start(w["bu"][:, :, :], a["bup"]).then_inc(s_b, 16)
                sp.dma_start(w["bd"][:, :], a["bd"]).then_inc(s_b, 16)
                wait(sp, s_b, 48)
                with sp.Fori(0, NIT) as it:
                    for u in range(NU):
                        e = NU * it + u
                        wait(sp, s_L, 2 * NU * it)
                        r_.carrier(sp)
                        wait(sp, s_bi, NU * it)
                        r_.carrier(sp)
                        for dst, src in ((upT, "WupT"), (up, "Wup"), (wg, "Wg"), (wd, "Wd")):
                            sp.dma_start(dst[u][:, :, :], a[src][bass.ds(e, 1)].rearrange("o (k p) n -> p (o k) n", p=P)
                                         ).then_inc(s_ld[u], 16)

            @block.scalar
            def _(act):
                with act.Fori(0, NIT) as it:
                    for u in range(NU):
                        e = NU * it + u
                        wait(act, s_ld[u], 64 * (it + 1))
                        for raw, h in ((up, "uH"), (wd, "dH")):
                            act.activation(w[h][:, bass.ds(e, 1)].rearrange("p o k n -> p (o k) n"), raw[u][:, :, :],
                                           ACT.Copy).then_inc(s_H, 1)
                        wait(act, s_c, e + 1)
                        act.activation(w["cH"][:, bass.ds(e, 1)].rearrange("p o k n -> p (o k) n"), comb[u][:, :, :],
                                       ACT.Copy).then_inc(s_cH, 1)

            @block.vector
            def _(dve):
                def low(dst, src, high, e):
                    v = lambda t: t[:, bass.ds(e, 1)].rearrange("p o k n -> p (o k n)")
                    return dve.tensor_tensor(v(w[dst]), src.rearrange("p k n -> p (k n)"), v(w[high]).bitcast(F32),
                                             ALU.subtract)

                wait(dve, s_b, 48)
                with dve.Fori(0, NIT) as it:
                    for u in range(NU):
                        e = NU * it + u
                        wait(dve, s_H, 2 * e + 2)
                        low("uL", up[u][:, :, :], "uH", e).then_inc(s_L, 1)
                        low("dL", wd[u][:, :, :], "dH", e).then_inc(s_L, 1)
                        wait(dve, s_cH, e + 1)
                        low("cL", comb[u][:, :, :], "cH", e).then_inc(s_cL, 1)
                        wait(dve, s_bi, e + 1)
                        dve.tensor_tensor(w["bc"][:, bass.ds(e, 1)].rearrange("p o k -> p (o k)"), bias[u][:, 0:KC],
                                          bg[:, bass.ds(e, 1)].rearrange("p o k -> p (o k)"), ALU.add).then_inc(s_bo, 1)

            @block.tensor
            def _(pe):
                wait(pe, s_b, 48)
                with pe.Fori(0, NIT) as it:
                    for u in range(NU):
                        e = NU * it + u
                        wait(pe, s_ld[u], 64 * (it + 1))
                        wait(pe, s_bo, NU * it)
                        for m in range(KC):
                            for k in range(KC):
                                ins = pe.matmul(comb[u][:, m, :], upT[u][:, k, m * P:(m + 1) * P], wg[u][:, k, :],
                                                start=k == 0, stop=k == KC - 1)
                        ins.then_inc(s_c, 1)
                        for m in range(KC):
                            for k in range(KC):
                                ins = pe.matmul(bias[u][:, m:m + 1], wg[u][:, k, m * P:(m + 1) * P],
                                                w["bu"][:, bass.ds(e, 1), k],
                                                start=k == 0, stop=k == KC - 1)
                        ins.then_inc(s_bi, 1)


def stage_mix(nc, a, YS, X1S, FS, tg, idf):
    with ExitStack() as ctx:
        r_ = Res(nc, ctx, "mx_")
        wraw, wH, wL = r_.sb("wraw", [P, KC, C]), r_.sb("wH", [P, KC, C], F32R), r_.sb("wL", [P, KC, C], F32R)
        bp = r_.sb("bp", [P, QT, C])
        NU = 2
        y, x, x1, xf = ([r_.sb(f"{n}{u}", [P, QT, C]) for u in range(NU)] for n in ("y", "x", "x1", "xf"))
        yH, yL = ([r_.sb(f"{n}{u}", [P, KC, T], F32R) for u in range(NU)] for n in ("yH", "yL"))
        st6, st2 = ([r_.sb(f"{n}{u}", [P, QT, m]) for u in range(NU)] for n, m in (("st6", 6), ("st2", 2)))
        var, rstd = ([r_.sb(f"{n}{u}", [P, QT]) for u in range(NU)] for n in ("var", "rstd"))
        expo = r_.sb("expo", [P, QT])
        tp = [r_.ps(f"tp{c}", [P, T]) for c in range(KC)]
        op = [[r_.ps(f"op{u}{i}", [P, 2, C]) for i in range(2)] for u in range(NU)]
        s_w, s_wH, s_wL, s_bp, s_xb, s_T, s_yH, s_yL, s_op, s_x1, s_st, s_ln, s_rs, s_xf, s_e = (
            r_.sem(n) for n in ("w", "wH", "wL", "bp", "xb", "T", "yH", "yL", "op", "x1", "st", "ln", "rs", "xf", "e"))
        s_ld, s_so = ([r_.sem(f"{n}{u}") for u in range(NU)] for n in ("ld", "so"))
        NIT = B // NU

        r_.prime()
        with nc.Block() as block:

            @block.sync
            def _(sp):
                sp.dma_start(wraw[:, :, :], a["Wp"].rearrange("(k p) n -> p k n", p=P)).then_inc(s_w, 16)
                for t in range(QT):
                    sp.dma_start(bp[:, t], a["bp"].rearrange("(o c) -> o c", o=1).to_broadcast([P, C])).then_inc(s_w, 16)
                with sp.Fori(0, NIT) as it:
                    for u in range(NU):
                        b = NU * it + u
                        wait(sp, s_T, KC * NU * it)
                        wait(sp, s_x1, QT // 2 * NU * it)
                        for g in range(NG):
                            sp.dma_start(y[u][:, :, g * GC:(g + 1) * GC],
                                         YS[bass.ds(NG * b + g + 1, 1)].rearrange("o p t c -> (o p) t c")).then_inc(s_ld[u], 16)
                        sp.dma_start(x[u][:, :, :], a["x"][bass.ds(b, 1)].rearrange("o (t p) c -> p (o t) c", p=P)
                                     ).then_inc(s_ld[u], 16)

            @block.gpsimd
            def _(pool):
                pool.memset(expo[:, :], -0.5).then_inc(s_e, 1)
                wait(pool, s_e, 1)
                wait(pool, s_bp, QT)
                with pool.Fori(0, NIT) as it:
                    for u in range(NU):
                        b = NU * it + u
                        wait(pool, s_ld[u], 16 * (NG + 1) * (it + 1))
                        pool.tensor_tensor(x[u][:, :, :], x[u][:, :, :], bp[:, :, :], ALU.add).then_inc(s_xb, 1)
                    for u in range(NU):
                        b = NU * it + u
                        wait(pool, s_ln, 2 * (b + 1))
                        pool.tensor_tensor(rstd[u][:, :], var[u][:, :], expo[:, :], ALU.pow).then_inc(s_rs, 1)

            @block.scalar
            def _(act):
                wait(act, s_w, 16 * (1 + QT))
                act.activation(wH[:, :, :], wraw[:, :, :], ACT.Copy).then_inc(s_wH, 1)
                for t in range(QT):
                    act.activation(bp[:, t], bp[:, t], ACT.Copy, scale=tg[:, 0:1]).then_inc(s_bp, 1)
                with act.Fori(0, NIT) as it:
                    for u in range(NU):
                        b = NU * it + u
                        wait(act, s_op, 2 * NU * it)
                        for c in range(KC):
                            wait(act, s_T, KC * b + c + 1)
                            act.activation(yH[u][:, c, :], tp[c][:, :], ACT.Copy).then_inc(s_yH, 1)
                    for u in range(NU):
                        b = NU * it + u
                        wait(act, s_x1, QT // 2 * (b + 1))
                        act.dma_start(X1S[bass.ds(b, 1)].rearrange("o p t c -> (o p) t c"), x1[u][:, :, :]).then_inc(s_so[u], 16)
                        wait(act, s_xf, QT * (b + 1))
                        act.dma_start(FS[bass.ds(b, 1)].rearrange("o p t c -> (o p) t c"), xf[u][:, :, :]).then_inc(s_so[u], 16)
                for u in range(NU):
                    wait(act, s_so[u], 32 * NIT)

            @block.vector
            def _(dve):
                wait(dve, s_wH, 1)
                dve.tensor_tensor(wL[:, :, :], wraw[:, :, :], wH[:, :, :].bitcast(F32), ALU.subtract).then_inc(s_wL, 1)
                with dve.Fori(0, NIT) as it:
                    for u in range(NU):
                        b = NU * it + u
                        for c in range(KC):
                            wait(dve, s_yH, KC * b + c + 1)
                            dve.tensor_tensor(yL[u][:, c, :], tp[c][:, :], yH[u][:, c, :].bitcast(F32), ALU.subtract
                                              ).then_inc(s_yL, 1)
                    for u in range(NU):
                        b = NU * it + u
                        wait(dve, s_xb, b + 1)
                        wait(dve, s_so[u], 32 * it)
                        for i in range(QT // 2):
                            wait(dve, s_op, 2 * b + i + 1)
                            dve.scalar_tensor_tensor(x1[u][:, 2 * i:2 * i + 2, :].rearrange("p t c -> p (t c)"),
                                                     op[u][i][:, :, :].rearrange("p t c -> p (t c)"), tg[:, 0:1],
                                                     x[u][:, 2 * i:2 * i + 2, :].rearrange("p t c -> p (t c)"),
                                                     ALU.mult, ALU.add).then_inc(s_x1, 1)
                        wait(dve, s_x1, QT // 2 * (b + 1))
                        for t in range(QT):
                            ins = dve.bn_stats(st6[u][:, t, :], x1[u][:, t, :])
                        ins.then_inc(s_st, 1)
                        wait(dve, s_st, b + 1)
                        r_.carrier(dve)
                        for t in range(QT):
                            ins = dve.bn_aggr(st2[u][:, t, :], st6[u][:, t, :])
                        ins.then_inc(s_ln, 1)
                        wait(dve, s_ln, 2 * b + 1)
                        dve.tensor_scalar(var[u][:, :], st2[u][:, :, 1], LN_EPS, None, ALU.add).then_inc(s_ln, 1)
                    for u in range(NU):
                        b = NU * it + u
                        wait(dve, s_rs, b + 1)
                        for t in range(QT):
                            dve.tensor_scalar(xf[u][:, t, :], x1[u][:, t, :], st2[u][:, t, 0:1], rstd[u][:, t:t + 1],
                                              ALU.subtract, ALU.mult).then_inc(s_xf, 1)

            @block.tensor
            def _(pe):
                wait(pe, s_wL, 1)
                with pe.Fori(0, NIT) as it:
                    for u in range(NU):
                        b = NU * it + u
                        wait(pe, s_ld[u], 16 * (NG + 1) * (it + 1))
                        wait(pe, s_yL, KC * b)
                        for c in range(KC):
                            for t in range(QT):
                                ins = pe.transpose(tp[c][:, t * P:(t + 1) * P], y[u][:, t, c * P:(c + 1) * P], idf[:, :])
                            ins.then_inc(s_T, 1)
                    for u in range(NU):
                        b = NU * it + u
                        wait(pe, s_yL, KC * (b + 1))
                        wait(pe, s_x1, QT // 2 * NU * it)
                        for t in range(QT):
                            tok = slice(t * P, (t + 1) * P)
                            for c in range(KC):
                                ins = mm3(pe, op[u][t // 2][:, t % 2, :], yH[u][:, c, tok], yL[u][:, c, tok],
                                          wH[:, c, :], wL[:, c, :], c == 0, c == KC - 1)
                            if t % 2:
                                ins.then_inc(s_op, 1)


def stage_experts(nc, a, FS, w, idf):
    with ExitStack() as ctx:
        r_ = Res(nc, ctx, "ex_")
        rraw = r_.sb("rraw", [P, NL, KC, NE])
        rw = r_.sb("rw", [P, NL, KC, 2 * NE], F32R)
        rb, gb = r_.sb("rb", [P, NL, QT, NE]), r_.sb("gb", [P, NL, QT, NE])
        nw = r_.sb("nw", [P, NL, C])
        prio, expo = r_.sb("prio", [P, QT, NE]), r_.sb("expo", [P, QT])
        xs = [r_.sb(f"xs{u}", [P, QT, C]) for u in range(2)]
        xH, xL = ([r_.sb(f"{n}{u}", [P, KC, T], F32R) for u in range(2)] for n in ("xH", "xL"))
        sg = [r_.sb(f"sg{c}", [P, T]) for c in range(KC)]
        af = [[r_.sb(f"af{u}{c}", [P, T]) for c in range(KC)] for u in range(2)]
        RA = 4
        aH, aL = ([[r_.sb(f"{n}{i}{c}", [P, T], F32R) for c in range(KC)] for i in range(RA)] for n in ("aH", "aL"))
        wt = [r_.sb(f"wt{u}", [P, QT, NE + 1]) for u in range(2)]
        wT = r_.sb("wT", [NE + 1, T])
        Z = [r_.sb(f"Z{u}", [P, QT, C]) for u in range(2)]
        sq = r_.sb("sq", [P, QT, C])
        ss, ms, rr = ([r_.sb(f"{n}{u}", [P, QT]) for u in range(2)] for n in ("ss", "ms", "rr"))
        sm = {n: r_.sb("g_" + n, [P, QT, NE]) for n in ("gt", "bi", "eq", "s1", "s2", "tmp")}
        s4 = {n: r_.sb("g4_" + n, [P, QT, 1]) for n in ("m", "v1", "v2", "d", "th", "w1", "w2")}
        GH = [r_.ps(f"GH{i}", [P, T]) for i in range(4)]
        Dn = [r_.ps(f"D{i}", [P, 2, C]) for i in range(2)]
        XT, RB = r_.ps("XT", [P, T]), r_.ps("RB", [P, T])

        (s_c, s_pool, s_rw, s_T, s_xH, s_xL, s_G, s_gate, s_d, s_th, s_WT, s_wT, s_up, s_sg, s_a, s_aH, s_aL, s_dn, s_z,
         s_ss, s_ms, s_rr, s_y, s_rwH, s_wt, s_nrm) = (
            r_.sem(n) for n in ("c", "pool", "rw", "T", "xH", "xL", "G", "gate", "d", "th", "WT", "wT", "up", "sg", "a",
                                "aH", "aL", "dn", "z", "ss", "ms", "rr", "y", "rwH", "wt", "nrm"))
        s_sum = r_.sem("sum")
        s_ld, s_st = ([r_.sem(f"{n}{u}") for u in range(2)] for n in ("ld", "st"))

        NM = NL * B
        ORDER = [NE + i for i in range(NS)] + list(range(NE))
        NDN = NX - NS + 1
        NDB = 2 * NDN
        LAST = NX - 1
        assert NX == 8 and NS == 2 and RA == 4
        REST = [("U", 1), ("tSq",), ("WT",), ("U", 2), ("tMs",), ("D", 1), ("U", 3), ("tNorm",), ("D", 2), ("tSt",),
                ("nT", 0), ("U", 4), ("D", 3), ("nT", 1), ("U", 5), ("D", 4), ("nR",), ("U", 6), ("nTh",), ("D", 5),
                ("U", 7), ("nGate",), ("D", 6), ("nU",), ("D", 7)]
        HEAD = [("nT", 0), ("nT", 1), ("nR",), ("nTh",), ("nGate",), ("nU",)]
        TAILS = [("tSq",), ("tMs",), ("tNorm",), ("tSt",)]

        def run(eng, do):
            def unit(m, h, u, prev, nxt):
                hp, hn = (h - 1 if u == 0 else h), (h if u == 0 else h + 1)
                for e in REST:
                    if e[0][0] == "n":
                        if nxt:
                            do(e, m + 1, 1 - u, hn)
                    elif e[0][0] == "t":
                        if prev:
                            do(e, m - 1, 1 - u, hp)
                    else:
                        do(e, m, u, h)

            for e in HEAD:
                do(e, 0, 0, 0)
            unit(0, 0, 0, False, True)
            with eng.Fori(0, NM // 2 - 1) as it:
                unit(2 * it + 1, it, 1, True, True)
                unit(2 * it + 2, it + 1, 0, True, True)
            unit(NM - 1, NM // 2 - 1, 1, True, False)
            for e in TAILS:
                do(e, NM - 1, 1, NM // 2 - 1)

        def freed_by(m, x):
            if x > RA:
                return NDB * (m + 1) + 2 * (x - RA)
            return NDB * m + 2 * (x + RA if x + RA < NX else x)

        def split(m, x):
            return 2 * (NDN * m + x - 1)

        r_.prime({s_aL.name: 4, s_a.name: 2, s_z.name: 2, s_sg.name: 2, s_dn.name: NDB})
        with nc.Block() as block:

            @block.sync
            def _(sp):
                sp.dma_start(rraw[:, :, :, :], a["router_W"]).then_inc(s_c, 16)
                for dst, src in ((rb, "router_b"), (gb, "gate_bias")):
                    for j in range(NL):
                        for t in range(QT):
                            sp.dma_start(dst[:, j, t], a[src][j:j + 1, :].to_broadcast([P, NE])).then_inc(s_c, 16)
                for j in range(NL):
                    sp.dma_start(nw[:, j], a["norm_w"][j:j + 1, :].to_broadcast([P, C])).then_inc(s_c, 16)

                def load(m, u):
                    sp.dma_start(xs[u][:, :, :], FS[bass.ds(m % B, 1)].rearrange("o p t c -> (o p) t c")).then_inc(s_ld[u], 16)

                for m in range(2):
                    load(m, m)
                with sp.Fori(1, B // 2) as h:
                    for u in range(2):
                        m = 2 * h + u
                        wait(sp, s_z, 2 + NDB * (m - 2) + 2)
                        load(m, u)
                with sp.Fori(B // 2, NM // 2) as h:
                    for u in range(2):
                        m = 2 * h + u
                        wait(sp, s_z, 2 + NDB * (m - 2) + 2)
                        wait(sp, s_st[u], 16 * (h - B // 2 + 1))
                        load(m, u)
                for u in range(2):
                    wait(sp, s_st[u], 16 * (NM // 2))

            @block.gpsimd
            def _(pool):
                pool.memset(expo[:, :], -0.5).then_inc(s_pool, 1)
                for e in range(NE):
                    pool.memset(prio[:, :, e:e + 1], float(NE - e)).then_inc(s_pool, 1)
                for u in range(2):
                    pool.memset(wt[u][:, :, NE:NE + 1], float(NS)).then_inc(s_pool, 1)
                wait(pool, s_pool, 1)

                def do(e, m, u, h):
                    if e[0] in ("U", "nU"):
                        x = e[1] if e[0] == "U" else 0
                        for c in range(KC if x else 0):
                            wait(pool, s_aH, split(m, x) + c + 1)
                            pool.tensor_tensor(aL[x % RA][c][:, :], af[x % 2][c][:, :],
                                               aH[x % RA][c][:, :].bitcast(F32), ALU.subtract).then_inc(s_aL, 1)
                    elif e[0] == "tMs":
                        wait(pool, s_ms, m + 1)
                        pool.tensor_tensor(rr[u][:, :], ms[u][:, :], expo[:, :], ALU.pow).then_inc(s_rr, 1)

                run(pool, do)

            @block.vector
            def _(dve):
                wait(dve, s_c, 16 * (1 + 2 * NL * QT + NL))
                wait(dve, s_rwH, 1)
                dve.tensor_tensor(rw[:, :, :, NE:2 * NE], rraw[:, :, :, :], rw[:, :, :, 0:NE].bitcast(F32), ALU.subtract
                                  ).then_inc(s_rw, 1)
                wait(dve, s_pool, NE + 3)
                GN = 18

                def wide(t):
                    return t[:, :, :].to_broadcast([P, QT, NE])

                def router_choice(m):
                    k = [0]

                    def link(ins):
                        k[0] += 1
                        ins.then_inc(s_gate, 1)
                        wait(dve, s_gate, GN * m + k[0])

                    gt, bi, eq, tmp = (sm[n][:, :, :] for n in ("gt", "bi", "eq", "tmp"))
                    j = m // B
                    lay = lambda t: t[:, bass.ds(j, 1)].rearrange("p o t e -> p (o t) e")
                    logits = RB[:, 0:QT * 2 * NE].rearrange("p (t e) -> p t e", t=QT)
                    wait(dve, s_G, m + 1)
                    wait(dve, s_WT, m)
                    link(dve.tensor_tensor(tmp, logits[:, :, 0:NE], lay(rb), ALU.add))
                    link(dve.tensor_tensor(gt, logits[:, :, NE:2 * NE], tmp, ALU.add))
                    link(dve.tensor_tensor(bi, gt, lay(gb), ALU.add))
                    for n, v in (("s1", "v1"), ("s2", "v2")):
                        s = sm[n][:, :, :]
                        link(dve.tensor_reduce(s4["m"][:, :, :], bi, AX.X, ALU.max))
                        link(dve.tensor_tensor(eq, bi, wide(s4["m"]), ALU.is_ge))
                        link(dve.tensor_tensor(eq, eq, prio[:, :, :], ALU.mult))
                        link(dve.tensor_reduce(s4["m"][:, :, :], eq, AX.X, ALU.max))
                        link(dve.tensor_tensor(s, eq, wide(s4["m"]), ALU.is_equal))
                        link(dve.tensor_tensor(tmp, s, gt, ALU.mult))
                        link(dve.tensor_reduce(s4[v][:, :, :], tmp, AX.X, ALU.add))
                        if n == "s1":
                            link(dve.scalar_tensor_tensor(bi, s, NEG, bi, ALU.mult, ALU.add))
                    assert k[0] == GN
                    dve.tensor_tensor(s4["d"][:, :, :], s4["v1"][:, :, :], s4["v2"][:, :, :], ALU.subtract).then_inc(s_d, 1)

                def router_weights(m, u):
                    w1, w2, th = (s4[n][:, :, :] for n in ("w1", "w2", "th"))
                    s1, s2 = sm["s1"][:, :, :], sm["s2"][:, :, :]
                    wait(dve, s_th, m + 1)
                    dve.tensor_scalar(w1, th, 0.5, 0.5, ALU.mult, ALU.add).then_inc(s_y, 1)
                    dve.tensor_scalar(w2, th, -0.5, 0.5, ALU.mult, ALU.add).then_inc(s_y, 1)
                    wait(dve, s_y, 4 * m + 2)
                    dve.tensor_tensor(s1, s1, wide(s4["w1"]), ALU.mult).then_inc(s_y, 1)
                    dve.tensor_tensor(s2, s2, wide(s4["w2"]), ALU.mult).then_inc(s_y, 1)
                    wait(dve, s_y, 4 * m + 4)
                    dve.tensor_tensor(wt[u][:, :, 0:NE], s1, s2, ALU.add).then_inc(s_wt, 1)

                def do(e, m, u, h):
                    if e[0] == "nT":
                        c = e[1]
                        wait(dve, s_xH, KC * m + c + 1)
                        dve.tensor_tensor(xL[u][:, c, :], XT[:, :], xH[u][:, c, :].bitcast(F32), ALU.subtract).then_inc(s_xL, 1)
                    elif e[0] == "nR":
                        router_choice(m)
                    elif e[0] == "nGate":
                        router_weights(m, u)
                    elif e[0] == "WT":
                        wait(dve, s_WT, m + 1)
                        wait(dve, s_dn, NDB * m + 2)
                        dve.tensor_copy(wT[:, :], RB[0:NE + 1, :]).then_inc(s_wT, 1)
                    elif e[0] in ("U", "nU"):
                        x = e[1] if e[0] == "U" else 0
                        for c in range(KC):
                            n = NX * m + x
                            wait(dve, s_up, 4 * n + 2 * c + 2)
                            wait(dve, s_sg, 2 + 2 * n + c + 1)
                            if x != 2:
                                wait(dve, s_aL, 2 * NDN * m + 2 * (x if x < 2 else x - 1) + c + 1)
                            dve.scalar_tensor_tensor(af[x % 2][c][:, :], GH[2 * c + 1][:, :], w["bu"][:, ORDER[x], c:c + 1],
                                                     sg[c][:, :], ALU.add, ALU.mult).then_inc(s_a, 1)
                        if x == 1:
                            for c in range(KC):
                                wait(dve, s_a, 2 + 2 * n + c + 1)
                                dve.tensor_tensor(af[1][c][:, :], af[1][c][:, :], af[0][c][:, :], ALU.add).then_inc(s_sum, 1)
                    elif e[0] == "D":
                        d = e[1] - 1
                        for k in range(2):
                            wait(dve, s_dn, NDB * (m + 1) + 2 * d + k + 1)
                            if d == 0:
                                if k == 0:
                                    wait(dve, s_st[u], 16 * h)
                                ins = dve.tensor_tensor(Z[u][:, 2 * k:2 * k + 2, :], Dn[k][:, :, :],
                                                        xs[u][:, 2 * k:2 * k + 2, :], ALU.add)
                            else:
                                wait(dve, s_z, NDB * m + 2 * d + k + 1)
                                for t in (2 * k, 2 * k + 1):
                                    ex = ORDER[e[1]]
                                    ins = dve.scalar_tensor_tensor(Z[u][:, t, :], Dn[k][:, t % 2, :], wt[u][:, t, ex:ex + 1],
                                                                   Z[u][:, t, :], ALU.mult, ALU.add)
                            ins.then_inc(s_z, 1)
                    elif e[0] == "tMs":
                        wait(dve, s_ss, m + 1)
                        dve.tensor_scalar(ms[u][:, :], ss[u][:, :], 1.0 / C, RMS_EPS, ALU.mult, ALU.add).then_inc(s_ms, 1)
                    elif e[0] == "tNorm":
                        wait(dve, s_rr, m + 1)
                        for t in range(QT):
                            ins = dve.scalar_tensor_tensor(
                                Z[u][:, t, :], Z[u][:, t, :], rr[u][:, t:t + 1],
                                nw[:, bass.ds(m // B, 1), :].rearrange("p o c -> p (o c)"), ALU.mult, ALU.mult)
                        ins.then_inc(s_nrm, 1)

                run(dve, do)

            @block.scalar
            def _(act):
                wait(act, s_c, 16 * (1 + 2 * NL * QT + NL))
                act.activation(rw[:, :, :, 0:NE], rraw[:, :, :, :], ACT.Copy).then_inc(s_rwH, 1)

                def do(e, m, u, h):
                    if e[0] == "nT":
                        c = e[1]
                        wait(act, s_T, KC * m + c + 1)
                        act.activation(xH[u][:, c, :], XT[:, :], ACT.Copy).then_inc(s_xH, 1)
                    elif e[0] == "nTh":
                        wait(act, s_d, m + 1)
                        act.activation(s4["th"][:, :, :], s4["d"][:, :, :], ACT.Tanh, scale=0.5).then_inc(s_th, 1)
                    elif e[0] in ("U", "nU"):
                        x = e[1] if e[0] == "U" else 0
                        n = NX * m + x
                        for c in range(KC):
                            wait(act, s_up, 4 * n + 2 * c + 1)
                            wait(act, s_a, 2 * n + c + 1)
                            act.activation(sg[c][:, :], GH[2 * c][:, :], ACT.Silu, bias=w["bc"][:, ORDER[x], c:c + 1],
                                           scale=1.0).then_inc(s_sg, 1)
                        if x == 0:
                            return
                        wait(act, s_dn, freed_by(m, x))
                        for c in range(KC):
                            if x == 1:
                                wait(act, s_sum, 2 * m + c + 1)
                            else:
                                wait(act, s_a, 2 + 2 * n + c + 1)
                            act.activation(aH[x % RA][c][:, :], af[x % 2][c][:, :], ACT.Copy).then_inc(s_aH, 1)
                    elif e[0] == "tSq":
                        wait(act, s_z, 2 + NDB * (m + 1))
                        for t in range(QT):
                            ins = act.activation(sq[:, t, :], Z[u][:, t, :], ACT.Square, accum_out=ss[u][:, t:t + 1])
                        ins.then_inc(s_ss, 1)
                    elif e[0] == "tSt":
                        wait(act, s_nrm, m + 1)
                        act.dma_start(FS[bass.ds(m % B, 1)].rearrange("o p t c -> (o p) t c"), Z[u][:, :, :]
                                      ).then_inc(s_st[u], 16)

                run(act, do)

            @block.tensor
            def _(pe):
                wait(pe, s_rw, 1)

                def up(m, x):
                    e, n = ORDER[x], NX * m + x
                    u = UP[0]
                    for c in range(KC):
                        cols = slice(c * P, (c + 1) * P)
                        for i, (wh, wl) in enumerate(((w["cH"], w["cL"]), (w["uH"], w["uL"]))):
                            wait(pe, (s_sg, s_a)[i], 2 * n + c + 1)
                            for k in range(KC):
                                ins = mm3(pe, GH[2 * c + i][:, :], wh[:, e, k, cols], wl[:, e, k, cols], xH[u][:, k, :],
                                          xL[u][:, k, :], k == 0, k == KC - 1)
                            ins.then_inc(s_up, 1)

                UP = [0]

                def do(e, m, u, h):
                    if e[0] == "nT":
                        c = e[1]
                        if c == 0:
                            wait(pe, s_ld[u], 16 * (h + 1))
                        wait(pe, s_xL, KC * m + c)
                        for t in range(QT):
                            ins = pe.transpose(XT[:, t * P:(t + 1) * P], xs[u][:, t, c * P:(c + 1) * P], idf[:, :])
                        ins.then_inc(s_T, 1)
                    elif e[0] == "nR":
                        wait(pe, s_xL, KC * (m + 1))
                        wait(pe, s_wT, m)
                        for t in range(QT):
                            tok = slice(t * P, (t + 1) * P)
                            for k in range(KC):
                                for i, x in enumerate((xL, xH)):
                                    ins = pe.matmul(RB[:, t * 2 * NE:(t + 1) * 2 * NE], x[u][:, k, tok],
                                                    rw[:, bass.ds(m // B, 1), k, :].rearrange("p o e -> p (o e)"),
                                                    start=k == 0 and i == 0, stop=k == KC - 1 and i == 1)
                        ins.then_inc(s_G, 1)
                    elif e[0] in ("U", "nU"):
                        UP[0] = u
                        up(m, e[1] if e[0] == "U" else 0)
                    elif e[0] == "WT":
                        wait(pe, s_wt, m + 1)
                        for t in range(QT):
                            ins = pe.transpose(RB[0:NE + 1, t * P:(t + 1) * P], wt[u][:, t, :], idf[:, :])
                        ins.then_inc(s_WT, 1)
                    elif e[0] == "D":
                        d = e[1] - 1
                        x = e[1]
                        wait(pe, s_aL, 4 + split(m, x) + 2)
                        if d == 0:
                            wait(pe, s_wT, m + 1)
                        for k in range(2):
                            wait(pe, s_z, NDB * m + 2 * d + k + 1)
                            for t in (2 * k, 2 * k + 1):
                                tok = slice(t * P, (t + 1) * P)
                                out = Dn[k][:, t % 2, :]
                                if d == 0:
                                    pe.matmul(out, wT[:, tok], w["bd"][:, :], start=True, stop=False)
                                for c in range(KC):
                                    ins = mm3(pe, out, aH[x % RA][c][:, tok], aL[x % RA][c][:, tok],
                                              w["dH"][:, ORDER[x], c, :], w["dL"][:, ORDER[x], c, :],
                                              d > 0 and c == 0, c == KC - 1)
                            ins.then_inc(s_dn, 1)

                run(pe, do)


def stage_finish(nc, X1S, FS, tg, out):
    with ExitStack() as ctx:
        r_ = Res(nc, ctx, "fi_")
        NU = 2
        x1, y = ([r_.sb(f"{n}{u}", [P, QT, C]) for u in range(NU)] for n in ("x1", "y"))
        s_ld, s_so = ([r_.sem(f"{n}{u}") for u in range(NU)] for n in ("ld", "so"))
        s_s = r_.sem("s")
        flat = lambda t: t[:, :, :].rearrange("p t c -> p (t c)")

        r_.prime()
        with nc.Block() as block:

            @block.sync
            def _(sp):
                with sp.Fori(0, B // NU) as it:
                    for u in range(NU):
                        b = NU * it + u
                        wait(sp, s_so[u], 16 * it)
                        sp.dma_start(x1[u][:, :, :], X1S[bass.ds(b, 1)].rearrange("o p t c -> (o p) t c")).then_inc(s_ld[u], 16)
                        sp.dma_start(y[u][:, :, :], FS[bass.ds(b, 1)].rearrange("o p t c -> (o p) t c")).then_inc(s_ld[u], 16)

            @block.vector
            def _(dve):
                with dve.Fori(0, B // NU) as it:
                    for u in range(NU):
                        b = NU * it + u
                        wait(dve, s_ld[u], 32 * (it + 1))
                        dve.scalar_tensor_tensor(flat(y[u]), flat(y[u]), tg[:, 1:2], flat(x1[u]), ALU.mult, ALU.add
                                                 ).then_inc(s_s, 1)

            @block.scalar
            def _(act):
                with act.Fori(0, B // NU) as it:
                    for u in range(NU):
                        b = NU * it + u
                        wait(act, s_s, b + 1)
                        act.dma_start(out[bass.ds(b, 1)].rearrange("o (t p) c -> p (o t) c", p=P), y[u][:, :, :]
                                      ).then_inc(s_so[u], 16)
                for u in range(NU):
                    wait(act, s_so[u], 16 * (B // NU))


def stage_constants(nc, a, idf, idb, mq, mk, tg, graw):
    with ExitStack() as ctx:
        r_ = Res(nc, ctx, "co_")
        s_g, s_m, s_t = r_.sem("g"), r_.sem("m"), r_.sem("t")
        r_.prime()
        with nc.Block() as block:

            @block.sync
            def _(sp):
                for n, g in enumerate(("g_xattn", "g_ffn")):
                    sp.dma_start(graw[:, n:n + 1], a[g].rearrange("(o c) -> o c", o=1).to_broadcast([P, 1])).then_inc(s_g, 16)

            @block.gpsimd
            def _(pool):
                for t, v in ((idf, 1.0), (idb, 1.0), (mq, 0.0), (mk, 0.0)):
                    pool.memset(t[:, :], v).then_inc(s_m, 1)
                wait(pool, s_m, 4)
                for t in (idf, idb):
                    pool.affine_select(out=t[:, :], in_=t[:, :], compare_op=ALU.is_equal, fill=0.0, base=0,
                                       pattern=[[-1, P]], channel_multiplier=1)
                pool.affine_select(out=mq[:, :], in_=mq[:, :], compare_op=ALU.is_ge, fill=NEG, base=0,
                                   pattern=[[-1, P]], channel_multiplier=1)
                pool.affine_select(out=mk[:, :], in_=mk[:, :], compare_op=ALU.is_ge, fill=NEG, base=0,
                                   pattern=[[1, P]], channel_multiplier=-1)

            @block.scalar
            def _(act):
                wait(act, s_g, 32)
                act.activation(tg[:, :], graw[:, :], ACT.Tanh).then_inc(s_t, 1)


def build(nc, a, out):
    QS = nc.dram_tensor("q_parts", [3, NI * GC, 2 * T], BF16).ap()
    KS = nc.dram_tensor("k_parts", [3, NI * GC, NK], BF16).ap()
    VS = nc.dram_tensor("v_items", [NI, P, NKT, GC], F32).ap()
    YS = nc.dram_tensor("y_items", [NI + 1, P, QT, GC], F32).ap()
    X1S = nc.dram_tensor("x1_blocks", [B, P, QT, C], F32).ap()
    FS = nc.dram_tensor("ffn_blocks", [B, P, QT, C], F32).ap()
    with ExitStack() as ctx:
        r_ = Res(nc, ctx, "c_")
        idf, idb = r_.sb("idf", [P, P]), r_.sb("idb", [P, P], BF16)
        mq, mk = r_.sb("mq", [P, P], BF16), r_.sb("mk", [P, P], BF16)
        tg, graw = r_.sb("tg", [P, 2]), r_.sb("graw", [P, 2])
        stage_constants(nc, a, idf, idb, mq, mk, tg, graw)
        stage_project(nc, a, QS, KS, VS, idf)
        stage_attend(nc, QS, KS, VS, YS, idf, idb, mq, mk)
        stage_mix(nc, a, YS, X1S, FS, tg, idf)
        w = {n: r_.sb(n, [P, NX, KC, IW], F32R) for n in ("uH", "uL", "cH", "cL", "dH", "dL")}
        w.update(bu=r_.sb("bu", [P, NX, KC]), bc=r_.sb("bc", [P, NX, KC]), bd=r_.sb("bd", [NE + 1, C]))
        stage_fold(nc, a, w)
        stage_experts(nc, a, FS, w, idf)
        stage_finish(nc, X1S, FS, tg, out)


def lay_out(i):
    f = lambda n: np.ascontiguousarray(np.asarray(i[n], np.float32))
    att, ffn = (lambda n: f("L0_xattn_" + n)), (lambda n: f("L0_ffn_" + n))
    up = np.concatenate([ffn("exp_Wup"), ffn("share_Wup").reshape(C, NS, IW).transpose(1, 0, 2)])
    shared = lambda e, s: np.concatenate([ffn(e)] + [ffn(s)[None]] * NS)
    cols = lambda v: v.reshape(*v.shape[:-1], KC, P)
    bup = np.concatenate([ffn("exp_bup"), ffn("share_bup").reshape(NS, IW)])
    d = {n: att(n) for n in ("Wk", "Wq", "Wv", "bv", "Wck", "Wcq", "Wcv", "bcv", "Wp", "bp")}
    d["bcol"] = cols(np.stack([att(n) for n in ("bq", "bcq", "bk", "bck")])).transpose(2, 0, 1)
    d.update(x=f("x"), ctxT=f("ctx_512").transpose(0, 2, 1), g_xattn=f("g_xattn"), g_ffn=f("g_ffn"),
             Wup=up, WupT=up.transpose(0, 2, 1), Wg=shared("exp_Wg", "share_Wg"), Wd=shared("exp_Wdown", "share_Wdown"),
             bup=cols(bup).transpose(2, 0, 1), bg=cols(shared("exp_bg", "share_bg")).transpose(2, 0, 1),
             bd=np.concatenate([ffn("exp_bdown"), ffn("share_bdown")[None]]),
             router_W=ffn("router_W").reshape(NL, KC, P, NE).transpose(2, 0, 1, 3), router_b=ffn("router_b"), gate_bias=ffn("gate_bias"), norm_w=ffn("norm_w"))
    return {n: np.ascontiguousarray(v) for n, v in d.items()}


def kernel(**inputs):
    import concourse.bacc as bacc
    from concourse.bass_utils import run_bass_kernel_spmd

    nc = bacc.Bacc("TRN2", target_bir_lowering=False, num_devices=1)
    arrays = lay_out(inputs)
    aps = {n: nc.dram_tensor("in_" + n, v.shape, mybir.dt.from_np(v.dtype), kind="ExternalInput").ap()
           for n, v in arrays.items()}
    out = nc.dram_tensor("out", (B, T, C), F32, kind="ExternalOutput").ap()
    build(nc, aps, out)
    r = run_bass_kernel_spmd(nc, [{"in_" + n: v for n, v in arrays.items()}], core_ids=[0])
    return r.results[0]["out"]
```

```python
from contextlib import ExitStack

import numpy as np

import concourse.bass as bass
import concourse.mybir as mybir
from concourse.alu_op_type import AluOpType as ALU

ACT = mybir.ActivationFunctionType
AX = mybir.AxisListType
F32, F32R, BF16 = mybir.dt.float32, mybir.dt.float32r, mybir.dt.bfloat16

P = 128
B, T, C = 8, 512, 256
H, D = 16, 16
TC, CC = 1601, 128
KC = C // P
QT = T // P
G = 4
NG = H // G
NI = B * NG
GC = G * D
NK = T + TC
CTXT = -(-TC // P)
NKT = QT + CTXT
LASTK = TC - (CTXT - 1) * P
TCE = TC + TC % 2
SCALE = 1.0 / float(np.sqrt(D))
NEG = -3.0e38
NE, NS, NL, IW = 6, 2, 2, 256
NX = NE + NS
LN_EPS, RMS_EPS = 1e-5, 1e-6

QPART = [0, 1, 2, 0, 1, 0]
KPART = [0, 0, 0, 1, 1, 2]
KROWS = D * len(QPART)
SROWS = KROWS + 3


def bcast(ap, n, axis):
    shape = list(ap.shape)
    shape[axis] = n
    return ap.to_broadcast(shape)


class Res:

    def __init__(self, nc, ctx, prefix):
        self.nc, self.ctx, self.prefix, self.spare, self.sems = nc, ctx, prefix, {}, []

    def sb(self, name, shape, dt=F32):
        return self.ctx.enter_context(self.nc.sbuf_tensor(self.prefix + name, shape, dt))

    def ps(self, name, shape, dt=F32):
        return self.ctx.enter_context(self.nc.psum_tensor(self.prefix + name, shape, dt))

    def sem(self, name):
        s = self.ctx.enter_context(self.nc.semaphore(self.prefix + name))
        self.sems.append(s)
        return s

    def prime(self, credit=()):
        extra = dict(credit)
        with self.nc.Block() as block:

            def share(k):
                def body(eng):
                    for s in self.sems[k::4]:
                        eng.sem_inc(s, 1 + extra.get(s.name, 0))
                return body

            for k, engine in enumerate((block.gpsimd, block.vector, block.scalar, block.sync)):
                engine(share(k))

    def carrier(self, eng):
        if id(eng) not in self.spare:
            self.spare[id(eng)] = self.sem(f"spare{len(self.spare)}")
        eng.sem_inc(self.spare[id(eng)], 1)


def wait(eng, sem, count):
    eng.wait_ge(sem, count + 1)


def mm3(pe, out, wH, wL, xH, xL, start, stop):
    pe.matmul(out, wL, xH, start=start, stop=False)
    pe.matmul(out, wH, xL, start=False, stop=False)
    return pe.matmul(out, wH, xH, start=False, stop=stop)


def stage_project(nc, a, QS, KS, VS, idf):
    with ExitStack() as ctx:
        r_ = Res(nc, ctx, "pj_")
        wraw = r_.sb("wraw", [P, 4, KC, C])
        craw = r_.sb("craw", [P, 2, C])
        wH, wL = r_.sb("wH", [P, 4, KC, C], F32R), r_.sb("wL", [P, 4, KC, C], F32R)
        cH, cL = r_.sb("cH", [P, 2, C], F32R), r_.sb("cL", [P, 2, C], F32R)
        bcol = r_.sb("bcol", [P, 4, KC])
        bvrow = r_.sb("bvrow", [P, 2, C])
        xin, xn = r_.sb("xin", [P, QT, C]), r_.sb("xn", [P, QT, C])
        st6, st2 = r_.sb("st6", [P, QT, 6]), r_.sb("st2", [P, QT, 2])
        var, rstd, expo = r_.sb("var", [P, QT]), r_.sb("rstd", [P, QT]), r_.sb("expo", [P, QT])
        xH, xL = r_.sb("xH", [P, KC, T], F32R), r_.sb("xL", [P, KC, T], F32R)
        ctxr = r_.sb("ctxr", [P, TCE])
        ctxH, ctxL = r_.sb("ctxH", [P, TCE], F32R), r_.sb("ctxL", [P, TCE], F32R)
        qpart = r_.sb("qpart", [P, 3, KC, 2 * T], BF16)
        kpart = r_.sb("kpart", [P, 3, KC, NK], BF16)
        vbuf = r_.sb("vbuf", [P, NG, NKT, GC])
        NR = 7
        rem = r_.sb("rem", [P, NR, T])
        NBANK = 6
        acc = [r_.ps(f"acc{i}", [P, T]) for i in range(NBANK)]
        tps = [r_.ps(f"tps{c}", [P, T]) for c in range(KC)]

        s_w, s_wH, s_wL = r_.sem("w"), r_.sem("wH"), r_.sem("wL")
        s_x, s_c = r_.sem("x"), r_.sem("c")
        s_cst, s_ln, s_var, s_rstd, s_xn = (r_.sem(n) for n in ("cst", "ln", "var", "rstd", "xn"))
        s_T, s_xH, s_xL = r_.sem("T"), r_.sem("xH"), r_.sem("xL")
        s_ctxH, s_ctxL = r_.sem("ctxH"), r_.sem("ctxL")
        s_out, s_h, s_fin, s_m, s_l = (r_.sem(n) for n in ("out", "h", "fin", "m", "l"))
        s_wr = {n: r_.sem("wr_" + n) for n in ("q0", "q1", "k0", "k1", "c0", "c1", "v")}

        CH = [402, 400, 400, 400]
        outs = [("q", 0, 0, "q0"), ("q", 1, 0, "q0"), ("q", 0, 1, "q1"), ("q", 1, 1, "q1"),
                ("k", 2, 0, "k0"), ("k", 2, 1, "k1"), ("vs", 0), ("vs", 2)]
        NSELF = len(outs)
        for cg in range(KC):
            at = 0
            for n in CH:
                outs.append(("c", at, cg, f"c{cg}", n))
                at += n
        outs += [("vc", t) for t in range(0, CTXT, 2)]
        NO = len(outs)
        split = [k for k, o in enumerate(outs) if o[0] in "qkc"]
        rank = {k: j for j, k in enumerate(split)}
        NSP = len(split)
        assert NSP == 2 * NR

        def parts(o):
            if o[0] == "q":
                return qpart, o[2], o[1] * T, T, bcol[:, o[1], o[2]:o[2] + 1]
            if o[0] == "k":
                return kpart, o[2], 0, T, bcol[:, 2, o[2]:o[2] + 1]
            n = min(o[4], TC - o[1])
            return kpart, o[2], T + o[1], n, bcol[:, 3, o[2]:o[2] + 1]

        def writes(tag):
            return [k for k in split if outs[k][3] == tag]

        r_.prime({s_fin.name: NO})
        with nc.Block() as block:

            @block.sync
            def _(sp):
                sp.dma_start(xin[:, :, :], a["x"][0].rearrange("(t p) c -> p t c", p=P)).then_inc(s_x, 16)
                for n, w in enumerate(("Wq", "Wcq", "Wk", "Wv")):
                    sp.dma_start(wraw[:, n], a[w].rearrange("(k p) n -> p k n", p=P)).then_inc(s_w, 16)
                for n, w in enumerate(("Wck", "Wcv")):
                    sp.dma_start(craw[:, n], a[w]).then_inc(s_w, 16)
                sp.dma_start(bcol[:, :, :], a["bcol"]).then_inc(s_w, 16)
                for n, w in enumerate(("bv", "bcv")):
                    sp.dma_start(bvrow[:, n], a[w].rearrange("(o c) -> o c", o=1).to_broadcast([P, C])).then_inc(s_w, 16)
                sp.dma_start(ctxr[:, 0:TC], a["ctxT"][0]).then_inc(s_c, 16)

                def write(b, tag):
                    ks = writes(tag)
                    tile, cg, c0, _, _ = parts(outs[ks[0]])
                    n = sum(parts(outs[k])[3] for k in ks)
                    wait(sp, s_l, b * NSP + rank[ks[-1]] + 1)
                    for part in range(3):
                        dst = QS if tile is qpart else KS
                        row = dst[part].rearrange("(b r) c -> b r c", b=B)[bass.ds(b, 1), cg * P:(cg + 1) * P, c0:c0 + n]
                        sp.dma_start(row.rearrange("o r c -> (o r) c"), tile[:, part, cg, c0:c0 + n]).then_inc(s_wr[tag], 16)

                def load_x(n):
                    wait(sp, s_xn, QT * n)
                    sp.dma_start(xin[:, :, :], a["x"][bass.ds(n, 1)].rearrange("o (t p) c -> p (o t) c", p=P)).then_inc(s_x, 16)

                def body(b, more, more2):
                    if more:
                        wait(sp, s_ctxL, b + 1)
                        wait(sp, s_ctxH, b + 1)
                        sp.dma_start(ctxr[:, 0:TC], a["ctxT"][bass.ds(b + 1, 1)].rearrange("o c t -> (o c) t")).then_inc(s_c, 16)
                    for tag in ("q0", "q1", "k0", "k1", "c0", "c1"):
                        write(b, tag)
                        if tag == "q1" and more2:
                            load_x(b + 2)
                    wait(sp, s_fin, NO * (b + 2))
                    for g in range(NG):
                        dst = VS.rearrange("(b g) p t c -> b g p t c", b=B)[bass.ds(b, 1), g]
                        sp.dma_start(dst.rearrange("o p t c -> (o p) t c"), vbuf[:, g]).then_inc(s_wr["v"], 16)

                load_x(1)
                with sp.Fori(0, B - 2) as b:
                    body(b, True, True)
                body(B - 2, True, False)
                body(B - 1, False, False)
                for tag, s in s_wr.items():
                    wait(sp, s, (64 if tag == "v" else 48) * B)

            @block.gpsimd
            def _(pool):
                pool.memset(expo[:, :], -0.5).then_inc(s_cst, 1)
                pool.memset(ctxr[:, TC:TCE], 0.0).then_inc(s_cst, 1)
                pool.memset(vbuf[:, :, NKT - 1, :], 0.0).then_inc(s_cst, 1)

                def power(n):
                    wait(pool, s_cst, 3)
                    wait(pool, s_var, n + 1)
                    pool.tensor_tensor(rstd[:, :], var[:, :], expo[:, :], ALU.pow).then_inc(s_rstd, 1)

                def body(b, more):
                    for j, k in enumerate(split):
                        if k == 2 and more:
                            power(b + 1)
                        tile, cg, c0, n, _ = parts(outs[k])
                        wait(pool, s_m, b * NSP + j + 1)
                        pool.tensor_tensor(tile[:, 2, cg, c0:c0 + n], rem[:, j % NR, 0:n], tile[:, 1, cg, c0:c0 + n],
                                           ALU.subtract).then_inc(s_l, 1)

                power(0)
                with pool.Fori(0, B - 1) as b:
                    body(b, True)
                body(B - 1, False)

            @block.vector
            def _(dve):
                wait(dve, s_cst, 3)
                wait(dve, s_wH, 6)
                for n in range(4):
                    dve.tensor_tensor(wL[:, n], wraw[:, n], wH[:, n].bitcast(F32), ALU.subtract).then_inc(s_wL, 1)
                for n in range(2):
                    dve.tensor_tensor(cL[:, n], craw[:, n], cH[:, n].bitcast(F32), ALU.subtract).then_inc(s_wL, 1)

                def statistics(n):
                    wait(dve, s_x, 16 * (n + 1))
                    for t in range(QT):
                        dve.bn_stats(st6[:, t, :], xin[:, t, :]).then_inc(s_ln, 1)
                    wait(dve, s_ln, 2 * QT * n + QT)
                    r_.carrier(dve)
                    for t in range(QT):
                        dve.bn_aggr(st2[:, t, :], st6[:, t, :]).then_inc(s_ln, 1)
                    wait(dve, s_ln, 2 * QT * (n + 1))
                    dve.tensor_scalar(var[:, :], st2[:, :, 1], LN_EPS, None, ALU.add).then_inc(s_var, 1)

                def normalise(n):
                    wait(dve, s_rstd, n + 1)
                    wait(dve, s_T, KC * n)
                    for t in range(QT):
                        dve.tensor_scalar(xn[:, t, :], xin[:, t, :], st2[:, t, 0:1], rstd[:, t:t + 1],
                                          ALU.subtract, ALU.mult).then_inc(s_xn, 1)

                def x_low(n):
                    for c in range(KC):
                        wait(dve, s_xH, KC * n + c + 1)
                        dve.tensor_tensor(xL[:, c, :], tps[c][:, :], xH[:, c, :].bitcast(F32), ALU.subtract).then_inc(s_xL, 1)

                def ctx_low(n):
                    wait(dve, s_ctxH, n + 1)
                    dve.tensor_tensor(ctxL[:, :], ctxr[:, :], ctxH[:, :].bitcast(F32), ALU.subtract).then_inc(s_ctxL, 1)

                def body(b, more):
                    for k, o in enumerate(outs):
                        bank = acc[k % NBANK]
                        if k == 1 and more:
                            statistics(b + 1)
                        if k == 4 and more:
                            normalise(b + 1)
                        if k == NSELF + 1 and more:
                            x_low(b + 1)
                        if k in rank:
                            j = rank[k]
                            tile, cg, c0, n, bias = parts(o)
                            wait(dve, s_h, b * NSP + j + 1)
                            if j >= NR:
                                wait(dve, s_l, b * NSP + j - NR + 1)
                            else:
                                wait(dve, s_l, b * NSP)
                            dve.scalar_tensor_tensor(rem[:, j % NR, 0:n], bank[:, 0:n], bias, tile[:, 0, cg, c0:c0 + n],
                                                     ALU.add, ALU.subtract).then_inc(s_fin, 1)
                            continue
                        wait(dve, s_out, b * NO + k + 1)
                        if o == ("vs", 0):
                            wait(dve, s_wr["v"], 64 * b)
                        kind, t = o
                        row = 0 if kind == "vs" else 1
                        for i in range(2):
                            tt = t + i
                            if kind == "vc" and tt >= CTXT:
                                continue
                            rows = LASTK if kind == "vc" and tt == CTXT - 1 else P
                            slot = tt if kind == "vs" else QT + tt
                            ins = dve.tensor_tensor(vbuf[0:rows, :, slot, :],
                                                    bank[0:rows, i * C:(i + 1) * C].rearrange("p (g c) -> p g c", g=NG),
                                                    bvrow[0:rows, row, :].rearrange("p (g c) -> p g c", g=NG), ALU.add)
                        ins.then_inc(s_fin, 1)
                    if more:
                        ctx_low(b + 1)

                statistics(0)
                normalise(0)
                x_low(0)
                ctx_low(0)
                with dve.Fori(0, B - 1) as b:
                    body(b, True)
                body(B - 1, False)

            @block.scalar
            def _(act):
                wait(act, s_w, 16 * 9)
                for n in range(4):
                    act.activation(wH[:, n], wraw[:, n], ACT.Copy).then_inc(s_wH, 1)
                for n in range(2):
                    act.activation(cH[:, n], craw[:, n], ACT.Copy).then_inc(s_wH, 1)

                def x_high(n):
                    wait(act, s_out, NO * n if isinstance(n, int) and n == 0 else NO * (n - 1) + NSELF)
                    for c in range(KC):
                        wait(act, s_T, KC * n + c + 1)
                        act.activation(xH[:, c, :], tps[c][:, :], ACT.Copy).then_inc(s_xH, 1)

                def ctx_high(n):
                    wait(act, s_c, 16 * (n + 1))
                    wait(act, s_cst, 3)
                    wait(act, s_out, NO * n)
                    act.activation(ctxH[:, :], ctxr[:, :], ACT.Copy).then_inc(s_ctxH, 1)

                def mid(b, k):
                    j = rank[k]
                    tile, cg, c0, n, _ = parts(outs[k])
                    wait(act, s_fin, NO * (b + 1) + k + 1)
                    act.activation(tile[:, 1, cg, c0:c0 + n], rem[:, j % NR, 0:n], ACT.Copy).then_inc(s_m, 1)

                def body(b, more):
                    seen, behind = set(), None
                    for k, o in enumerate(outs):
                        if k == NSELF:
                            mid(b, behind)
                            behind = None
                            if more:
                                x_high(b + 1)
                        if k not in rank:
                            continue
                        tile, cg, c0, n, bias = parts(o)
                        if o[3] not in seen:
                            wait(act, s_wr[o[3]], 48 * b)
                            seen.add(o[3])
                        wait(act, s_out, b * NO + k + 1)
                        act.activation(tile[:, 0, cg, c0:c0 + n], acc[k % NBANK][:, 0:n], ACT.Identity,
                                       bias=bias, scale=1.0).then_inc(s_h, 1)
                        if behind is not None:
                            mid(b, behind)
                        behind = k
                    mid(b, behind)
                    if more:
                        ctx_high(b + 1)

                x_high(0)
                ctx_high(0)
                with act.Fori(0, B - 1) as b:
                    body(b, True)
                body(B - 1, False)

            @block.tensor
            def _(pe):
                def transpose_x(n):
                    wait(pe, s_xn, QT * (n + 1))
                    wait(pe, s_xL, KC * n)
                    for c in range(KC):
                        for t in range(QT):
                            ins = pe.transpose(tps[c][:, t * P:(t + 1) * P], xn[:, t, c * P:(c + 1) * P], idf[:, :])
                        ins.then_inc(s_T, 1)

                def body(b, more):
                    for k, o in enumerate(outs):
                        if k == NSELF and more:
                            transpose_x(b + 1)
                        bank = acc[k % NBANK]
                        if k == 0:
                            wait(pe, s_xL, KC * (b + 1))
                        if k == NSELF:
                            wait(pe, s_ctxL, b + 1)
                        prev = k - NBANK if k >= NBANK else max(i for i in range(NO) if i % NBANK == k) - NO
                        wait(pe, s_fin, NO * (b + 1) + prev + 1)
                        if o[0] in "qk":
                            w, cg = o[1], o[2]
                            for c in range(KC):
                                cols = slice(cg * P, (cg + 1) * P)
                                ins = mm3(pe, bank[:, :], wH[:, w, c, cols], wL[:, w, c, cols], xH[:, c, :], xL[:, c, :],
                                          c == 0, c == KC - 1)
                        elif o[0] == "vs":
                            for i in range(2):
                                tok = slice((o[1] + i) * P, (o[1] + i + 1) * P)
                                for c in range(KC):
                                    ins = mm3(pe, bank[:, i * C:(i + 1) * C], xH[:, c, tok], xL[:, c, tok],
                                              wH[:, 3, c, :], wL[:, 3, c, :], c == 0, c == KC - 1)
                        elif o[0] == "c":
                            cols = slice(o[2] * P, (o[2] + 1) * P)
                            at, n = o[1], o[4]
                            ins = mm3(pe, bank[:, 0:n], cH[:, 0, cols], cL[:, 0, cols], ctxH[:, at:at + n],
                                      ctxL[:, at:at + n], True, True)
                        else:
                            for i in range(2):
                                tt = o[1] + i
                                if tt >= CTXT:
                                    continue
                                rows = LASTK if tt == CTXT - 1 else P
                                tok = slice(tt * P, tt * P + rows)
                                ins = mm3(pe, bank[0:rows, i * C:(i + 1) * C], ctxH[:, tok], ctxL[:, tok],
                                          cH[:, 1, :], cL[:, 1, :], True, True)
                        ins.then_inc(s_out, 1)

                wait(pe, s_wL, 6)
                transpose_x(0)
                with pe.Fori(0, B - 1) as b:
                    body(b, True)
                body(B - 1, False)


def stage_attend(nc, QS, KS, VS, YS, idf, idb, mq, mk):
    with ExitStack() as ctx:
        r_ = Res(nc, ctx, "at_")
        K = [r_.sb(f"K{u}", [SROWS, G, NK], BF16) for u in range(2)]
        Q = [r_.sb(f"Q{u}", [SROWS, 2, G, T], BF16) for u in range(2)]
        vraw = [r_.sb(f"vraw{u}", [P, NKT, GC]) for u in range(2)]
        V = [r_.sb(f"V{u}", [P, NKT, G, 2 * D]) for u in range(2)]
        Pt = [r_.sb(f"P{u}", [P, G, T]) for u in range(2)]
        part = r_.sb("part", [P, 2, G, QT, 2])
        mx = r_.sb("mx", [P, 2, G * QT])
        sh = [r_.sb(f"sh{k}", [G * QT, 3, P], BF16) for k in range(2)]
        rest = r_.sb("rest", [G * QT, 1, P])
        O = [r_.sb(f"O{k}", [P, T]) for k in range(2)]
        den = r_.sb("den", [P, 2, QT, G])
        yk = [r_.sb(f"y{k}", [P, QT, G, D]) for k in range(2)]
        ysum = [r_.sb(f"ysum{u}", [P, QT, GC]) for u in range(2)]
        NB = 3
        ST = [r_.ps(f"ST{i}", [P, T]) for i in range(NB)]
        R = [r_.ps(f"R{i}", [P, 2, T]) for i in range(2)]
        OP = r_.ps("OP", [P, T])

        s_ld = [[r_.sem(f"ld{k}{u}") for u in range(2)] for k in range(2)]
        s_vld = [r_.sem(f"vld{u}") for u in range(2)]
        (s_cst, s_v, s_st, s_ex, s_av, s_fill, s_drain, s_oe, s_ya, s_pm, s_sr, s_rc) = (
            r_.sem(n) for n in ("cst", "v", "st", "ex", "av", "fill", "drain", "oe", "ya", "pm", "sr", "rc"))
        s_y0 = r_.sem("y0")
        s_yst = [r_.sem(f"yst{u}") for u in range(2)]
        s_shD, s_shd = ([r_.sem(f"{n}{k}") for k in range(2)] for n in ("shD", "shd"))

        SELF, CROSS = 0, 1
        LAST = NKT - 1

        def key_tile(s):
            return QT + s if s < CTXT else s - CTXT

        def kind_of(s):
            return CROSS if s < CTXT else SELF

        XC = -(-TC // 4)
        XOFF = [[0, TC // 4], [2 * (TC // 4), TC - XC]]
        assert all(o1 - o0 <= XC for o0, o1 in XOFF) and XOFF[1][0] <= XOFF[0][1] + XC and XC <= T
        mtiles = [("x", h, q, half) for h in range(G) for q in range(QT) for half in range(2)]
        NMX = len(mtiles)
        mtiles += [("s", h, q) for h in range(G) for q in (0, 2)]
        NM = len(mtiles)
        NST = NKT * G

        def schedule():
            last_cross = 11
            n_self = {12: 1, 13: 2, 14: 2, 15: 1, 16: 2}
            ev, done = [], 0
            for s in range(NKT):
                upto = (s + 1) * NMX // (last_cross + 1) if s <= last_cross else done + n_self[s]
                ms = [("MAX", m, 1) for m in range(done, upto)]
                done = upto
                st = [("ST", s + 1, 0, h) if s < LAST else ("ST", 0, 1, h) for h in range(G)]
                before = ms[:min(len(ms) - 1, 2)] if s < LAST else []
                ev += [st[0]] + before[:1] + [st[1], st[2]] + before[1:]
                if s == last_cross + 1:
                    ev.append(("SHIFT", CROSS, 1))
                ev += [("AV", s, 0)] + [("OUT", CROSS, 0)] * (s == CTXT + 1) + ms[len(before):] + [st[3]]
                if s == NKT // 2 - 1:
                    ev.append(("SHIFT", SELF, 0))
                if s == LAST:
                    ev.append(("OUT", SELF, 0))
            assert done == NM
            return ev

        body_events = schedule()
        first_events = [e for e in body_events if e[0] in ("MAX", "SHIFT") and e[2] == 1]
        first_events += [("ST", 0, 1, h) for h in range(G)]
        last_events = [e for e in body_events if e[2] == 0]

        def slots(evs):
            return [e for e in evs if e[0] in ("MAX", "SHIFT", "OUT")]

        n_first, n_body = len(slots(first_events)), len(slots(body_events))
        assert n_body % 2 == 0

        def slot(i, evs, e):
            k = slots(evs).index(e) + (0 if evs is first_events else n_first)
            return (k if evs is first_events else n_body * i + k), R[k % 2]

        def loop(eng, body):
            body(-1, -1, 1, first_events)
            with eng.Fori(0, NI // 2 - 1) as it:
                for u in range(2):
                    body(2 * it + u, it, u, body_events)
            body(NI - 2, NI // 2 - 1, 0, body_events)
            body(NI - 1, NI // 2 - 1, 1, last_events)

        def st_cols(s):
            return 0 if s < CTXT else key_tile(s) * P

        def st_rows(s):
            return LASTK if s == CTXT - 1 else P

        r_.prime()
        with nc.Block() as block:

            @block.sync
            def _(sp):
                def load(kind, n, u):
                    cols = slice(T, NK) if kind == CROSS else slice(0, T)
                    for r in range(len(QPART)):
                        rows = slice(r * D, (r + 1) * D)
                        k = KS[KPART[r]].rearrange("(i h d) c -> i h d c", i=NI, h=G)[bass.ds(n, 1)]
                        sp.dma_start(K[u][rows, :, cols], k[:, :, :, cols].rearrange("o h d c -> (o d) h c")
                                     ).then_inc(s_ld[kind][u], 16)
                        q = QS[QPART[r]].rearrange("(i h d) (k c) -> i h d k c", i=NI, h=G, k=2)[bass.ds(n, 1)]
                        sp.dma_start(Q[u][rows, kind], q[:, :, :, kind].rearrange("o h d c -> (o d) h c")
                                     ).then_inc(s_ld[kind][u], 16)

                def load_values(n, u):
                    sp.dma_start(vraw[u][:, :, :], VS[bass.ds(n, 1)].rearrange("o p t c -> (o p) t c")).then_inc(s_vld[u], 16)

                def shift_rows(kind, n, u):
                    wait(sp, s_shD[kind], n + 1)
                    for p in range(3):
                        sp.dma_start(Q[u][KROWS + p:KROWS + p + 1, kind], sh[kind][:, p]).then_inc(s_shd[kind], 16)

                def store(n, u):
                    wait(sp, s_ya, n)
                    sp.dma_start(YS[bass.ds(n, 1)].rearrange("o p t c -> (o p) t c"), ysum[u][:, :, :]).then_inc(s_yst[u], 16)

                def body(i, it, u, evs):
                    if evs is first_events:
                        load(CROSS, 0, 0)
                        load(SELF, 0, 0)
                        load_values(0, 0)
                        load(CROSS, 1, 1)
                        shift_rows(CROSS, 0, 0)
                        wait(sp, s_y0, 1)
                        return
                    if evs is body_events:
                        wait(sp, s_st, NST * i)
                        r_.carrier(sp)
                        load(SELF, i + 1, 1 - u)
                        wait(sp, s_v, i)
                        load_values(i + 1, 1 - u)
                    store(i, 1 - u)
                    shift_rows(SELF, i, u)
                    if not isinstance(i, int):
                        wait(sp, s_st, NST * i + CTXT * G)
                        r_.carrier(sp)
                        load(CROSS, i + 2, u)
                    if evs is body_events:
                        shift_rows(CROSS, i + 1, 1 - u)

                loop(sp, body)
                store(NI, 1)
                wait(sp, s_yst[0], 16 * (NI // 2))
                wait(sp, s_yst[1], 16 * (NI // 2 + 1))

            @block.gpsimd
            def _(pool):
                for u in range(2):
                    pool.memset(V[u][:, :, :, D:2 * D], 1.0).then_inc(s_cst, 1)
                pool.memset(ysum[1][:, :, :], 0.0).then_inc(s_y0, 1)

                def body(i, it, u, evs):
                    if evs is not last_events:
                        nit = it if u == 0 else it + 1
                        wait(pool, s_vld[1 - u], 16 * (nit + 1))
                        if evs is body_events:
                            wait(pool, s_av, NKT * i)
                        r_.carrier(pool)
                        pool.tensor_copy(V[1 - u][:, :, :, 0:D],
                                         vraw[1 - u][:, :, :].rearrange("p t (h d) -> p t h d", h=G)).then_inc(s_v, 1)
                    if evs is first_events:
                        return
                    k, _ = slot(i, evs, ("OUT", SELF, 0))
                    wait(pool, s_drain, k + 1)
                    wait(pool, s_yst[u], 16 * (it + u))
                    pool.tensor_tensor(ysum[u][:, :, :].rearrange("p t c -> p (t c)"),
                                       yk[0][:, :, :, :].rearrange("p t h d -> p (t h d)"),
                                       yk[1][:, :, :, :].rearrange("p t h d -> p (t h d)"), ALU.add).then_inc(s_ya, 1)

                loop(pool, body)

            @block.vector
            def _(dve):
                for u in range(2):
                    dve.memset(K[u][KROWS:SROWS, :, :], 1.0).then_inc(s_cst, 1)

                def reduce_tile(m, k, buf, n):
                    tile = mtiles[m]
                    if tile[0] == "s":
                        _, h, q = tile
                        for j in range(2):
                            col = h * QT + q + j
                            ins = dve.tensor_reduce(mx[:, SELF, col:col + 1], buf[:, j, 0:(q + j + 1) * P], AX.X, ALU.max)
                    else:
                        _, h, q, half = tile
                        ins = dve.tensor_reduce(part[:, half, h, q, 0:1], buf[:, :, 0:XC], AX.XY, ALU.max)
                    ins.then_inc(s_drain, 1)
                    if m == NMX - 1:
                        wait(dve, s_drain, k + 1)
                        dve.tensor_tensor(mx[:, CROSS, :], part[:, 0, :, :, 0].rearrange("p h q -> p (h q)"),
                                          part[:, 1, :, :, 0].rearrange("p h q -> p (h q)"), ALU.max).then_inc(s_pm, 1)

                def shift_parts(kind, n, k, buf):
                    t, rem, out = buf[0:G * QT, 0, 0:P], rest[:, 0], sh[kind]
                    own = 2 * (2 * n + (1 if kind == SELF else 0))
                    wait(dve, s_shd[kind], 48 * n)
                    dve.tensor_scalar(out[:, 0], t, -1.0, None, ALU.mult).then_inc(s_sr, 1)
                    wait(dve, s_sr, own + 1)
                    dve.scalar_tensor_tensor(rem, t, -1.0, out[:, 0], ALU.mult, ALU.subtract).then_inc(s_drain, 1)
                    wait(dve, s_drain, k + 1)
                    dve.tensor_copy(out[:, 1], rem).then_inc(s_sr, 1)
                    wait(dve, s_sr, own + 2)
                    dve.tensor_tensor(out[:, 2], rem, out[:, 1], ALU.subtract).then_inc(s_shD[kind], 1)

                def output(kind, n, buf):
                    t = buf[:, 0, :].rearrange("p (q h e) -> p q h e", q=QT, h=G)
                    dve.reciprocal(den[:, kind], t[:, :, :, D]).then_inc(s_rc, 1)
                    wait(dve, s_rc, 2 * n + (2 if kind == SELF else 1))
                    wait(dve, s_ya, n)
                    dk = bcast(den[:, kind].rearrange("p q (h o) -> p (q h) o", o=1), D, 2)
                    dve.tensor_tensor(yk[kind][:, :, :, :].rearrange("p q h d -> p (q h) d"),
                                      t[:, :, :, 0:D].rearrange("p q h d -> p (q h) d"), dk, ALU.mult
                                      ).then_inc(s_drain, 1)

                def body(i, it, u, evs):
                    for e in slots(evs):
                        k, buf = slot(i, evs, e)
                        wait(dve, s_fill, k + 1)
                        if e[0] == "MAX":
                            reduce_tile(e[1], k, buf, i + e[2])
                        elif e[0] == "SHIFT":
                            shift_parts(e[1], i + e[2], k, buf)
                        else:
                            output(e[1], i, buf)

                loop(dve, body)

            @block.scalar
            def _(act):
                def exp(n, u, s, h, first):
                    rows, c0 = st_rows(s), st_cols(s)
                    wait(act, s_st, NST * n + s * G + h + 1)
                    if h == 0 and not first:
                        wait(act, s_av, NKT * n + s - 1)
                    act.activation(Pt[(s + u) % 2][0:rows, h, c0:T], ST[(s * G + h) % NB][0:rows, c0:T], ACT.Exp,
                                   scale=SCALE).then_inc(s_ex, 1)

                def body(i, it, u, evs):
                    for e in evs:
                        if e[0] == "ST":
                            exp(i + e[2], u if e[2] == 0 else 1 - u, e[1], e[3], evs is first_events)
                        elif e[0] == "AV" and e[1] in (CTXT - 1, LAST):
                            kind = kind_of(e[1])
                            wait(act, s_av, NKT * i + e[1] + 1)
                            act.activation(O[kind][:, :], OP[:, :], ACT.Copy).then_inc(s_oe, 1)

                loop(act, body)

            @block.tensor
            def _(pe):
                def max_tile(u, m, buf):
                    tile = mtiles[m]
                    if tile[0] == "s":
                        _, h, q = tile
                        for j in range(2):
                            w = (q + j + 1) * P
                            pe.matmul(buf[:, j, 0:w], Q[u][0:KROWS, SELF, h, (q + j) * P:w], K[u][0:KROWS, h, 0:w],
                                      start=True, stop=True)
                            ins = pe.matmul(buf[:, j, w - P:w], idb[:, :], mq[:, :], start=False, stop=True,
                                            skip_group_check=True)
                    else:
                        _, h, q, half = tile
                        for j in range(2):
                            at = T + XOFF[half][j]
                            ins = pe.matmul(buf[:, j, 0:XC], Q[u][0:KROWS, CROSS, h, q * P:(q + 1) * P],
                                            K[u][0:KROWS, h, at:at + XC], start=True, stop=True)
                    return ins

                def scores(n, u, s, h):
                    kind, t = kind_of(s), s * G + h
                    if h == 0 and s in (0, CTXT):
                        wait(pe, s_shd[kind], 48 * (n + 1))
                    if t >= NB:
                        wait(pe, s_ex, NST * n + t - NB + 1)
                    elif not isinstance(n, int) or n > 0:
                        wait(pe, s_ex, NST * (n - 1) + max(x for x in range(NST) if x % NB == t % NB) + 1)
                    rows, c0 = st_rows(s), st_cols(s)
                    keys = slice(key_tile(s) * P, key_tile(s) * P + rows)
                    out = ST[t % NB]
                    ins = pe.matmul(out[0:rows, c0:T], K[u][:, h, keys], Q[u][:, kind, h, c0:T], start=True,
                                    stop=True)
                    if kind == SELF:
                        ins = pe.matmul(out[:, c0:c0 + P], idb[:, :], mk[:, :], start=False, stop=True,
                                        skip_group_check=True)
                    ins.then_inc(s_st, 1)

                def values(i, u, s):
                    wait(pe, s_ex, NST * i + (s + 1) * G)
                    if s == 0:
                        wait(pe, s_v, i + 1)
                        wait(pe, s_oe, 2 * i)
                    if s == CTXT:
                        wait(pe, s_oe, 2 * i + 1)
                    rows, c0 = st_rows(s), st_cols(s)
                    for h in range(G):
                        ins = pe.matmul(OP[32 * h:32 * h + 2 * D, c0:T], V[u][0:rows, key_tile(s), h, :],
                                        Pt[(s + u) % 2][0:rows, h, c0:T],
                                        start=s in (0, CTXT), stop=s >= CTXT or s == CTXT - 1, skip_group_check=True)
                    ins.then_inc(s_av, 1)

                def body(i, it, u, evs):
                    for e in evs:
                        n, un = i + e[2], u if e[2] == 0 else 1 - u
                        if e[0] == "ST":
                            scores(n, un, e[1], e[3])
                            continue
                        if e[0] == "AV":
                            values(i, u, e[1])
                            continue
                        k, buf = slot(i, evs, e)
                        if evs is not first_events or k >= 2:
                            wait(pe, s_drain, k - 1)
                        if e[0] == "MAX":
                            if e[1:] in ((0, 1), (NMX, 1)):
                                nit = it if u == 0 else it + 1
                                wait(pe, s_ld[CROSS if e[1] == 0 else SELF][1 - u], 16 * 2 * len(QPART) * (nit + 1))
                            ins = max_tile(un, e[1], buf)
                        elif e[0] == "SHIFT":
                            if e[1] == CROSS:
                                wait(pe, s_pm, n + 1)
                            ins = pe.transpose(buf[0:G * QT, 0, 0:P], mx[:, e[1], :], idf[:, :])
                        else:
                            wait(pe, s_oe, 2 * n + (1 if e[1] == CROSS else 2))
                            for q in range(QT):
                                ins = pe.transpose(buf[:, 0, q * P:(q + 1) * P], O[e[1]][:, q * P:(q + 1) * P], idf[:, :])
                        ins.then_inc(s_fill, 1)

                wait(pe, s_cst, 4)
                loop(pe, body)


def fold_programs(r_, a, w, comb, bias):
    NU = 2
    upT, up, wg, wd = ([r_.sb(f"{n}{u}", [P, KC, IW]) for u in range(NU)] for n in ("upT", "up", "wg", "wd"))
    bg = r_.sb("bg", [P, NX, KC])
    s_b, s_H, s_L, s_c, s_cH, s_cL, s_bi, s_bo = (r_.sem("f" + n) for n in ("b", "H", "L", "c", "cH", "cL", "bi", "bo"))
    s_ld = [r_.sem(f"fld{u}") for u in range(NU)]
    NIT = NX // NU

    def sync(sp):
        sp.dma_start(bg[:, :, :], a["bg"]).then_inc(s_b, 16)
        sp.dma_start(w["bu"][:, :, :], a["bup"]).then_inc(s_b, 16)
        sp.dma_start(w["bd"][:, :], a["bd"]).then_inc(s_b, 16)
        wait(sp, s_b, 48)
        with sp.Fori(0, NIT) as it:
            for u in range(NU):
                e = NU * it + u
                wait(sp, s_L, 2 * e)
                r_.carrier(sp)
                wait(sp, s_bi, e)
                r_.carrier(sp)
                for dst, src in ((upT, "WupT"), (up, "Wup"), (wg, "Wg"), (wd, "Wd")):
                    sp.dma_start(dst[u][:, :, :], a[src][bass.ds(e, 1)].rearrange("o (k p) n -> p (o k) n", p=P)
                                 ).then_inc(s_ld[u], 16)

    def scalar(act):
        with act.Fori(0, NIT) as it:
            for u in range(NU):
                e = NU * it + u
                wait(act, s_ld[u], 64 * (it + 1))
                for raw, h in ((up, "uH"), (wd, "dH")):
                    act.activation(w[h][:, bass.ds(e, 1)].rearrange("p o k n -> p (o k) n"), raw[u][:, :, :],
                                   ACT.Copy).then_inc(s_H, 1)
                wait(act, s_c, e + 1)
                act.activation(w["cH"][:, bass.ds(e, 1)].rearrange("p o k n -> p (o k) n"), comb[u][:, :, :],
                               ACT.Copy).then_inc(s_cH, 1)

    def vector(dve):
        def low(dst, src, high, e):
            v = lambda t: t[:, bass.ds(e, 1)].rearrange("p o k n -> p (o k n)")
            return dve.tensor_tensor(v(w[dst]), src.rearrange("p k n -> p (k n)"), v(w[high]).bitcast(F32),
                                     ALU.subtract)

        wait(dve, s_b, 48)
        with dve.Fori(0, NIT) as it:
            for u in range(NU):
                e = NU * it + u
                wait(dve, s_H, 2 * e + 2)
                low("uL", up[u][:, :, :], "uH", e).then_inc(s_L, 1)
                low("dL", wd[u][:, :, :], "dH", e).then_inc(s_L, 1)
                wait(dve, s_cH, e + 1)
                low("cL", comb[u][:, :, :], "cH", e).then_inc(s_cL, 1)
                wait(dve, s_bi, e + 2)
                dve.tensor_tensor(w["bc"][:, bass.ds(e, 1)].rearrange("p o k -> p (o k)"), bias[u][:, 0:KC],
                                  bg[:, bass.ds(e, 1)].rearrange("p o k -> p (o k)"), ALU.add).then_inc(s_bo, 1)

    def tensor(pe):
        wait(pe, s_b, 48)
        with pe.Fori(0, NIT) as it:
            for u in range(NU):
                e = NU * it + u
                wait(pe, s_ld[u], 64 * (it + 1))
                wait(pe, s_bo, e)
                for m in range(KC):
                    for k in range(KC):
                        ins = pe.matmul(comb[u][:, m, :], upT[u][:, k, m * P:(m + 1) * P], wg[u][:, k, :],
                                        start=k == 0, stop=k == KC - 1)
                ins.then_inc(s_c, 1)
                for m in range(KC):
                    for k in range(KC):
                        ins = pe.matmul(bias[u][:, m:m + 1], wg[u][:, k, m * P:(m + 1) * P],
                                        w["bu"][:, bass.ds(e, 1), k],
                                        start=k == 0, stop=k == KC - 1)
                ins.then_inc(s_bi, 1)

    return (dict(sync=sync, scalar=scalar, vector=vector, tensor=tensor),
            {s_L.name: 2, s_bi.name: 1, s_bo.name: 1})


def stage_mix(nc, a, YS, X1S, FS, w, tg, idf):
    with ExitStack() as ctx:
        r_ = Res(nc, ctx, "mx_")
        wraw, wH, wL = r_.sb("wraw", [P, KC, C]), r_.sb("wH", [P, KC, C], F32R), r_.sb("wL", [P, KC, C], F32R)
        bp = r_.sb("bp", [P, QT, C])
        NU = 2
        y, x1, xf = ([r_.sb(f"{n}{u}", [P, QT, C]) for u in range(NU)] for n in ("y", "x1", "xf"))
        x = r_.sb("x", [P, B, QT * C])
        yH, yL = ([r_.sb(f"{n}{u}", [P, KC, T], F32R) for u in range(NU)] for n in ("yH", "yL"))
        st6, st2 = ([r_.sb(f"{n}{u}", [P, QT, m]) for u in range(NU)] for n, m in (("st6", 6), ("st2", 2)))
        var, rstd = ([r_.sb(f"{n}{u}", [P, QT]) for u in range(NU)] for n in ("var", "rstd"))
        expo = r_.sb("expo", [P, QT])
        tp = [r_.ps(f"tp{c}", [P, T]) for c in range(KC)]
        op = [[r_.ps(f"op{u}{i}", [P, 2, C]) for i in range(2)] for u in range(NU)]
        s_w, s_wH, s_wL, s_bp, s_xb, s_T, s_yH, s_yL, s_op, s_x1, s_st, s_ln, s_rs, s_xf, s_e = (
            r_.sem(n) for n in ("w", "wH", "wL", "bp", "xb", "T", "yH", "yL", "op", "x1", "st", "ln", "rs", "xf", "e"))
        s_ly, s_lx, s_so = ([r_.sem(f"{n}{u}") for u in range(NU)] for n in ("ly", "lx", "so"))

        def before(b, n):
            return max(b - n + 1, 0) if isinstance(b, int) else b - n + 1

        def run(eng, phases, do):
            def slot(h, u, live):
                for ph in phases:
                    if ph in live:
                        lag = "ABC".index(ph)
                        do(ph, 2 * h + u - lag, (u + lag) % 2, h if u >= lag else h - 1)

            slot(0, 0, "A")
            slot(0, 1, "AB")
            with eng.Fori(1, B // 2) as h:
                for u in range(2):
                    slot(h, u, "ABC")
            slot(B // 2, 0, "BC")
            slot(B // 2, 1, "C")

        fold, credit = fold_programs(r_, a, w, [t[:, :].rearrange("p (k n) -> p k n", k=KC) for t in tp],
                                     [op[u][0][:, 0, :] for u in range(NU)])
        r_.prime(credit)
        with nc.Block() as block:

            @block.sync
            def _(sp):
                sp.dma_start(wraw[:, :, :], a["Wp"].rearrange("(k p) n -> p k n", p=P)).then_inc(s_w, 16)
                for t in range(QT):
                    sp.dma_start(bp[:, t], a["bp"].rearrange("(o c) -> o c", o=1).to_broadcast([P, C])).then_inc(s_w, 16)

                def load(b, u, h):
                    wait(sp, s_T, KC * before(b, 2))
                    for g in range(NG):
                        sp.dma_start(y[u][:, :, g * GC:(g + 1) * GC],
                                     YS[bass.ds(NG * b + g + 1, 1)].rearrange("o p t c -> (o p) t c")).then_inc(s_ly[u], 16)
                    wait(sp, s_lx[u], 16 * h)
                    sp.dma_start(x[:, bass.ds(b, 1)].rearrange("p o (t c) -> p (o t) c", t=QT),
                                 a["x"][bass.ds(b, 1)].rearrange("o (t p) c -> p (o t) c", p=P)).then_inc(s_lx[u], 16)

                for b in range(NU):
                    load(b, b, 0)
                with sp.Fori(1, B // 2) as h:
                    for u in range(NU):
                        load(2 * h + u, u, h)
                fold["sync"](sp)

            @block.gpsimd
            def _(pool):
                pool.memset(expo[:, :], -0.5).then_inc(s_e, 1)
                wait(pool, s_e, 1)
                wait(pool, s_bp, QT)

                def do(ph, b, u, h):
                    if ph == "B":
                        wait(pool, s_lx[u], 16 * (h + 1))
                        xb = x[:, bass.ds(b, 1)].rearrange("p o n -> p (o n)")
                        pool.tensor_tensor(xb, xb, bp[:, :, :].rearrange("p t c -> p (t c)"), ALU.add).then_inc(s_xb, 1)
                    else:
                        wait(pool, s_ln, 2 * (b + 1))
                        pool.tensor_tensor(rstd[u][:, :], var[u][:, :], expo[:, :], ALU.pow).then_inc(s_rs, 1)

                run(pool, "CB", do)

            @block.scalar
            def _(act):
                wait(act, s_w, 16 * (1 + QT))
                act.activation(wH[:, :, :], wraw[:, :, :], ACT.Copy).then_inc(s_wH, 1)
                for t in range(QT):
                    act.activation(bp[:, t], bp[:, t], ACT.Copy, scale=tg[:, 0:1]).then_inc(s_bp, 1)

                def do(ph, b, u, h):
                    if ph == "A":
                        wait(act, s_op, 2 * before(b, 2))
                        for c in range(KC):
                            wait(act, s_T, KC * b + c + 1)
                            act.activation(yH[u][:, c, :], tp[c][:, :], ACT.Copy).then_inc(s_yH, 1)
                    else:
                        wait(act, s_x1, QT // 2 * (b + 1))
                        act.dma_start(X1S[bass.ds(b, 1)].rearrange("o p t c -> (o p) t c"), x1[u][:, :, :]).then_inc(s_so[u], 16)
                        wait(act, s_xf, QT * (b + 1))
                        act.dma_start(FS[bass.ds(b, 1)].rearrange("o p t c -> (o p) t c"), xf[u][:, :, :]).then_inc(s_so[u], 16)

                run(act, "AC", do)
                fold["scalar"](act)
                for u in range(NU):
                    wait(act, s_so[u], 32 * (B // 2))

            @block.vector
            def _(dve):
                wait(dve, s_wH, 1)
                dve.tensor_tensor(wL[:, :, :], wraw[:, :, :], wH[:, :, :].bitcast(F32), ALU.subtract).then_inc(s_wL, 1)

                def do(ph, b, u, h):
                    if ph == "A":
                        for c in range(KC):
                            wait(dve, s_yH, KC * b + c + 1)
                            dve.tensor_tensor(yL[u][:, c, :], tp[c][:, :], yH[u][:, c, :].bitcast(F32), ALU.subtract
                                              ).then_inc(s_yL, 1)
                    elif ph == "B":
                        wait(dve, s_xb, b + 1)
                        wait(dve, s_so[u], 32 * h)
                        for i in range(QT // 2):
                            wait(dve, s_op, 2 * b + i + 1)
                            dve.scalar_tensor_tensor(x1[u][:, 2 * i:2 * i + 2, :].rearrange("p t c -> p (t c)"),
                                                     op[u][i][:, :, :].rearrange("p t c -> p (t c)"), tg[:, 0:1],
                                                     x[:, bass.ds(b, 1), 2 * i * C:(2 * i + 2) * C].rearrange("p o n -> p (o n)"),
                                                     ALU.mult, ALU.add).then_inc(s_x1, 1)
                        wait(dve, s_x1, QT // 2 * (b + 1))
                        for t in range(QT):
                            ins = dve.bn_stats(st6[u][:, t, :], x1[u][:, t, :])
                        ins.then_inc(s_st, 1)
                        wait(dve, s_st, b + 1)
                        r_.carrier(dve)
                        for t in range(QT):
                            ins = dve.bn_aggr(st2[u][:, t, :], st6[u][:, t, :])
                        ins.then_inc(s_ln, 1)
                        wait(dve, s_ln, 2 * b + 1)
                        dve.tensor_scalar(var[u][:, :], st2[u][:, :, 1], LN_EPS, None, ALU.add).then_inc(s_ln, 1)
                    else:
                        wait(dve, s_rs, b + 1)
                        for t in range(QT):
                            dve.tensor_scalar(xf[u][:, t, :], x1[u][:, t, :], st2[u][:, t, 0:1], rstd[u][:, t:t + 1],
                                              ALU.subtract, ALU.mult).then_inc(s_xf, 1)

                run(dve, "CAB", do)
                fold["vector"](dve)

            @block.tensor
            def _(pe):
                wait(pe, s_wL, 1)

                def do(ph, b, u, h):
                    if ph == "A":
                        wait(pe, s_ly[u], 16 * NG * (h + 1))
                        wait(pe, s_yL, KC * b)
                        for c in range(KC):
                            for t in range(QT):
                                ins = pe.transpose(tp[c][:, t * P:(t + 1) * P], y[u][:, t, c * P:(c + 1) * P], idf[:, :])
                            ins.then_inc(s_T, 1)
                    else:
                        wait(pe, s_yL, KC * (b + 1))
                        wait(pe, s_x1, QT // 2 * before(b, 2))
                        for t in range(QT):
                            tok = slice(t * P, (t + 1) * P)
                            for c in range(KC):
                                ins = mm3(pe, op[u][t // 2][:, t % 2, :], yH[u][:, c, tok], yL[u][:, c, tok],
                                          wH[:, c, :], wL[:, c, :], c == 0, c == KC - 1)
                            if t % 2:
                                ins.then_inc(s_op, 1)

                run(pe, "AB", do)
                wait(pe, s_yL, KC * B)
                wait(pe, s_x1, QT // 2 * B)
                fold["tensor"](pe)


def stage_experts(nc, a, FS, X1S, w, tg, out, idf):
    with ExitStack() as ctx:
        r_ = Res(nc, ctx, "ex_")
        rraw = r_.sb("rraw", [P, NL, KC, NE])
        rw = r_.sb("rw", [P, NL, KC, 2 * NE], F32R)
        rb, gb = r_.sb("rb", [P, NL, NE]), r_.sb("gb", [P, NL, NE])
        nw = r_.sb("nw", [P, NL, C])
        prio, expo = r_.sb("prio", [P, QT, NE]), r_.sb("expo", [P, QT])
        xs = [r_.sb(f"xs{u}", [P, QT, C]) for u in range(2)]
        xH, xL = ([r_.sb(f"{n}{u}", [P, KC, T], F32R) for u in range(2)] for n in ("xH", "xL"))
        sg = [r_.sb(f"sg{c}", [P, T]) for c in range(KC)]
        af = [[r_.sb(f"af{u}{c}", [P, T]) for c in range(KC)] for u in range(2)]
        RA = 4
        aH, aL = ([[r_.sb(f"{n}{i}{c}", [P, T], F32R) for c in range(KC)] for i in range(RA)] for n in ("aH", "aL"))
        wt = [r_.sb(f"wt{u}", [P, QT, NE + 1]) for u in range(2)]
        wT = r_.sb("wT", [NE + 1, T])
        Z = [r_.sb(f"Z{u}", [P, QT, C]) for u in range(2)]
        sq = r_.sb("sq", [P, QT, C])
        ss, ms, rr = ([r_.sb(f"{n}{u}", [P, QT]) for u in range(2)] for n in ("ss", "ms", "rr"))
        sm = {n: r_.sb("g_" + n, [P, QT, NE]) for n in ("gt", "bi", "eq", "s1", "s2", "tmp")}
        s4 = {n: r_.sb("g4_" + n, [P, QT, 1]) for n in ("m", "v1", "v2", "d", "th", "w1", "w2")}
        GH = [r_.ps(f"GH{i}", [P, T]) for i in range(4)]
        Dn = [r_.ps(f"D{i}", [P, 2, C]) for i in range(2)]
        XT, RB = r_.ps("XT", [P, T]), r_.ps("RB", [P, T])

        (s_c, s_pool, s_rw, s_T, s_xH, s_xL, s_G, s_gate, s_d, s_th, s_WT, s_wT, s_up, s_sg, s_a, s_aH, s_aL, s_dn, s_z,
         s_ss, s_ms, s_rr, s_y, s_rwH, s_wt, s_nrm) = (
            r_.sem(n) for n in ("c", "pool", "rw", "T", "xH", "xL", "G", "gate", "d", "th", "WT", "wT", "up", "sg", "a",
                                "aH", "aL", "dn", "z", "ss", "ms", "rr", "y", "rwH", "wt", "nrm"))
        s_sum, s_out = r_.sem("sum"), r_.sem("out")
        s_x1 = [r_.sem(f"x1{u}") for u in range(2)]
        x1 = [r_.sb(f"x1{u}", [P, QT, C]) for u in range(2)]
        s_ld, s_st = ([r_.sem(f"{n}{u}") for u in range(2)] for n in ("ld", "st"))

        NM = NL * B
        ORDER = [NE + i for i in range(NS)] + list(range(NE))
        NDN = NX - NS + 1
        NDB = 2 * NDN
        LAST = NX - 1
        assert NX == 8 and NS == 2 and RA == 4
        REST = [("U", 1), ("tSq",), ("WT",), ("U", 2), ("tMs",), ("D", 1), ("U", 3), ("tNorm",), ("tOut",), ("D", 2), ("tSt",),
                ("nT", 0), ("U", 4), ("D", 3), ("nT", 1), ("U", 5), ("D", 4), ("nR",), ("U", 6), ("nTh",), ("D", 5),
                ("U", 7), ("nGate",), ("D", 6), ("nU",), ("D", 7)]
        HEAD = [("nT", 0), ("nT", 1), ("nR",), ("nTh",), ("nGate",), ("nU",)]
        TAILS = [("tSq",), ("tMs",), ("tNorm",), ("tOut",), ("tSt",)]

        def run(eng, do):
            def unit(m, h, u, prev, nxt):
                hp, hn = (h - 1 if u == 0 else h), (h if u == 0 else h + 1)
                for e in REST:
                    if e[0][0] == "n":
                        if nxt:
                            do(e, m + 1, 1 - u, hn)
                    elif e[0][0] == "t":
                        if prev is not None:
                            tail(e, m - 1, 1 - u, hp, prev)
                    else:
                        do(e, m, u, h)

            def tail(e, m, u, h, layer):
                if e[0] == "tSt":
                    do(("tSt", layer), m, u, h)
                elif e[0] != "tOut" or layer == NL - 1:
                    do(e, m, u, h)

            for e in HEAD:
                do(e, 0, 0, 0)
            unit(0, 0, 0, None, True)
            for layer in range(NL):
                with eng.Fori(layer * B // 2, (layer + 1) * B // 2 - (layer == NL - 1)) as it:
                    unit(2 * it + 1, it, 1, layer, True)
                    unit(2 * it + 2, it + 1, 0, layer, True)
            unit(NM - 1, NM // 2 - 1, 1, NL - 1, False)
            for e in TAILS:
                tail(e, NM - 1, 1, NM // 2 - 1, NL - 1)

        def freed_by(m, x):
            if x > RA:
                return NDB * (m + 1) + 2 * (x - RA)
            return NDB * m + 2 * (x + RA if x + RA < NX else x)

        def split(m, x):
            return 2 * (NDN * m + x - 1)

        r_.prime({s_aL.name: 4, s_a.name: 2, s_z.name: 2, s_sg.name: 2, s_dn.name: NDB, s_out.name: 1})
        with nc.Block() as block:

            @block.sync
            def _(sp):
                def load(m, u):
                    sp.dma_start(xs[u][:, :, :], FS[bass.ds(m % B, 1)].rearrange("o p t c -> (o p) t c")).then_inc(s_ld[u], 16)

                sp.dma_start(rraw[:, :, :, :], a["router_W"]).then_inc(s_c, 16)
                load(0, 0)
                for dst, src in ((rb, "router_b"), (gb, "gate_bias")):
                    for j in range(NL):
                        sp.dma_start(dst[:, j], a[src][j:j + 1, :].to_broadcast([P, NE])).then_inc(s_c, 16)
                for j in range(NL):
                    sp.dma_start(nw[:, j], a["norm_w"][j:j + 1, :].to_broadcast([P, C])).then_inc(s_c, 16)

                load(1, 1)

                def load_x1(m, u):
                    sp.dma_start(x1[u][:, :, :], X1S[bass.ds(m % B, 1)].rearrange("o p t c -> (o p) t c")).then_inc(s_x1[u], 16)

                with sp.Fori(1, B // 2) as h:
                    for u in range(2):
                        m = 2 * h + u
                        wait(sp, s_z, 2 + NDB * (m - 2) + 2)
                        load(m, u)
                with sp.Fori(B // 2, NM // 2) as h:
                    for u in range(2):
                        m = 2 * h + u
                        wait(sp, s_z, 2 + NDB * (m - 2) + 2)
                        wait(sp, s_st[u], 16 * (h - B // 2 + 1))
                        load(m, u)
                        wait(sp, s_out, m - (NM - B))
                        load_x1(m, u)
                for u in range(2):
                    wait(sp, s_st[u], 16 * (NM // 2))

            @block.gpsimd
            def _(pool):
                pool.memset(expo[:, :], -0.5).then_inc(s_pool, 1)
                for e in range(NE):
                    pool.memset(prio[:, :, e:e + 1], float(NE - e)).then_inc(s_pool, 1)
                for u in range(2):
                    pool.memset(wt[u][:, :, NE:NE + 1], float(NS)).then_inc(s_pool, 1)
                wait(pool, s_pool, 1)

                def do(e, m, u, h):
                    if e[0] in ("U", "nU"):
                        x = e[1] if e[0] == "U" else 0
                        for c in range(KC if x else 0):
                            wait(pool, s_aH, split(m, x) + c + 1)
                            pool.tensor_tensor(aL[x % RA][c][:, :], af[x % 2][c][:, :],
                                               aH[x % RA][c][:, :].bitcast(F32), ALU.subtract).then_inc(s_aL, 1)
                    elif e[0] == "tMs":
                        wait(pool, s_ms, m + 1)
                        pool.tensor_tensor(rr[u][:, :], ms[u][:, :], expo[:, :], ALU.pow).then_inc(s_rr, 1)

                run(pool, do)

            @block.vector
            def _(dve):
                wait(dve, s_c, 16 * (1 + 3 * NL))
                wait(dve, s_rwH, 1)
                dve.tensor_tensor(rw[:, :, :, NE:2 * NE], rraw[:, :, :, :], rw[:, :, :, 0:NE].bitcast(F32), ALU.subtract
                                  ).then_inc(s_rw, 1)
                wait(dve, s_pool, NE + 3)
                GN = 18

                def wide(t):
                    return t[:, :, :].to_broadcast([P, QT, NE])

                def router_choice(m):
                    k = [0]

                    def link(ins):
                        k[0] += 1
                        ins.then_inc(s_gate, 1)
                        wait(dve, s_gate, GN * m + k[0])

                    gt, bi, eq, tmp = (sm[n][:, :, :] for n in ("gt", "bi", "eq", "tmp"))
                    j = m // B
                    lay = lambda t: bcast(t[:, bass.ds(j, 1)], QT, 1)
                    logits = RB[:, 0:QT * 2 * NE].rearrange("p (t e) -> p t e", t=QT)
                    wait(dve, s_G, m + 1)
                    wait(dve, s_WT, m)
                    link(dve.tensor_tensor(tmp, logits[:, :, 0:NE], lay(rb), ALU.add))
                    link(dve.tensor_tensor(gt, logits[:, :, NE:2 * NE], tmp, ALU.add))
                    link(dve.tensor_tensor(bi, gt, lay(gb), ALU.add))
                    for n, v in (("s1", "v1"), ("s2", "v2")):
                        s = sm[n][:, :, :]
                        link(dve.tensor_reduce(s4["m"][:, :, :], bi, AX.X, ALU.max))
                        link(dve.tensor_tensor(eq, bi, wide(s4["m"]), ALU.is_ge))
                        link(dve.tensor_tensor(eq, eq, prio[:, :, :], ALU.mult))
                        link(dve.tensor_reduce(s4["m"][:, :, :], eq, AX.X, ALU.max))
                        link(dve.tensor_tensor(s, eq, wide(s4["m"]), ALU.is_equal))
                        link(dve.tensor_tensor(tmp, s, gt, ALU.mult))
                        link(dve.tensor_reduce(s4[v][:, :, :], tmp, AX.X, ALU.add))
                        if n == "s1":
                            link(dve.scalar_tensor_tensor(bi, s, NEG, bi, ALU.mult, ALU.add))
                    assert k[0] == GN
                    dve.tensor_tensor(s4["d"][:, :, :], s4["v1"][:, :, :], s4["v2"][:, :, :], ALU.subtract).then_inc(s_d, 1)

                def router_weights(m, u):
                    w1, w2, th = (s4[n][:, :, :] for n in ("w1", "w2", "th"))
                    s1, s2 = sm["s1"][:, :, :], sm["s2"][:, :, :]
                    wait(dve, s_th, m + 1)
                    dve.tensor_scalar(w1, th, 0.5, 0.5, ALU.mult, ALU.add).then_inc(s_y, 1)
                    dve.tensor_scalar(w2, th, -0.5, 0.5, ALU.mult, ALU.add).then_inc(s_y, 1)
                    wait(dve, s_y, 4 * m + 2)
                    dve.tensor_tensor(s1, s1, wide(s4["w1"]), ALU.mult).then_inc(s_y, 1)
                    dve.tensor_tensor(s2, s2, wide(s4["w2"]), ALU.mult).then_inc(s_y, 1)
                    wait(dve, s_y, 4 * m + 4)
                    dve.tensor_tensor(wt[u][:, :, 0:NE], s1, s2, ALU.add).then_inc(s_wt, 1)

                def do(e, m, u, h):
                    if e[0] == "nT":
                        c = e[1]
                        wait(dve, s_xH, KC * m + c + 1)
                        dve.tensor_tensor(xL[u][:, c, :], XT[:, :], xH[u][:, c, :].bitcast(F32), ALU.subtract).then_inc(s_xL, 1)
                    elif e[0] == "nR":
                        router_choice(m)
                    elif e[0] == "nGate":
                        router_weights(m, u)
                    elif e[0] == "WT":
                        wait(dve, s_WT, m + 1)
                        wait(dve, s_dn, NDB * m + 2)
                        dve.tensor_copy(wT[:, :], RB[0:NE + 1, :]).then_inc(s_wT, 1)
                    elif e[0] in ("U", "nU"):
                        x = e[1] if e[0] == "U" else 0
                        for c in range(KC):
                            n = NX * m + x
                            wait(dve, s_up, 4 * n + 2 * c + 2)
                            wait(dve, s_sg, 2 + 2 * n + c + 1)
                            if x != 2:
                                wait(dve, s_aL, 2 * NDN * m + 2 * (x if x < 2 else x - 1) + c + 1)
                            dve.scalar_tensor_tensor(af[x % 2][c][:, :], GH[2 * c + 1][:, :], w["bu"][:, ORDER[x], c:c + 1],
                                                     sg[c][:, :], ALU.add, ALU.mult).then_inc(s_a, 1)
                        if x == 1:
                            for c in range(KC):
                                wait(dve, s_a, 2 + 2 * n + c + 1)
                                dve.tensor_tensor(af[1][c][:, :], af[1][c][:, :], af[0][c][:, :], ALU.add).then_inc(s_sum, 1)
                    elif e[0] == "D":
                        d = e[1] - 1
                        for k in range(2):
                            wait(dve, s_dn, NDB * (m + 1) + 2 * d + k + 1)
                            if d == 0:
                                if k == 0:
                                    wait(dve, s_st[u], 16 * h)
                                ins = dve.tensor_tensor(Z[u][:, 2 * k:2 * k + 2, :], Dn[k][:, :, :],
                                                        xs[u][:, 2 * k:2 * k + 2, :], ALU.add)
                            else:
                                wait(dve, s_z, NDB * m + 2 * d + k + 1)
                                for t in (2 * k, 2 * k + 1):
                                    ex = ORDER[e[1]]
                                    ins = dve.scalar_tensor_tensor(Z[u][:, t, :], Dn[k][:, t % 2, :], wt[u][:, t, ex:ex + 1],
                                                                   Z[u][:, t, :], ALU.mult, ALU.add)
                            ins.then_inc(s_z, 1)
                    elif e[0] == "tMs":
                        wait(dve, s_ss, m + 1)
                        dve.tensor_scalar(ms[u][:, :], ss[u][:, :], 1.0 / C, RMS_EPS, ALU.mult, ALU.add).then_inc(s_ms, 1)
                    elif e[0] == "tNorm":
                        wait(dve, s_rr, m + 1)
                        for t in range(QT):
                            ins = dve.scalar_tensor_tensor(
                                Z[u][:, t, :], Z[u][:, t, :], rr[u][:, t:t + 1],
                                nw[:, bass.ds(m // B, 1), :].rearrange("p o c -> p (o c)"), ALU.mult, ALU.mult)
                        ins.then_inc(s_nrm, 1)
                    elif e[0] == "tOut":
                        wait(dve, s_nrm, m + 1)
                        wait(dve, s_x1[u], 16 * (h - B // 2 + 1))
                        flat = lambda t: t[:, :, :].rearrange("p t c -> p (t c)")
                        dve.scalar_tensor_tensor(flat(Z[u]), flat(Z[u]), tg[:, 1:2], flat(x1[u]), ALU.mult, ALU.add
                                                 ).then_inc(s_out, 1)

                run(dve, do)

            @block.scalar
            def _(act):
                wait(act, s_c, 16 * (1 + 3 * NL))
                act.activation(rw[:, :, :, 0:NE], rraw[:, :, :, :], ACT.Copy).then_inc(s_rwH, 1)

                def do(e, m, u, h):
                    if e[0] == "nT":
                        c = e[1]
                        wait(act, s_T, KC * m + c + 1)
                        act.activation(xH[u][:, c, :], XT[:, :], ACT.Copy).then_inc(s_xH, 1)
                    elif e[0] == "nTh":
                        wait(act, s_d, m + 1)
                        act.activation(s4["th"][:, :, :], s4["d"][:, :, :], ACT.Tanh, scale=0.5).then_inc(s_th, 1)
                    elif e[0] in ("U", "nU"):
                        x = e[1] if e[0] == "U" else 0
                        n = NX * m + x
                        for c in range(KC):
                            wait(act, s_up, 4 * n + 2 * c + 1)
                            wait(act, s_a, 2 * n + c + 1)
                            act.activation(sg[c][:, :], GH[2 * c][:, :], ACT.Silu, bias=w["bc"][:, ORDER[x], c:c + 1],
                                           scale=1.0).then_inc(s_sg, 1)
                        if x == 0:
                            return
                        wait(act, s_dn, freed_by(m, x))
                        for c in range(KC):
                            if x == 1:
                                wait(act, s_sum, 2 * m + c + 1)
                            else:
                                wait(act, s_a, 2 + 2 * n + c + 1)
                            act.activation(aH[x % RA][c][:, :], af[x % 2][c][:, :], ACT.Copy).then_inc(s_aH, 1)
                    elif e[0] == "tSq":
                        wait(act, s_z, 2 + NDB * (m + 1))
                        for t in range(QT):
                            ins = act.activation(sq[:, t, :], Z[u][:, t, :], ACT.Square, accum_out=ss[u][:, t:t + 1])
                        ins.then_inc(s_ss, 1)
                    elif e[0] == "tSt":
                        if e[1] < NL - 1:
                            wait(act, s_nrm, m + 1)
                            dst = FS[bass.ds(m % B, 1)].rearrange("o p t c -> (o p) t c")
                        else:
                            wait(act, s_out, 1 + m - (NM - B) + 1)
                            dst = out[bass.ds(m % B, 1)].rearrange("o (t p) c -> p (o t) c", p=P)
                        act.dma_start(dst, Z[u][:, :, :]).then_inc(s_st[u], 16)

                run(act, do)

            @block.tensor
            def _(pe):
                wait(pe, s_rw, 1)

                def up(m, x):
                    e, n = ORDER[x], NX * m + x
                    u = UP[0]
                    for c in range(KC):
                        cols = slice(c * P, (c + 1) * P)
                        for i, (wh, wl) in enumerate(((w["cH"], w["cL"]), (w["uH"], w["uL"]))):
                            wait(pe, (s_sg, s_a)[i], 2 * n + c + 1)
                            for k in range(KC):
                                ins = mm3(pe, GH[2 * c + i][:, :], wh[:, e, k, cols], wl[:, e, k, cols], xH[u][:, k, :],
                                          xL[u][:, k, :], k == 0, k == KC - 1)
                            ins.then_inc(s_up, 1)

                UP = [0]

                def do(e, m, u, h):
                    if e[0] == "nT":
                        c = e[1]
                        if c == 0:
                            wait(pe, s_ld[u], 16 * (h + 1))
                        wait(pe, s_xL, KC * m + c)
                        for t in range(QT):
                            ins = pe.transpose(XT[:, t * P:(t + 1) * P], xs[u][:, t, c * P:(c + 1) * P], idf[:, :])
                        ins.then_inc(s_T, 1)
                    elif e[0] == "nR":
                        wait(pe, s_xL, KC * (m + 1))
                        wait(pe, s_wT, m)
                        for t in range(QT):
                            tok = slice(t * P, (t + 1) * P)
                            for k in range(KC):
                                for i, x in enumerate((xL, xH)):
                                    ins = pe.matmul(RB[:, t * 2 * NE:(t + 1) * 2 * NE], x[u][:, k, tok],
                                                    rw[:, bass.ds(m // B, 1), k, :].rearrange("p o e -> p (o e)"),
                                                    start=k == 0 and i == 0, stop=k == KC - 1 and i == 1)
                        ins.then_inc(s_G, 1)
                    elif e[0] in ("U", "nU"):
                        UP[0] = u
                        up(m, e[1] if e[0] == "U" else 0)
                    elif e[0] == "WT":
                        wait(pe, s_wt, m + 1)
                        for t in range(QT):
                            ins = pe.transpose(RB[0:NE + 1, t * P:(t + 1) * P], wt[u][:, t, :], idf[:, :])
                        ins.then_inc(s_WT, 1)
                    elif e[0] == "D":
                        d = e[1] - 1
                        x = e[1]
                        wait(pe, s_aL, 4 + split(m, x) + 2)
                        if d == 0:
                            wait(pe, s_wT, m + 1)
                        for k in range(2):
                            wait(pe, s_z, NDB * m + 2 * d + k + 1)
                            for t in (2 * k, 2 * k + 1):
                                tok = slice(t * P, (t + 1) * P)
                                out = Dn[k][:, t % 2, :]
                                if d == 0:
                                    pe.matmul(out, wT[:, tok], w["bd"][:, :], start=True, stop=False)
                                for c in range(KC):
                                    ins = mm3(pe, out, aH[x % RA][c][:, tok], aL[x % RA][c][:, tok],
                                              w["dH"][:, ORDER[x], c, :], w["dL"][:, ORDER[x], c, :],
                                              d > 0 and c == 0, c == KC - 1)
                            ins.then_inc(s_dn, 1)

                run(pe, do)


def stage_constants(nc, a, idf, idb, mq, mk, tg, graw):
    with ExitStack() as ctx:
        r_ = Res(nc, ctx, "co_")
        s_g, s_m, s_t = r_.sem("g"), r_.sem("m"), r_.sem("t")
        r_.prime()
        with nc.Block() as block:

            @block.sync
            def _(sp):
                for n, g in enumerate(("g_xattn", "g_ffn")):
                    sp.dma_start(graw[:, n:n + 1], a[g].rearrange("(o c) -> o c", o=1).to_broadcast([P, 1])).then_inc(s_g, 16)

            @block.gpsimd
            def _(pool):
                for t, v in ((idf, 1.0), (idb, 1.0), (mq, 0.0), (mk, 0.0)):
                    pool.memset(t[:, :], v).then_inc(s_m, 1)
                wait(pool, s_m, 4)
                for t in (idf, idb):
                    pool.affine_select(out=t[:, :], in_=t[:, :], compare_op=ALU.is_equal, fill=0.0, base=0,
                                       pattern=[[-1, P]], channel_multiplier=1)
                pool.affine_select(out=mq[:, :], in_=mq[:, :], compare_op=ALU.is_ge, fill=NEG, base=0,
                                   pattern=[[-1, P]], channel_multiplier=1)
                pool.affine_select(out=mk[:, :], in_=mk[:, :], compare_op=ALU.is_ge, fill=NEG, base=0,
                                   pattern=[[1, P]], channel_multiplier=-1)

            @block.scalar
            def _(act):
                wait(act, s_g, 32)
                act.activation(tg[:, :], graw[:, :], ACT.Tanh).then_inc(s_t, 1)


def build(nc, a, out):
    QS = nc.dram_tensor("q_parts", [3, NI * GC, 2 * T], BF16).ap()
    KS = nc.dram_tensor("k_parts", [3, NI * GC, NK], BF16).ap()
    VS = nc.dram_tensor("v_items", [NI, P, NKT, GC], F32).ap()
    YS = nc.dram_tensor("y_items", [NI + 1, P, QT, GC], F32).ap()
    X1S = nc.dram_tensor("x1_blocks", [B, P, QT, C], F32).ap()
    FS = nc.dram_tensor("ffn_blocks", [B, P, QT, C], F32).ap()
    with ExitStack() as ctx:
        r_ = Res(nc, ctx, "c_")
        idf, idb = r_.sb("idf", [P, P]), r_.sb("idb", [P, P], BF16)
        mq, mk = r_.sb("mq", [P, P], BF16), r_.sb("mk", [P, P], BF16)
        tg, graw = r_.sb("tg", [P, 2]), r_.sb("graw", [P, 2])
        stage_constants(nc, a, idf, idb, mq, mk, tg, graw)
        stage_project(nc, a, QS, KS, VS, idf)
        stage_attend(nc, QS, KS, VS, YS, idf, idb, mq, mk)
        w = {n: r_.sb(n, [P, NX, KC, IW], F32R) for n in ("uH", "uL", "cH", "cL", "dH", "dL")}
        w.update(bu=r_.sb("bu", [P, NX, KC]), bc=r_.sb("bc", [P, NX, KC]), bd=r_.sb("bd", [NE + 1, C]))
        stage_mix(nc, a, YS, X1S, FS, w, tg, idf)
        stage_experts(nc, a, FS, X1S, w, tg, out, idf)


def lay_out(i):
    f = lambda n: np.ascontiguousarray(np.asarray(i[n], np.float32))
    att, ffn = (lambda n: f("L0_xattn_" + n)), (lambda n: f("L0_ffn_" + n))
    up = np.concatenate([ffn("exp_Wup"), ffn("share_Wup").reshape(C, NS, IW).transpose(1, 0, 2)])
    shared = lambda e, s: np.concatenate([ffn(e)] + [ffn(s)[None]] * NS)
    cols = lambda v: v.reshape(*v.shape[:-1], KC, P)
    bup = np.concatenate([ffn("exp_bup"), ffn("share_bup").reshape(NS, IW)])
    d = {n: att(n) for n in ("Wk", "Wq", "Wv", "bv", "Wck", "Wcq", "Wcv", "bcv", "Wp", "bp")}
    d["bcol"] = cols(np.stack([att(n) for n in ("bq", "bcq", "bk", "bck")])).transpose(2, 0, 1)
    d.update(x=f("x"), ctxT=f("ctx_512").transpose(0, 2, 1), g_xattn=f("g_xattn"), g_ffn=f("g_ffn"),
             Wup=up, WupT=up.transpose(0, 2, 1), Wg=shared("exp_Wg", "share_Wg"), Wd=shared("exp_Wdown", "share_Wdown"),
             bup=cols(bup).transpose(2, 0, 1), bg=cols(shared("exp_bg", "share_bg")).transpose(2, 0, 1),
             bd=np.concatenate([ffn("exp_bdown"), ffn("share_bdown")[None]]),
             router_W=ffn("router_W").reshape(NL, KC, P, NE).transpose(2, 0, 1, 3), router_b=ffn("router_b"), gate_bias=ffn("gate_bias"), norm_w=ffn("norm_w"))
    return {n: np.ascontiguousarray(v) for n, v in d.items()}


def kernel(**inputs):
    import concourse.bacc as bacc
    from concourse.bass_utils import run_bass_kernel_spmd

    nc = bacc.Bacc("TRN2", target_bir_lowering=False, num_devices=1)
    arrays = lay_out(inputs)
    aps = {n: nc.dram_tensor("in_" + n, v.shape, mybir.dt.from_np(v.dtype), kind="ExternalInput").ap()
           for n, v in arrays.items()}
    out = nc.dram_tensor("out", (B, T, C), F32, kind="ExternalOutput").ap()
    build(nc, aps, out)
    r = run_bass_kernel_spmd(nc, [{"in_" + n: v for n, v in arrays.items()}], core_ids=[0])
    return r.results[0]["out"]
```
